# Optimizing a Trainium2 kernel written in Bass

```python
import numpy as np
import jax
import jax.numpy as jnp

def _softmax(x, axis=-1):
    return jax.nn.softmax(x, axis=axis)

def _gelu(x):
    return jax.nn.gelu(x, approximate=True)

def _silu(x):
    return jax.nn.silu(x)

def _sigmoid(x):
    return jax.nn.sigmoid(x)

def _layernorm(x, axis=-1, eps=1e-05):
    m = jnp.mean(x, axis=axis, keepdims=True)
    v = jnp.var(x, axis=axis, keepdims=True)
    return (x - m) / jnp.sqrt(v + eps)

def _scatter_add(tgt, idx, src, axis=0):
    return tgt.at[idx].add(src)

def _segment_sum(src, seg, n):
    return jax.ops.segment_sum(src, seg, n)
kernel_name = 'mk_perceiver_d1_seqx_r4_f44c73'

def setup_inputs(seed: int=0):
    np.random.seed(seed)
    _w = jnp.asarray

    def _rec_inputs():
        import jax
        import jax.numpy as jnp
        _rk = jax.random.key(seed)
        x = 7.22e-05 + 1 * jax.random.normal(jax.random.fold_in(_rk, 1), (16, 64, 512), jnp.float32)
        _lenS = 64 - jax.random.randint(jax.random.fold_in(_rk, 7), (16,), 0, max(1, 64 // 4) + 1, jnp.int32)
        _lenS2 = 1601 - jax.random.randint(jax.random.fold_in(_rk, 8), (16,), 0, max(1, 1601 // 4) + 1, jnp.int32)
        _ctx_512P = jax.random.normal(jax.random.fold_in(_rk, 11), (16, 16, 128), jnp.float32)
        _ctx_512c = jax.random.dirichlet(jax.random.fold_in(_rk, 511), 0.3 * jnp.ones((16,), jnp.float32), (16, 1601))
        _ctx_512t = jnp.einsum('bsk,bkd->bsd', _ctx_512c, _ctx_512P)
        _ctx_512t = _ctx_512t * jax.lax.rsqrt(jnp.mean(jnp.square(_ctx_512t)) + 1e-12) * 0.953939
        ctx_512 = -0.000514642 + 1.00011 * (_ctx_512t + 0.3 * jax.random.normal(jax.random.fold_in(_rk, 611), (16, 1601, 128), jnp.float32))
        return (x, ctx_512)
    x, ctx_512 = _rec_inputs()

    def _L0_xattn_setup():
        import jax, jax.numpy as jnp
        import numpy as np
        B, S, H, NH, L = (2, 512, 512, 16, 128)
        HD = H // NH
        key = jax.random.key(seed)
        k1, k2, k3, k4, k5 = jax.random.split(key, 5)
        scale = 0.02
        return {'q': jax.random.normal(k1, (B, S, H), dtype=jnp.float32), 'latent_kv': jax.random.normal(k2, (B, S, L), dtype=jnp.float32), 'Wq': jax.random.normal(k3, (H, H), dtype=jnp.float32) * scale, 'Wkv_expand': jax.random.normal(k4, (2 * H, L), dtype=jnp.float32) * scale, 'Wout': jax.random.normal(k5, (H, H), dtype=jnp.float32) * scale}
    _L0_xattn_all = _L0_xattn_setup()
    _L0_xattn_in = {k: v for k, v in _L0_xattn_all.items() if k in ('Wq', 'Wkv_expand', 'Wout')}
    del _L0_xattn_all

    def _L0_attn_setup():
        import jax, jax.numpy as jnp
        import numpy as np
        H = 20
        D_NOPE = 192
        D_ROPE = 64
        D_QK = D_NOPE + D_ROPE
        D_V = 64
        KV_LORA = 128
        THETA = 1000000.0
        EPS = 1e-06

        def _rms_norm(x, w):
            var = jnp.mean(jnp.square(x), axis=-1, keepdims=True)
            return x * jax.lax.rsqrt(var + EPS) * w

        def _rotate_half(x):
            x1, x2 = jnp.split(x, 2, axis=-1)
            return jnp.concatenate([-x2, x1], axis=-1)

        def _rope_cos_sin(seq_len, dtype):
            inv_freq = 1.0 / THETA ** (jnp.arange(0, D_ROPE, 2, dtype=jnp.float32) / D_ROPE)
            pos = jnp.arange(seq_len, dtype=jnp.float32)
            freqs = pos[:, None] * inv_freq[None, :]
            emb = jnp.concatenate([freqs, freqs], axis=-1)
            return (jnp.cos(emb).astype(dtype), jnp.sin(emb).astype(dtype))
        key = jax.random.key(seed)
        ks = jax.random.split(key, 6)
        B, S, HID = (2, 512, 512)
        sc = 0.02
        return {'hidden_states': jax.random.normal(ks[0], (B, S, HID), jnp.float32), 'q_a_w': jax.random.normal(ks[1], (192, HID), jnp.float32) * sc, 'q_a_ln_w': jnp.ones((192,), jnp.float32), 'q_b_w': jax.random.normal(ks[2], (H * D_QK, 192), jnp.float32) * sc, 'kv_a_w': jax.random.normal(ks[3], (KV_LORA + D_ROPE, HID), jnp.float32) * sc, 'kv_a_ln_w': jnp.ones((KV_LORA,), jnp.float32), 'kv_b_w': jax.random.normal(ks[4], (H * (D_NOPE + D_V), KV_LORA), jnp.float32) * sc, 'o_w': jax.random.normal(ks[5], (HID, H * D_V), jnp.float32) * sc}
    _L0_attn_all = _L0_attn_setup()
    _L0_attn_in = {k: v for k, v in _L0_attn_all.items() if k in ('q_a_w', 'q_a_ln_w', 'q_b_w', 'kv_a_w', 'kv_a_ln_w', 'kv_b_w', 'o_w')}
    del _L0_attn_all

    def _L0_ffn_setup():
        import jax, jax.numpy as jnp
        import numpy as np
        E = 64
        K = 6
        CAP = 128
        SCALE = 1.0
        H = 512
        I = 192
        SI = I * 2
        B, S = (2, 256)

        def _moe(x, gate_w, gate_up_proj, down_proj, shared_gate_w, shared_up_w, shared_down_w):
            b, s, h = x.shape
            T = b * s
            xf = x.reshape(T, h)
            scores = jax.nn.softmax(xf @ gate_w.T, axis=-1)
            topk_w, topk_idx = jax.lax.top_k(scores, K)
            topk_w = topk_w * SCALE
            flat_e = topk_idx.reshape(-1)
            order = jnp.argsort(flat_e)
            sorted_e = flat_e[order]
            sorted_tok = (order // K).astype(jnp.int32)
            sorted_w = topk_w.reshape(-1)[order]
            counts = jnp.zeros((E,), jnp.int32).at[flat_e].add(1)
            offsets = jnp.cumsum(counts) - counts
            pos = jnp.arange(T * K, dtype=jnp.int32) - offsets[sorted_e]
            buf_tok = jnp.full((E, CAP), T, jnp.int32).at[sorted_e, pos].set(sorted_tok, mode='drop')
            buf_w = jnp.zeros((E, CAP), x.dtype).at[sorted_e, pos].set(sorted_w, mode='drop')
            xp = jnp.concatenate([xf, jnp.zeros((1, h), x.dtype)], axis=0)
            gx = xp[buf_tok]
            gu = jnp.einsum('ech,ehi->eci', gx, gate_up_proj)
            g, u = jnp.split(gu, 2, axis=-1)
            hid = jax.nn.silu(g) * u
            eo = jnp.einsum('eci,eih->ech', hid, down_proj) * buf_w[..., None]
            routed = jnp.zeros((T + 1, h), x.dtype).at[buf_tok.reshape(-1)].add(eo.reshape(-1, h))[:T]
            shared = jax.nn.silu(xf @ shared_gate_w.T) * (xf @ shared_up_w.T) @ shared_down_w.T
            return (routed + shared).reshape(b, s, h)
        key = jax.random.key(seed)
        ks = jax.random.split(key, 7)
        x = jax.random.normal(ks[0], (B, S, H), jnp.float32)
        gate_w = jax.random.normal(ks[1], (E, H), jnp.float32) * 0.02
        gate_up_proj = jax.random.normal(ks[2], (E, H, 2 * I), jnp.float32) * 0.02
        down_proj = jax.random.normal(ks[3], (E, I, H), jnp.float32) * 0.02
        shared_gate_w = jax.random.normal(ks[4], (SI, H), jnp.float32) * 0.02
        shared_up_w = jax.random.normal(ks[5], (SI, H), jnp.float32) * 0.02
        shared_down_w = jax.random.normal(ks[6], (H, SI), jnp.float32) * 0.02
        return dict(x=x, gate_w=gate_w, gate_up_proj=gate_up_proj, down_proj=down_proj, shared_gate_w=shared_gate_w, shared_up_w=shared_up_w, shared_down_w=shared_down_w)
    _L0_ffn_all = _L0_ffn_setup()
    _L0_ffn_in = {k: v for k, v in _L0_ffn_all.items() if k in ('gate_w', 'gate_up_proj', 'down_proj', 'shared_gate_w', 'shared_up_w', 'shared_down_w')}
    del _L0_ffn_all
    return {'x': x, 'ctx_512': ctx_512, 'L0_xattn_Wq': _L0_xattn_in['Wq'], 'L0_xattn_Wkv_expand': _L0_xattn_in['Wkv_expand'], 'L0_xattn_Wout': _L0_xattn_in['Wout'], 'L0_attn_q_a_w': _L0_attn_in['q_a_w'], 'L0_attn_q_a_ln_w': _L0_attn_in['q_a_ln_w'], 'L0_attn_q_b_w': _L0_attn_in['q_b_w'], 'L0_attn_kv_a_w': _L0_attn_in['kv_a_w'], 'L0_attn_kv_a_ln_w': _L0_attn_in['kv_a_ln_w'], 'L0_attn_kv_b_w': _L0_attn_in['kv_b_w'], 'L0_attn_o_w': _L0_attn_in['o_w'], 'L0_ffn_gate_w': _L0_ffn_in['gate_w'], 'L0_ffn_gate_up_proj': _L0_ffn_in['gate_up_proj'], 'L0_ffn_down_proj': _L0_ffn_in['down_proj'], 'L0_ffn_shared_gate_w': _L0_ffn_in['shared_gate_w'], 'L0_ffn_shared_up_w': _L0_ffn_in['shared_up_w'], 'L0_ffn_shared_down_w': _L0_ffn_in['shared_down_w']}

def reference(x, ctx_512, L0_xattn_Wq, L0_xattn_Wkv_expand, L0_xattn_Wout, L0_attn_q_a_w, L0_attn_q_a_ln_w, L0_attn_q_b_w, L0_attn_kv_a_w, L0_attn_kv_a_ln_w, L0_attn_kv_b_w, L0_attn_o_w, L0_ffn_gate_w, L0_ffn_gate_up_proj, L0_ffn_down_proj, L0_ffn_shared_gate_w, L0_ffn_shared_up_w, L0_ffn_shared_down_w):
    import jax
    import jax.numpy as jnp

    def _L0_xattn_ref(q, latent_kv, Wq, Wkv_expand, Wout):
        import jax, jax.numpy as jnp
        import numpy as np
        B, S, H, NH, L = (2, 512, 512, 16, 128)
        HD = H // NH
        b, sq, _ = q.shape
        sk = latent_kv.shape[1]
        qp = q @ Wq.T
        kv = latent_kv @ Wkv_expand.T
        k, v = jnp.split(kv, 2, axis=-1)
        qh = qp.reshape(b, sq, NH, HD).transpose(0, 2, 1, 3)
        kh = k.reshape(b, sk, NH, HD).transpose(0, 2, 1, 3)
        vh = v.reshape(b, sk, NH, HD).transpose(0, 2, 1, 3)
        inv_sqrt_d = 1.0 / jnp.sqrt(jnp.float32(HD))
        scores = jnp.einsum('bhqd,bhkd->bhqk', qh, kh) * inv_sqrt_d
        causal = jnp.tril(jnp.ones((sq, sk), dtype=bool))
        scores = jnp.where(causal, scores, jnp.finfo(scores.dtype).min)
        attn = jax.nn.softmax(scores, axis=-1)
        out = jnp.einsum('bhqk,bhkd->bhqd', attn, vh)
        out = out.transpose(0, 2, 1, 3).reshape(b, sq, H)
        return out @ Wout.T

    def _L0_attn_ref(hidden_states, q_a_w, q_a_ln_w, q_b_w, kv_a_w, kv_a_ln_w, kv_b_w, o_w):
        import jax, jax.numpy as jnp
        import numpy as np
        H = 20
        D_NOPE = 192
        D_ROPE = 64
        D_QK = D_NOPE + D_ROPE
        D_V = 64
        KV_LORA = 128
        THETA = 1000000.0
        EPS = 1e-06

        def _rms_norm(x, w):
            var = jnp.mean(jnp.square(x), axis=-1, keepdims=True)
            return x * jax.lax.rsqrt(var + EPS) * w

        def _rotate_half(x):
            x1, x2 = jnp.split(x, 2, axis=-1)
            return jnp.concatenate([-x2, x1], axis=-1)

        def _rope_cos_sin(seq_len, dtype):
            inv_freq = 1.0 / THETA ** (jnp.arange(0, D_ROPE, 2, dtype=jnp.float32) / D_ROPE)
            pos = jnp.arange(seq_len, dtype=jnp.float32)
            freqs = pos[:, None] * inv_freq[None, :]
            emb = jnp.concatenate([freqs, freqs], axis=-1)
            return (jnp.cos(emb).astype(dtype), jnp.sin(emb).astype(dtype))
        B, S, _ = hidden_states.shape
        scale = D_QK ** (-0.5)
        q_c = jnp.einsum('bsh,rh->bsr', hidden_states, q_a_w)
        q_c = _rms_norm(q_c, q_a_ln_w)
        q = jnp.einsum('bsr,dr->bsd', q_c, q_b_w)
        q = q.reshape(B, S, H, D_QK).transpose(0, 2, 1, 3)
        q_nope, q_rope = (q[..., :D_NOPE], q[..., D_NOPE:])
        ckv = jnp.einsum('bsh,ch->bsc', hidden_states, kv_a_w)
        k_latent, k_rope = (ckv[..., :KV_LORA], ckv[..., KV_LORA:])
        k_latent = _rms_norm(k_latent, kv_a_ln_w)
        kvd = jnp.einsum('bsr,dr->bsd', k_latent, kv_b_w)
        kvd = kvd.reshape(B, S, H, D_NOPE + D_V).transpose(0, 2, 1, 3)
        k_nope, v = (kvd[..., :D_NOPE], kvd[..., D_NOPE:])
        cos, sin = _rope_cos_sin(S, q_rope.dtype)
        q_rope = q_rope * cos + _rotate_half(q_rope) * sin
        k_rope = k_rope[:, None, :, :]
        k_rope = k_rope * cos + _rotate_half(k_rope) * sin
        k = jnp.concatenate([k_nope, jnp.broadcast_to(k_rope, (B, H, S, D_ROPE))], axis=-1)
        scores = jnp.einsum('bhqd,bhkd->bhqk', q, k) * scale
        causal = jnp.tril(jnp.ones((S, S), bool))
        scores = jnp.where(causal, scores, jnp.finfo(scores.dtype).min)
        probs = jax.nn.softmax(scores, axis=-1)
        ctx = jnp.einsum('bhqk,bhkd->bhqd', probs, v)
        ctx = ctx.transpose(0, 2, 1, 3).reshape(B, S, H * D_V)
        return jnp.einsum('bsd,hd->bsh', ctx, o_w)

    def _L0_ffn_ref(x, gate_w, gate_up_proj, down_proj, shared_gate_w, shared_up_w, shared_down_w):
        import jax, jax.numpy as jnp
        import numpy as np
        E = 64
        K = 6
        CAP = 128
        SCALE = 1.0
        H = 512
        I = 192
        SI = I * 2
        B, S = (2, 256)

        def _moe(x, gate_w, gate_up_proj, down_proj, shared_gate_w, shared_up_w, shared_down_w):
            b, s, h = x.shape
            T = b * s
            xf = x.reshape(T, h)
            scores = jax.nn.softmax(xf @ gate_w.T, axis=-1)
            topk_w, topk_idx = jax.lax.top_k(scores, K)
            topk_w = topk_w * SCALE
            flat_e = topk_idx.reshape(-1)
            order = jnp.argsort(flat_e)
            sorted_e = flat_e[order]
            sorted_tok = (order // K).astype(jnp.int32)
            sorted_w = topk_w.reshape(-1)[order]
            counts = jnp.zeros((E,), jnp.int32).at[flat_e].add(1)
            offsets = jnp.cumsum(counts) - counts
            pos = jnp.arange(T * K, dtype=jnp.int32) - offsets[sorted_e]
            buf_tok = jnp.full((E, CAP), T, jnp.int32).at[sorted_e, pos].set(sorted_tok, mode='drop')
            buf_w = jnp.zeros((E, CAP), x.dtype).at[sorted_e, pos].set(sorted_w, mode='drop')
            xp = jnp.concatenate([xf, jnp.zeros((1, h), x.dtype)], axis=0)
            gx = xp[buf_tok]
            gu = jnp.einsum('ech,ehi->eci', gx, gate_up_proj)
            g, u = jnp.split(gu, 2, axis=-1)
            hid = jax.nn.silu(g) * u
            eo = jnp.einsum('eci,eih->ech', hid, down_proj) * buf_w[..., None]
            routed = jnp.zeros((T + 1, h), x.dtype).at[buf_tok.reshape(-1)].add(eo.reshape(-1, h))[:T]
            shared = jax.nn.silu(xf @ shared_gate_w.T) * (xf @ shared_up_w.T) @ shared_down_w.T
            return (routed + shared).reshape(b, s, h)
        return _moe(x, gate_w, gate_up_proj, down_proj, shared_gate_w, shared_up_w, shared_down_w)
    x = x + _L0_xattn_ref(_layernorm(x, axis=-1), ctx_512, L0_xattn_Wq, L0_xattn_Wkv_expand, L0_xattn_Wout)
    x = x + _L0_attn_ref(_layernorm(x, axis=-1), L0_attn_q_a_w, L0_attn_q_a_ln_w, L0_attn_q_b_w, L0_attn_kv_a_w, L0_attn_kv_a_ln_w, L0_attn_kv_b_w, L0_attn_o_w)
    x = x + _L0_ffn_ref(_layernorm(x, axis=-1), L0_ffn_gate_w, L0_ffn_gate_up_proj, L0_ffn_down_proj, L0_ffn_shared_gate_w, L0_ffn_shared_up_w, L0_ffn_shared_down_w)
    return x

_drawn_inputs = setup_inputs


def setup_inputs(seed=0):
    import zlib

    import numpy as np

    out = dict(_drawn_inputs(seed))
    spreads = {'L0_attn_q_a_ln_w': (1.0, 0.6), 'L0_attn_kv_a_ln_w': (1.0, 0.6)}
    factors = {'L0_xattn_Wq': 8.0,
     'L0_attn_q_a_w': 8.0,
     'L0_attn_q_b_w': 8.0,
     'L0_ffn_gate_w': 8.0,
     'L0_ffn_gate_up_proj': 7.212,
     'L0_ffn_down_proj': 7.276,
     'L0_ffn_shared_gate_w': 8.0,
     'L0_ffn_shared_up_w': 8.0,
     'L0_ffn_shared_down_w': 8.0}
    for name, (base, spread) in spreads.items():
        noise = np.random.default_rng([zlib.crc32(name.encode()), seed]).standard_normal(out[name].shape)
        drawn = base * np.exp(spread * noise) if base else spread * noise
        out[name] = jnp.asarray(drawn.astype(out[name].dtype))
    for name, factor in factors.items():
        out[name] = (out[name] * factor).astype(out[name].dtype)
    return out
```

```python
from contextlib import ExitStack

import numpy as np
import concourse.bass as bass
from concourse import mybir

B, SQ, D = 16, 64, 512
TOK = B * SQ
P = 128
NT = TOK // P
KD = D // P
G = 2
NI = NT // G
GT = G * P
XH, XD, XL = 16, 32, 128
MH, DN, DR, DV = 20, 192, 64, 64
QR, KL = 192, 128
E, TOPK, CAP, FI = 64, 6, 128, 192
SI = 2 * FI
H3 = FI // 3
R = 4
ROWS = TOK + CAP
NEG = -1.0e30
FLOOR = -3.0e38

C_ID, C_MASK, C_BEFORE, C_IOTA, C_ONES = 0, 128, 256, 384, 512
C_COS, C_SIN, C_TOK = 640, 704, 768
C_SPARE, C_EPS5, C_EPS6, C_HEAD, C_COLS = 776, 777, 778, 779, 784


def constant_table():
    c = np.zeros((P, C_COLS), np.float32)
    p = np.arange(P)
    c[:, C_ID:C_ID + P] = np.eye(P)
    same = (p[:, None] // SQ) == (p[None, :] // SQ)
    c[:, C_MASK:C_MASK + P] = np.where(same & (p[None, :] <= p[:, None]), 0.0, NEG)
    c[:, C_BEFORE:C_BEFORE + P] = p[:, None] < p[None, :]
    c[:, C_IOTA:C_IOTA + P] = p[None, :]
    c[:, C_ONES:C_ONES + P] = 1.0
    inv_freq = (1.0 / np.float32(1000000.0) ** (np.arange(0, DR, 2, dtype=np.float32) / np.float32(DR))).astype(np.float32)
    freqs = np.arange(SQ, dtype=np.float32)[:, None] * inv_freq[None, :]
    emb = np.concatenate([freqs, freqs], axis=-1)
    sign = np.where(np.arange(DR) < DR // 2, -1.0, 1.0).astype(np.float32)
    cos, sin = np.cos(emb), np.sin(emb) * sign
    c[:, C_COS:C_COS + DR] = np.tile(cos, (2, 1))
    c[:, C_SIN:C_SIN + DR] = np.tile(sin, (2, 1))
    c[:, C_TOK:C_TOK + NT] = P * np.arange(NT)[None, :] + p[:, None] + 1
    c[:, C_SPARE] = TOK + 1 + p
    c[:, C_HEAD:C_HEAD + 4] = p[:, None] // XD == np.arange(4)[None, :]
    c[:, C_EPS5] = 1e-5
    c[:, C_EPS6] = 1e-6
    return c


XU = G * XH // 4
MU = G * MH // 4
NU = XU + MU


def unit(n):
    if n < XU:
        return False, n // (XH // 4), n % (XH // 4)
    n -= XU
    return True, n // (MH // 4), n % (MH // 4)


def iteration_order():
    o = [("ln", 0), ("ln", 1)]
    o += [("job", j) for j in ("k0", "k1", "v0", "v1", "xT0", "xT1", "q0", "q1")]

    def attend(first, n, extra):
        for u in range(n + 3):
            o.extend(extra.get(u, []))
            if u < n:
                o.append(("S", first + u))
            if 1 <= u < n + 1:
                o.append(("R", first + u - 1))
            if 2 <= u < n + 2:
                o.append(("T", first + u - 2))
            if 3 <= u:
                o.append(("A", first + u - 3))

    attend(0, XU, {XU - 1: [("job", "o0"), ("ln", 2)]})
    o += [("job", "o1"), ("ln", 3), ("job", "x2T0"), ("job", "a0"), ("job", "x2T1"), ("job", "a1"),
          ("job", "aT0"), ("job", "v2_0"), ("job", "v2_1"), ("job", "aT1"), ("job", "v2_2"),
          ("job", "v2_3"), ("job", "v2_4")]
    o += [("job", f"r{m}") for m in range(5)]
    o += [("job", f"l{m}") for m in range(4)]
    extra = {u: [("job", f"l{2 * u + 2}"), ("job", f"l{2 * u + 3}")] for u in range(1, MH // 4 - 1)}
    extra[MU // 2 + 4] = [("job", "o2_0"), ("ln", 4)]
    attend(XU, MU, extra)
    o += [("job", "o2_1"), ("ln", 5), ("job", "x3T0"), ("job", "x3T1")]
    return o


ORDER = iteration_order()
JOBS = [n for kind, n in ORDER if kind == "job"]
JOB = {name: n for n, name in enumerate(JOBS)}
assert len(JOBS) % 2 == 0


def build(nc, x, ctxT, consts, wqT, wkvT, woutT, waT, lnq, lnkv, wqb, wqrT, wkb, wvbT, woT,
          gateT, gate_up, down, sgT, suT, sdT, out):
    fp32, u32 = mybir.dt.float32, mybir.dt.uint32
    ALU, ACT, AX = mybir.AluOpType, mybir.ActivationFunctionType, mybir.AxisListType

    hold = ExitStack()
    with hold:
        x3n_rows = nc.dram_tensor("x3n_rows", [ROWS, D], fp32).ap()
        sums = nc.dram_tensor("sums", [ROWS, D], fp32).ap()

        def sb(name, shape, dt=fp32):
            return hold.enter_context(nc.sbuf_tensor(name, shape, dt))

        cst = sb("cst", [P, C_COLS])
        x_all = sb("x_all", [P, NT, D])
        x3nT = sb("x3nT", [P, KD, TOK])
        small = sb("small", [P, 64])
        ARENA = 43700
        arena = sb("arena", [P, ARENA])
        used = [0]

        def take(*shape):
            n = int(np.prod(shape))
            v = arena[:, used[0]:used[0] + n]
            used[0] += n
            assert used[0] <= ARENA, used
            if len(shape) == 2:
                v = v.rearrange("p (a b) -> p a b", b=shape[1])
            elif len(shape) == 3:
                v = v.rearrange("p (a b c) -> p a b c", b=shape[1], c=shape[2])
            return v

        ctxT_all = take(TOK)
        WqT, WkvT, WoutT, WaT = take(KD, D), take(2 * D), take(KD, D), take(KD, QR + KL + DR)
        M0, M1 = take(MH, KL), take(MH, KL)
        WqrT0, WqrT1, WvbT, WoT = take(MH * DR), take(MH * DR), take(MH * DV), take(MH // 2, D)
        xn, xnT, ctx_cur = take(G, D), take(KD, GT), take(GT)
        an = xn
        mark = used[0]
        ql = take(MH, GT)
        used[0] = mark
        qT, kT, v, cT = take(KD, GT), take(KD, GT), take(G, D), take(KD, GT)
        used[0] = mark + MH * GT
        masked, probs, probsT = take(2, 4, P), take(3, 4, P), take(2, 4, P)
        qc0, qc1, klT = take(GT), take(GT), take(GT)
        mark = used[0]
        v2, qr, c2T = take(G, MH * DV), take(MH // 2, GT), take(MH // 2, GT)
        end_attention = used[0]
        used[0] = mark - 3 * GT - 7 * 4 * P - MH * GT
        wqb0, wqb1, wkb0, wkb1 = take(MH, QR), take(MH, QR), take(MH, KL), take(MH, KL)
        used[0] = max(used[0], end_attention)
        rot1, rot2, junk = take(DR), take(DR), take(QR + KL)
        kz = take(2, 4, P)
        krz = take(2, GT)

        used[0] = 0
        WgT, WsgT, WsuT, WsdT = take(KD, E), take(KD, SI), take(KD, SI), take(SI // P, D)
        hidT, silu_s = take(SI // P, TOK), take(2, 512)
        wgu, wd0, wd1 = take(R, KD, 2 * FI), take(R, D), take(R, D)
        choice_at = used[0]
        gx, gxT, eo = take(R, D), take(2, D), take(R, D)
        choice = arena[:, choice_at:choice_at + NT * TOPK * E].rearrange("p (a b) -> p a b", b=E)
        silu_e, hid_e = take(2, 3 * P), take(2, 2 * P)
        idx_w = take(2, E)
        spare = take(E)
        gather_rows, add_rows = take(R).bitcast(u32), take(R).bitcast(u32)
        row_of = take(E).bitcast(u32)
        lgT, lg, ex = take(TOK), take(NT, E), take(NT, E)
        top_w, top_i, top_f = take(NT, 8), take(NT, 8).bitcast(u32), take(NT, 8)
        chosen_by, before, rank_of = take(NT, E), take(NT, E), take(NT * TOPK)
        mark = used[0]
        hot = take(NT * TOPK, P)
        used[0] = mark
        scratch = take(NT * TOPK, E)
        used[0] = mark + NT * TOPK * P
        pair = take(NT * TOPK, 2, E)

        stat, mv = small[:, 0:6], small[:, 6:10].rearrange("p (s c) -> p s c", c=2)
        std, rstd = small[:, 10:12], small[:, 12:14]
        ss, rms, rrms = (small[:, 14 + 4 * k:18 + 4 * k].rearrange("p (s c) -> p s c", c=2) for k in range(3))
        lnq0, lnq1, lnk = small[:, 26:27], small[:, 27:28], small[:, 28:29]
        mx, nmx, den, rden = (sb(n, [P, 3, 4]) for n in ("mx", "nmx", "den", "rden"))
        mx8, sum8, rsum8 = small[:, 32:40], small[:, 40:48], small[:, 48:56]

        ident, mask = cst[:, C_ID:C_ID + P], cst[:, C_MASK:C_MASK + P]
        eps5, eps6 = cst[:, C_EPS5:C_EPS5 + 1], cst[:, C_EPS6:C_EPS6 + 1]

        def bank_pair(name):
            return [hold.enter_context(nc.psum_tensor(f"{name}{k}", [P, 512], fp32)) for k in range(2)]

        job_bank, s_bank, t_bank, a_bank = (bank_pair(n) for n in ("job_bank", "s_bank", "t_bank", "a_bank"))

        PER = {}

        def sem(name, per=0):
            s = hold.enter_context(nc.semaphore(name))
            PER[name] = per
            return s, name

        PRIMED = ("filled0", "filled1", "copied0", "copied1", "masked_ready", "scores_ready", "pT_ready",
                  "pT_copied", "av_ready", "av_copied", "rows_gone")

        def at(s, i, k):
            return i * PER[s[1]] + k + (s[1] in PRIMED)

        def prime(eng, *sems):
            for s in sems:
                eng.sem_inc(s[0], 1)

        loaded = {n: sem(f"loaded_{n}") for n in (
            "consts", "ctx", "x", "wkv", "wq", "qb0", "qb1", "kb0", "kb1", "wout", "wa", "qr0", "qr1",
            "wvb", "wo", "lnq0", "lnq1", "lnkv", "gate", "sg", "su", "sd")}
        m_filled = [sem(f"m_filled{k}") for k in range(2)]
        m_copied = [sem(f"m_copied{k}") for k in range(2)]
        filled = [sem(f"filled{k}", len(JOBS) // 2) for k in range(2)]
        copied = [sem(f"copied{k}", len(JOBS) // 2) for k in range(2)]
        ctx_ready = sem("ctx_ready", 1)
        ln_var, ln_std, ln_done = sem("ln_var", 6), sem("ln_std", 6), sem("ln_done", 6)
        rms_sum, rms_std = sem("rms_sum", 2), sem("rms_std", 2)
        zeros_ready = sem("zeros_ready")
        kz_ready = sem("kz_ready", XU)
        scores_ready, masked_ready = sem("scores_ready", NU), sem("masked_ready", NU)
        exp_done, rden_ready, norm_done = sem("exp_done", NU), sem("rden_ready", NU), sem("norm_done", NU)
        pT_ready, pT_copied = sem("pT_ready", NU), sem("pT_copied", NU)
        av_ready, av_copied = sem("av_ready", NU), sem("av_copied", NU)
        DVE_LINKS = 6 * 2 + 2 * 2 + NU
        dve_chain = sem("dve_chain", DVE_LINKS)
        rows_stored = sem("rows_stored", 16 * G)
        rows_gone = sem("rows_gone", 1)
        zero_ready, spare_stored = sem("zero_ready"), sem("spare_stored")

        def bank_of(name):
            return job_bank[JOB[name] % 2]

        def wait_filled(eng, i, name):
            eng.wait_ge(filled[JOB[name] % 2][0], at(filled[JOB[name] % 2], i, JOB[name] // 2 + 1))

        def wait_copied(eng, i, name):
            eng.wait_ge(copied[JOB[name] % 2][0], at(copied[JOB[name] % 2], i, JOB[name] // 2 + 1))

        gate_filled, gate_copied = sem("gate_filled"), sem("gate_copied")
        logits_ready = sem("logits_ready")
        lg_shifted, lg_exp = sem("lg_shifted"), sem("lg_exp")
        up_filled, up_silu, up_done = sem("up_filled"), sem("up_silu"), sem("up_done")
        down_filled, down_added = sem("down_filled"), sem("down_added")
        before_ready, pos_filled = sem("before_ready"), sem("pos_filled")
        choice_ready, pair_ready, hot_ready = sem("choice_ready"), sem("pair_ready"), sem("hot_ready")
        table_filled, table_copied, table_turned = sem("table_filled"), sem("table_copied"), sem("table_turned")
        rows_known = sem("rows_known")
        route_chain = sem("route_chain")
        pool_chain = sem("pool_chain")
        sums_stored = sem("sums_stored")
        w_loaded = [sem(f"w_loaded{r}", 64) for r in range(R)]
        gx_loaded = [sem(f"gx_loaded{r}", 16) for r in range(R)]
        gx_turned, gxT_copied = sem("gx_turned", R), sem("gxT_copied", R)
        gu_filled, silu_done, hid_ready = sem("gu_filled", R), sem("silu_done", R), sem("hid_ready", R)
        rows_copied = sem("rows_copied")
        eo_filled, eo_ready = sem("eo_filled", R), sem("eo_ready", R)
        added = sem("added", 16 * R)
        out_stored = sem("out_stored")

        block = hold.enter_context(nc.Block())

        @block.sync
        def _(sp):
            prime(sp, rows_gone)
            for name, dst, src in (
                    ("consts", cst[:], consts), ("qb0", wqb0, wqb[0:P]), ("kb0", wkb0, wkb[0:P]),
                    ("qb1", wqb1[0:DN - P], wqb[P:DN]), ("kb1", wkb1[0:DN - P], wkb[P:DN]),
                    ("x", x_all[:], x.rearrange("(t p) d -> p t d", p=P)), ("ctx", ctxT_all, ctxT),
                    ("wkv", WkvT, wkvT), ("wq", WqT, wqT.rearrange("(k p) n -> p k n", p=P)),
                    ("wout", WoutT, woutT.rearrange("(k p) n -> p k n", p=P)),
                    ("wa", WaT, waT.rearrange("(k p) n -> p k n", p=P)),
                    ("lnq0", lnq0, lnq[0:P]), ("lnq1", lnq1[0:QR - P], lnq[P:QR]), ("lnkv", lnk, lnkv),
                    ("wvb", WvbT, wvbT), ("qr0", WqrT0, wqrT[0:P]), ("qr1", WqrT1[0:QR - P], wqrT[P:QR]),
                    ("wo", WoT, woT.rearrange("(k p) n -> p k n", p=P))):
                sp.dma_start(dst, src).then_inc(loaded[name][0], 16)
            with sp.Fori(0, NI) as i:
                for s in range(G):
                    sp.wait_ge(ln_done[0], at(ln_done, i, 5 + s))
                    sp.dma_start(x3n_rows[bass.ds((i * G + s) * P, P), :], xn[:, s, :]).then_inc(rows_stored[0], 16)
                sp.wait_ge(rows_stored[0], at(rows_stored, i, 16 * G))
                sp.sem_inc(rows_gone[0], 1)
            for k in range(2):
                sp.wait_ge(copied[k][0], at(copied[k], NI, 0))
            sp.dma_start(WgT, gateT.rearrange("(k p) n -> p k n", p=P)).then_inc(loaded["gate"][0], 16)
            sp.dma_start(WsgT, sgT.rearrange("(k p) n -> p k n", p=P)).then_inc(loaded["sg"][0], 16)
            sp.dma_start(WsuT, suT.rearrange("(k p) n -> p k n", p=P)).then_inc(loaded["su"][0], 16)
            sp.dma_start(WsdT, sdT.rearrange("(k p) n -> p k n", p=P)).then_inc(loaded["sd"][0], 16)

            def load_expert(i, r):
                e = i * R + r
                sp.dma_start(wgu[:, r], gate_up[bass.ds(e, 1)].rearrange("o (k p) n -> p (o k) n", p=P)).then_inc(w_loaded[r][0], 16)
                rows = down[bass.ds(e, 1)].rearrange("o (f m) n -> m (o f) n", m=3)
                for m in range(3):
                    dst = wd1[0:H3, r] if m == 2 else wd0[m * H3:(m + 1) * H3, r]
                    sp.dma_start(dst, rows[m]).then_inc(w_loaded[r][0], 16)

            for r in range(R):
                load_expert(0, r)
            for h in range(2):
                sp.wait_ge(down_added[0], (h + 1) * NT // 2)
                sp.dma_start(sums[h * TOK // 2:(h + 1) * TOK // 2].rearrange("(t p) d -> p t d", p=P),
                             x_all[:, h * NT // 2:(h + 1) * NT // 2]).then_inc(sums_stored[0], 16)
            with sp.Fori(1, E // R) as i:
                for r in range(R):
                    sp.wait_ge(eo_filled[0], i * R + (r + 1 - R))
                    load_expert(i, r)
            sp.wait_ge(added[0], 16 * E)
            sp.dma_start(out, sums[0:TOK]).then_inc(out_stored[0], 16)
            sp.wait_ge(out_stored[0], 16)

        @block.gpsimd
        def _(pool):
            def stand():
                nc.gpsimd.tensor_tensor(small[:, 61:62], eps5, eps5, ALU.add)

            pool.memset(x3nT[:, 0, 0:D], 0.0).then_inc(zero_ready[0], 1)
            pool.wait_ge(zero_ready[0], 1)
            pool.dma_start(x3n_rows[TOK:ROWS], x3nT[:, 0, 0:D]).then_inc(spare_stored[0], 16)
            pool.dma_start(sums[TOK:ROWS], x3nT[:, 0, 0:D]).then_inc(spare_stored[0], 16)
            pool.wait_ge(spare_stored[0], 32)
            pool.wait_ge(loaded["consts"][0], 16)
            pool.wait_ge(loaded["ctx"][0], 16)
            nc.gpsimd.memset(krz, 0.0).then_inc(zeros_ready[0], 1)
            pool.wait_ge(zeros_ready[0], 1)
            with pool.Fori(0, NI) as i:
                for k in range(2):
                    pool.wait_ge(filled[k][0], at(filled[k], i, 0))
                nc.gpsimd.tensor_copy(ctx_cur, ctxT_all[:, bass.ds(i * GT, GT)]).then_inc(ctx_ready[0], 1)
                for kind, n in ORDER:
                    if kind == "S" and not unit(n)[0]:
                        _, s, hg = unit(n)
                        if n == 0:
                            wait_copied(pool, i, "k1")
                        pool.wait_ge(scores_ready[0], at(scores_ready, i, max(n - 1, 0)))
                        nc.gpsimd.tensor_tensor(
                            kz[:, n % 2], kT[:, hg, s * P:(s + 1) * P].unsqueeze(1).to_broadcast([P, 4, P]),
                            cst[:, C_HEAD:C_HEAD + 4].unsqueeze(2).to_broadcast([P, 4, P]), ALU.mult).then_inc(kz_ready[0], 1)
                    elif kind == "R":
                        pool.wait_ge(rden_ready[0], at(rden_ready, i, n + 1))
                        nc.gpsimd.tensor_tensor(
                            probs[:, n % 3], probs[:, n % 3], rden[:, n % 3, :].unsqueeze(2).to_broadcast([P, 4, P]),
                            ALU.mult).then_inc(norm_done[0], 1)
            pool.wait_ge(choice_ready[0], 1)
            for t in range(NT):
                nc.gpsimd.tensor_scalar(
                    pair[:, t * TOPK:(t + 1) * TOPK, 0], choice[:, t * TOPK:(t + 1) * TOPK],
                    cst[:, C_TOK + t:C_TOK + t + 1], None, ALU.mult)
                last = nc.gpsimd.tensor_tensor(
                    pair[:, t * TOPK:(t + 1) * TOPK, 1], choice[:, t * TOPK:(t + 1) * TOPK],
                    top_w[:, t, 0:TOPK].unsqueeze(2).to_broadcast([P, TOPK, E]), ALU.mult)
            last.then_inc(pair_ready[0], 1)

            def rows_in_place(dst, e, n):
                nc.gpsimd.tensor_copy(dst, row_of[:, bass.ds(e, 1)]).then_inc(rows_copied[0], 1)
                pool.wait_ge(rows_copied[0], n + 1)
                stand()

            def gather(i, r, n):
                pool.wait_ge(gx_turned[0], i * R + (r + 1 - R))
                rows_in_place(gather_rows[:, r:r + 1], i * R + r, n)
                nc.gpsimd.indirect_dma_start(
                    gx[:, r], None, x3n_rows, bass.IndirectOffsetOnAxis(gather_rows[:, r:r + 1], 0)
                ).then_inc(gx_loaded[r][0], 16)

            def add(i, r, n):
                pool.wait_ge(eo_ready[0], at(eo_ready, i, r + 1))
                rows_in_place(add_rows[:, r:r + 1], i * R + r, n)
                nc.gpsimd.indirect_dma_start(
                    sums, bass.IndirectOffsetOnAxis(add_rows[:, r:r + 1], 0), eo[:, r], None,
                    compute_op=ALU.add).then_inc(added[0], 16)

            pool.wait_ge(rows_known[0], 1)
            pool.wait_ge(rows_stored[0], at(rows_stored, NI, 0))
            for r in range(R):
                nc.gpsimd.indirect_dma_start(
                    gx[:, r], None, x3n_rows, bass.IndirectOffsetOnAxis(row_of[:, r:r + 1], 0)
                ).then_inc(gx_loaded[r][0], 16)
            pool.wait_ge(sums_stored[0], 32)
            with pool.Fori(0, E // R - 1) as i:
                for r in range(R):
                    add(i, r, i * 2 * R + 2 * r)
                    gather(i + 1, r, i * 2 * R + 2 * r + 1)
                    pool.wait_ge(added[0], at(added, i, 16 * (r + 1)))
            for r in range(R):
                add(E // R - 1, r, (E // R - 1) * 2 * R + r)
                pool.wait_ge(added[0], at(added, E // R - 1, 16 * (r + 1)))

        @block.scalar
        def _(act):
            prime(act, av_copied, copied[0])
            for m in range(MH // 2):
                act.wait_ge(m_filled[m % 2][0], m // 2 + 1)
                bank = job_bank[m % 2][:, :].rearrange("p (a b c) -> p a b c", a=2, c=P)
                nc.scalar.copy(M0[:, 2 * m:2 * m + 2], bank[:, 0])
                nc.scalar.copy(M1[0:QR - P, 2 * m:2 * m + 2], bank[0:QR - P, 1]).then_inc(m_copied[m % 2][0], 1)
            act.wait_ge(loaded["consts"][0], 16)

            def to(i, name, dst, src=None):
                wait_filled(act, i, name)
                nc.scalar.copy(dst, bank_of(name)[:, :] if src is None else src).then_inc(copied[JOB[name] % 2][0], 1)

            with act.Fori(0, NI) as i:
                for kind, n in ORDER:
                    if kind == "ln":
                        act.wait_ge(ln_var[0], at(ln_var, i, n + 1))
                        nc.scalar.activation(std[:, n % 2:n % 2 + 1], mv[:, n % 2, 1:2], ACT.Sqrt, bias=eps5).then_inc(ln_std[0], 1)
                    elif kind == "S":
                        scale = float(DN + DR) ** -0.5 if unit(n)[0] else float(XD) ** -0.5
                        act.wait_ge(masked_ready[0], at(masked_ready, i, n + 1))
                        act.wait_ge(pT_ready[0], at(pT_ready, i, max(n - 2, 0)))
                        for j in range(4):
                            last = nc.scalar.activation(
                                probs[:, n % 3, j], masked[:, n % 2, j], ACT.Exp, bias=nmx[:, n % 3, j:j + 1],
                                scale=scale, accum_out=den[:, n % 3, j:j + 1])
                        last.then_inc(exp_done[0], 1)
                    elif kind == "A":
                        second, s, hg = unit(n)
                        act.wait_ge(av_ready[0], at(av_ready, i, n + 1))
                        if second:
                            nc.scalar.copy(c2T[:, 2 * hg:2 * hg + 2, s * P:(s + 1) * P],
                                           a_bank[n % 2][:, 0:2 * P].rearrange("p (a b) -> p a b", b=P)).then_inc(av_copied[0], 1)
                        else:
                            nc.scalar.copy(cT[:, hg, s * P:(s + 1) * P], a_bank[n % 2][:, 0:P]).then_inc(av_copied[0], 1)
                    elif kind == "job":
                        if n in ("k0", "k1"):
                            c = int(n[1])
                            to(i, n, kT[:, 2 * c:2 * c + 2].rearrange("p a b -> p (a b)"))
                        elif n in ("xT0", "x2T0", "x2T1"):
                            s = int(n[-1])
                            to(i, n, xnT[:, :, s * P:(s + 1) * P], bank_of(n)[:, :].rearrange("p (k t) -> p k t", t=P))
                        elif n == "q0":
                            to(i, n, qT[:, 0:2].rearrange("p a b -> p (a b)"))
                        elif n in ("a0", "a1"):
                            s = int(n[1])
                            wait_filled(act, i, n)
                            nc.scalar.activation(junk[:, 0:QR], bank_of(n)[:, 0:QR], ACT.Square, accum_out=ss[:, s, 0:1])
                            nc.scalar.activation(junk[:, QR:QR + KL], bank_of(n)[:, QR:QR + KL], ACT.Square,
                                                 accum_out=ss[:, s, 1:2]).then_inc(rms_sum[0], 1)
                            act.wait_ge(rms_sum[0], at(rms_sum, i, s + 1))
                            nc.scalar.activation(rms[:, s, 0:1], ss[:, s, 0:1], ACT.Sqrt, bias=eps6, scale=1.0 / QR)
                            nc.scalar.activation(rms[:, s, 1:2], ss[:, s, 1:2], ACT.Sqrt, bias=eps6,
                                                 scale=1.0 / KL).then_inc(rms_std[0], 1)
                        elif n.startswith("v2_") and n != "v2_4":
                            s, half = int(n[3]) // 2, int(n[3]) % 2
                            to(i, n, v2[:, s, half * 512:(half + 1) * 512])
                        elif n == "v2_4":
                            to(i, n, v2[:, :, 1024:MH * DV], bank_of(n)[:, :].rearrange("p (s n) -> p s n", s=G))
                        elif n[0] == "r":
                            m = int(n[1])
                            to(i, n, qr[:, 2 * m:2 * m + 2].rearrange("p a b -> p (a b)"))
                        elif n[0] == "l" and int(n[1]) % 2 == 0:
                            m = int(n[1])
                            to(i, n, ql[:, 2 * m:2 * m + 2].rearrange("p a b -> p (a b)"))
                        elif n in ("x3T0", "x3T1"):
                            s = int(n[-1])
                            to(i, n, x3nT[:, :, bass.ds(i * GT + s * P, P)], bank_of(n)[:, :].rearrange("p (k t) -> p k t", t=P))
            for n in range(2):
                act.wait_ge(gate_filled[0], n + 1)
                nc.scalar.copy(lgT[0:E, n * 512:(n + 1) * 512], job_bank[n][0:E, :]).then_inc(gate_copied[0], 1)
            for n in range(2 * (SI // P)):
                act.wait_ge(up_filled[0], n + 1)
                if n >= 2:
                    act.wait_ge(up_done[0], n - 1)
                nc.scalar.activation(silu_s[:, n % 2], [s_bank, t_bank][n % 2][0][:, :], ACT.Silu).then_inc(up_silu[0], 1)
                if n == 0:
                    act.wait_ge(lg_shifted[0], 1)
                    nc.scalar.activation(ex, lg, ACT.Exp).then_inc(lg_exp[0], 1)
            act.wait_ge(table_filled[0], 1)
            nc.scalar.copy(silu_e[:, 0, 0:P], a_bank[1][:, 0:P]).then_inc(table_copied[0], 1)

            def expert(i, r):
                act.wait_ge(gx_turned[0], at(gx_turned, i, r + 1))
                act.wait_ge(gu_filled[0], i * R + max(r - 1, 0) if type(i) is int and i == 0 else i * R + (r - 1))
                nc.scalar.copy(gxT[:, r % 2], t_bank[r % 2][:, :]).then_inc(gxT_copied[0], 1)
                act.wait_ge(gu_filled[0], at(gu_filled, i, r + 1))
                act.wait_ge(hid_ready[0], i * R + max(r - 1, 0) if type(i) is int and i == 0 else i * R + (r - 1))
                nc.scalar.activation(silu_e[0:H3, r % 2], s_bank[r % 2][0:H3, 0:3 * P], ACT.Silu).then_inc(silu_done[0], 1)

            act.wait_ge(table_turned[0], 1)
            for r in range(R):
                expert(0, r)
            with act.Fori(1, E // R) as i:
                for r in range(R):
                    expert(i, r)

        @block.vector
        def _(dve):
            prime(dve, masked_ready, pT_copied, copied[1])
            for n in ("consts", "x", "lnq0", "lnq1", "lnkv"):
                dve.wait_ge(loaded[n][0], 16)
            dve.wait_ge(zeros_ready[0], 1)
            with dve.Fori(0, NI) as i:
                links = [0]

                def link(ins):
                    links[0] += 1
                    ins.then_inc(dve_chain[0], 1)
                    dve.wait_ge(dve_chain[0], at(dve_chain, i, links[0]))

                def stand():
                    nc.vector.memset(small[:, 60:61], 0.0)

                def to(name, dst, src=None):
                    wait_filled(dve, i, name)
                    nc.vector.tensor_copy(dst, bank_of(name)[:, :] if src is None else src).then_inc(copied[JOB[name] % 2][0], 1)

                for kind, n in ORDER:
                    if kind == "ln":
                        s = n % 2
                        xs = x_all[:, bass.ds(i * G + s, 1), :].rearrange("p o d -> p (o d)")
                        if n == 0:
                            dve.wait_ge(rows_gone[0], at(rows_gone, i, 0))
                        elif n >= 2:
                            wait_copied(dve, i, f"o{s}" if n < 4 else f"o2_{s}")
                        stand()
                        link(nc.vector.bn_stats(stat, xs))
                        stand()
                        nc.vector.bn_aggr(mv[:, s], stat).then_inc(ln_var[0], 1)
                        dve.wait_ge(ln_std[0], at(ln_std, i, n + 1))
                        link(nc.vector.reciprocal(rstd[:, s:s + 1], std[:, s:s + 1]))
                        nc.vector.tensor_scalar(xn[:, s], xs, mv[:, s, 0:1], rstd[:, s:s + 1],
                                                ALU.subtract, ALU.mult).then_inc(ln_done[0], 1)
                    elif kind == "S":
                        dve.wait_ge(scores_ready[0], at(scores_ready, i, n + 1))
                        stand()
                        for j in range(4):
                            last = nc.vector.tensor_tensor_reduce(
                                out=masked[:, n % 2, j], in0=s_bank[n % 2][:, j * P:(j + 1) * P], in1=mask,
                                scale=1.0, scalar=FLOOR, op0=ALU.add, op1=ALU.max, accum_out=mx[:, n % 3, j:j + 1])
                        link(last)
                        scale = float(DN + DR) ** -0.5 if unit(n)[0] else float(XD) ** -0.5
                        nc.vector.tensor_scalar(nmx[:, n % 3], mx[:, n % 3], -scale, None, ALU.mult).then_inc(masked_ready[0], 1)
                    elif kind == "R":
                        dve.wait_ge(exp_done[0], at(exp_done, i, n + 1))
                        nc.vector.reciprocal(rden[:, n % 3], den[:, n % 3]).then_inc(rden_ready[0], 1)
                    elif kind == "T":
                        dve.wait_ge(pT_ready[0], at(pT_ready, i, n + 1))
                        dve.wait_ge(av_ready[0], at(av_ready, i, max(n - 1, 0)))
                        nc.vector.tensor_copy(probsT[:, n % 2].rearrange("p a b -> p (a b)"), t_bank[n % 2][:, :]).then_inc(pT_copied[0], 1)
                    elif kind == "job":
                        if n in ("v0", "v1"):
                            to(n, v[:, int(n[1])])
                        elif n == "xT1":
                            to(n, xnT[:, :, P:2 * P], bank_of(n)[:, :].rearrange("p (k t) -> p k t", t=P))
                        elif n == "q1":
                            to(n, qT[:, 2:4].rearrange("p a b -> p (a b)"))
                        elif n[0] == "l" and int(n[1]) % 2 == 1:
                            m = int(n[1])
                            to(n, ql[:, 2 * m:2 * m + 2].rearrange("p a b -> p (a b)"))
                        elif n[0] == "o":
                            s = int(n[-1])
                            xs = x_all[:, bass.ds(i * G + s, 1), :].rearrange("p o d -> p (o d)")
                            wait_filled(dve, i, n)
                            nc.vector.tensor_tensor(xs, xs, bank_of(n)[:, :], ALU.add).then_inc(copied[JOB[n] % 2][0], 1)
                        elif n in ("a0", "a1"):
                            s, bank = int(n[1]), bank_of(n)
                            kr = bank[:, QR + KL:QR + KL + DR]
                            cos, sin, h = cst[:, C_COS:C_COS + DR], cst[:, C_SIN:C_SIN + DR], DR // 2
                            dve.wait_ge(rms_std[0], at(rms_std, i, s + 1))
                            link(nc.vector.reciprocal(rrms[:, s], rms[:, s]))
                            nc.vector.tensor_scalar(an[:, s, 0:QR], bank[:, 0:QR], rrms[:, s, 0:1], None, ALU.mult)
                            nc.vector.tensor_scalar(an[:, s, QR:QR + KL], bank[:, QR:QR + KL], rrms[:, s, 1:2], None, ALU.mult)
                            nc.vector.tensor_tensor(rot1, kr, cos, ALU.mult)
                            nc.vector.tensor_tensor(rot2[:, 0:h], kr[:, h:DR], sin[:, 0:h], ALU.mult)
                            link(nc.vector.tensor_tensor(rot2[:, h:DR], kr[:, 0:h], sin[:, h:DR], ALU.mult))
                            for c in range(2):
                                last = nc.vector.tensor_tensor(an[:, s, QR + KL + c * DR:QR + KL + (c + 1) * DR], rot1, rot2, ALU.add)
                            last.then_inc(copied[JOB[n] % 2][0], 1)
                        elif n in ("aT0", "aT1"):
                            s, bank = int(n[2]), bank_of(n)
                            cols = slice(s * P, (s + 1) * P)
                            wait_filled(dve, i, n)
                            nc.vector.tensor_scalar(qc0[:, cols], bank[:, 0:P], lnq0, None, ALU.mult)
                            nc.vector.tensor_scalar(qc1[0:QR - P, cols], bank[0:QR - P, P:2 * P], lnq1[0:QR - P], None, ALU.mult)
                            nc.vector.tensor_scalar(klT[:, cols], bank[:, 2 * P:3 * P], lnk, None, ALU.mult)
                            nc.vector.tensor_copy(krz[0:DR, 0, cols], bank[0:DR, 3 * P:4 * P])
                            nc.vector.tensor_copy(krz[DR:2 * DR, 1, cols], bank[DR:2 * DR, 3 * P:4 * P]).then_inc(copied[JOB[n] % 2][0], 1)
                assert links[0] == DVE_LINKS

            count = [0]

            def link(ins):
                count[0] += 1
                ins.then_inc(route_chain[0], 1)
                dve.wait_ge(route_chain[0], count[0])

            def bc8(v8):
                return v8.unsqueeze(2).to_broadcast([P, NT, E])

            def shared_product(n):
                m, half = n % (SI // P), n // (SI // P)
                dve.wait_ge(up_silu[0], n + 1)
                nc.vector.tensor_tensor(hidT[:, m, half * 512:(half + 1) * 512], silu_s[:, n % 2],
                                        [s_bank, t_bank][n % 2][1][:, :], ALU.mult).then_inc(up_done[0], 1)

            dve.wait_ge(logits_ready[0], 1)
            logits = a_bank[0][:, :].rearrange("p (t e) -> p t e", e=E)
            link(nc.vector.tensor_reduce(mx8, logits, AX.X, ALU.max))
            nc.vector.tensor_tensor(lg, logits, bc8(mx8), ALU.subtract).then_inc(lg_shifted[0], 1)
            shared_product(0)
            dve.wait_ge(lg_exp[0], 1)
            link(nc.vector.tensor_reduce(sum8, ex, AX.X, ALU.add))
            link(nc.vector.reciprocal(rsum8, sum8))
            link(nc.vector.tensor_tensor(lg, ex, bc8(rsum8), ALU.mult))
            for t in range(NT):
                last = nc.vector.max(top_w[:, t], lg[:, t])
            link(last)
            shared_product(1)
            for t in range(NT):
                last = nc.vector.max_index(top_i[:, t], top_w[:, t], lg[:, t])
            link(last)
            link(nc.vector.tensor_copy(top_f, top_i))
            for t in range(NT):
                last = nc.vector.tensor_tensor(
                    choice[:, t * TOPK:(t + 1) * TOPK], cst[:, C_IOTA:C_IOTA + E].unsqueeze(1).to_broadcast([P, TOPK, E]),
                    top_f[:, t, 0:TOPK].unsqueeze(2).to_broadcast([P, TOPK, E]), ALU.is_equal)
                if t == NT // 2:
                    shared_product(2)
            last.then_inc(choice_ready[0], 1)
            dve.wait_ge(choice_ready[0], 1)
            link(nc.vector.tensor_reduce(chosen_by, choice.rearrange("p (t k) e -> p t e k", k=TOPK), AX.X, ALU.add))
            shared_product(3)
            link(nc.vector.memset(before[:, 0], 0.0))
            for t in range(1, NT):
                last = nc.vector.tensor_tensor(before[:, t], before[:, t - 1], chosen_by[:, t - 1], ALU.add)
                if t < NT - 1:
                    link(last)
            last.then_inc(before_ready[0], 1)
            shared_product(4)
            shared_product(5)
            dve.wait_ge(pos_filled[0], 1)
            for t in range(NT):
                last = nc.vector.tensor_tensor(
                    scratch[:, t * TOPK:(t + 1) * TOPK], choice[:, t * TOPK:(t + 1) * TOPK],
                    a_bank[0][:, t * E:(t + 1) * E].unsqueeze(1).to_broadcast([P, TOPK, E]), ALU.mult)
            link(last)
            link(nc.vector.tensor_reduce(rank_of, scratch, AX.X, ALU.add))
            for n in range(NT * TOPK):
                last = nc.vector.tensor_scalar(hot[:, n], cst[:, C_IOTA:C_IOTA + P], rank_of[:, n:n + 1], None, ALU.is_equal)
                if n % TOPK == TOPK - 1:
                    last.then_inc(hot_ready[0], 1)
            for t in range(NT):
                dve.wait_ge(down_filled[0], t + 1)
                nc.vector.tensor_tensor(x_all[:, t], x_all[:, t], [s_bank, t_bank][t % 2][t // 2 % 2][:, :], ALU.add).then_inc(down_added[0], 1)
            dve.wait_ge(table_turned[0], 1)
            link(nc.vector.tensor_copy(idx_w.rearrange("p a b -> p (a b)"), a_bank[1][:, P:2 * P]))
            link(nc.vector.tensor_scalar(spare, idx_w[:, 0], 0.0, cst[:, C_SPARE:C_SPARE + 1], ALU.is_equal, ALU.mult))
            nc.vector.scalar_tensor_tensor(row_of, idx_w[:, 0], -1.0, spare, ALU.add, ALU.add).then_inc(rows_known[0], 1)

            def expert(i, r):
                dve.wait_ge(silu_done[0], at(silu_done, i, r + 1))
                dve.wait_ge(eo_filled[0], i * R + max(r - 1, 0) if type(i) is int and i == 0 else i * R + (r - 1))
                g = silu_e[0:H3, r % 2].rearrange("p (m t) -> p m t", t=P)
                u = s_bank[r % 2][H3:2 * H3, 0:3 * P].rearrange("p (m t) -> p m t", t=P)
                nc.vector.tensor_tensor(hid_e[0:H3, r % 2].rearrange("p (m t) -> p m t", t=P), g[:, 0:3:2], u[:, 0:3:2], ALU.mult)
                nc.vector.tensor_tensor(hid_e[H3:2 * H3, r % 2, 0:P], g[:, 1], u[:, 1], ALU.mult).then_inc(hid_ready[0], 1)

            def output(i, r):
                dve.wait_ge(eo_filled[0], at(eo_filled, i, r + 1))
                if not (type(i) is int and i == 0):
                    dve.wait_ge(added[0], 16 * (i * R + (r + 1 - R)))
                e = i * R + r
                w = idx_w[:, 1, bass.ds(e, 1)] if type(i) is not int else idx_w[:, 1, e:e + 1]
                nc.vector.tensor_scalar(eo[:, r], job_bank[r % 2][:, :], w, None, ALU.mult).then_inc(eo_ready[0], 1)

            for r in range(R):
                expert(0, r)
                if r:
                    output(0, r - 1)
            with dve.Fori(1, E // R) as i:
                for r in range(R):
                    expert(i, r)
                    output(i - 1, R - 1) if r == 0 else output(i, r - 1)
            output(E // R - 1, R - 1)

        @block.tensor
        def _(pe):
            prime(pe, *filled, scores_ready, pT_ready, av_ready)
            mm = nc.tensor.matmul
            for n in ("qb0", "kb0", "qb1", "kb1"):
                pe.wait_ge(loaded[n][0], 16)
            for m in range(MH // 2):
                if m >= 2:
                    pe.wait_ge(m_copied[m % 2][0], m // 2)
                for a, (r0, rn) in enumerate(((0, P), (P, QR - P))):
                    for b in range(2):
                        h = 2 * m + b
                        o = job_bank[m % 2][0:rn, (2 * a + b) * P:(2 * a + b + 1) * P]
                        mm(o, wqb0[:, h, r0:r0 + rn], wkb0[:, h], start=True, stop=False)
                        last = mm(o, wqb1[0:DN - P, h, r0:r0 + rn], wkb1[0:DN - P, h], start=False, stop=True)
                last.then_inc(m_filled[m % 2][0], 1)
            for k in range(2):
                pe.wait_ge(m_copied[k][0], MH // 4)
            for n in ("consts", "ctx", "wkv", "wq", "wout", "wa", "wvb", "qr0", "qr1", "wo"):
                pe.wait_ge(loaded[n][0], 16)

            with pe.Fori(0, NI) as i:
                def also_copied(job, name):
                    if JOB[name] % 2 != JOB[job] % 2:
                        wait_copied(pe, i, name)

                for kind, n in ORDER:
                    if kind == "job":
                        bank, slot = bank_of(n), JOB[n] % 2
                        pe.wait_ge(copied[slot][0], at(copied[slot], i, JOB[n] // 2))
                        if n in ("k0", "k1"):
                            c = int(n[1])
                            for m in range(2):
                                f = (2 * c + m) * P
                                last = mm(bank[:, m * GT:(m + 1) * GT], WkvT[:, f:f + P],
                                          ctxT_all[:, bass.ds(i * GT, GT)], start=True, stop=True)
                        elif n in ("v0", "v1"):
                            s = int(n[1])
                            pe.wait_ge(ctx_ready[0], at(ctx_ready, i, 1))
                            last = mm(bank[:, :], ctx_cur[:, s * P:(s + 1) * P], WkvT[:, D:2 * D], start=True, stop=True)
                        elif n in ("xT0", "xT1", "x2T0", "x2T1", "x3T0", "x3T1"):
                            s = int(n[-1])
                            which = {"x": 0, "2": 2, "3": 4}[n[1] if n[1] != "T" else "x"]
                            pe.wait_ge(ln_done[0], at(ln_done, i, which + s + 1))
                            for k in range(KD):
                                last = nc.tensor.transpose(bank[:, k * P:(k + 1) * P], xn[:, s, k * P:(k + 1) * P], ident)
                        elif n in ("q0", "q1"):
                            c = int(n[1])
                            for s in range(G):
                                also_copied(n, f"xT{s}")
                            for m in range(2):
                                f = (2 * c + m) * P
                                for k in range(KD):
                                    last = mm(bank[:, m * GT:(m + 1) * GT], WqT[:, k, f:f + P], xnT[:, k], start=k == 0, stop=k == KD - 1)
                        elif n in ("o0", "o1"):
                            s = int(n[1])
                            pe.wait_ge(av_copied[0], at(av_copied, i, 4 * (s + 1)))
                            for k in range(KD):
                                last = mm(bank[:, :], cT[:, k, s * P:(s + 1) * P], WoutT[:, k], start=k == 0, stop=k == KD - 1)
                        elif n in ("a0", "a1"):
                            s = int(n[1])
                            also_copied(n, f"x2T{s}")
                            for k in range(KD):
                                last = mm(bank[:, 0:QR + KL + DR], xnT[:, k, s * P:(s + 1) * P], WaT[:, k], start=k == 0, stop=k == KD - 1)
                        elif n in ("aT0", "aT1"):
                            s = int(n[2])
                            also_copied(n, f"a{s}")
                            for c, (f, w) in enumerate(((0, P), (P, QR - P), (QR, KL), (QR + KL, 2 * DR))):
                                last = nc.tensor.transpose(bank[0:w, c * P:(c + 1) * P], an[:, s, f:f + w], ident)
                        elif n[0:2] == "v2":
                            c = int(n[3])
                            if c == 4:
                                for s in range(G):
                                    last = mm(bank[:, s * 256:(s + 1) * 256], klT[:, s * P:(s + 1) * P], WvbT[:, 1024:MH * DV], start=True, stop=True)
                            else:
                                s = c // 2
                                also_copied(n, f"aT{s}")
                                last = mm(bank[:, :], klT[:, s * P:(s + 1) * P], WvbT[:, c % 2 * 512:c % 2 * 512 + 512], start=True, stop=True)
                        elif n[0] == "r":
                            for m in range(2):
                                f, o = (2 * int(n[1]) + m) * P, bank[:, m * GT:(m + 1) * GT]
                                mm(o, WqrT0[:, f:f + P], qc0, start=True, stop=False)
                                last = mm(o, WqrT1[0:QR - P, f:f + P], qc1[0:QR - P], start=False, stop=True)
                        elif n[0] == "l":
                            for m in range(2):
                                h, o = 2 * int(n[1]) + m, bank[:, m * GT:(m + 1) * GT]
                                mm(o, M0[:, h], qc0, start=True, stop=False)
                                last = mm(o, M1[0:QR - P, h], qc1[0:QR - P], start=False, stop=True)
                        elif n in ("o2_0", "o2_1"):
                            s = int(n[3])
                            pe.wait_ge(av_copied[0], at(av_copied, i, XU + MU // 2 * (s + 1)))
                            for k in range(MH // 2):
                                last = mm(bank[:, :], c2T[:, k, s * P:(s + 1) * P], WoT[:, k], start=k == 0, stop=k == MH // 2 - 1)
                        last.then_inc(filled[slot][0], 1)
                    elif kind == "S":
                        second, s, hg = unit(n)
                        cols = slice(s * P, (s + 1) * P)
                        pe.wait_ge(masked_ready[0], at(masked_ready, i, max(n - 1, 0)))
                        if n == 0:
                            for c in ("q0", "q1"):
                                wait_copied(pe, i, c)
                        if second and s == 0:
                            for c in range(2):
                                wait_copied(pe, i, f"l{2 * hg + c}")
                        if second:
                            for j in range(4):
                                o, h = s_bank[n % 2][:, j * P:(j + 1) * P], 4 * hg + j
                                mm(o, ql[:, h, cols], klT[:, cols], start=True, stop=False)
                                last = mm(o, qr[:, h // 2, cols], krz[:, h % 2, cols], start=False, stop=True)
                        else:
                            pe.wait_ge(kz_ready[0], at(kz_ready, i, n + 1))
                            last = mm(s_bank[n % 2][:, :], qT[:, hg, cols], kz[:, n % 2].rearrange("p a b -> p (a b)"), start=True, stop=True)
                        last.then_inc(scores_ready[0], 1)
                    elif kind == "T":
                        pe.wait_ge(norm_done[0], at(norm_done, i, n + 1))
                        pe.wait_ge(pT_copied[0], at(pT_copied, i, max(n - 1, 0)))
                        for j in range(4):
                            last = nc.tensor.transpose(t_bank[n % 2][:, j * P:(j + 1) * P], probs[:, n % 3, j], ident)
                        last.then_inc(pT_ready[0], 1)
                    elif kind == "A":
                        second, s, hg = unit(n)
                        pe.wait_ge(pT_copied[0], at(pT_copied, i, n + 1))
                        pe.wait_ge(av_copied[0], at(av_copied, i, max(n - 1, 0)))
                        if n == 0:
                            for c in ("v0", "v1"):
                                wait_copied(pe, i, c)
                        elif n == XU:
                            wait_copied(pe, i, "v2_4")
                        for j in range(4):
                            h = 4 * hg + j
                            if second:
                                o = a_bank[n % 2][DV * (j % 2):DV * (j % 2) + DV, j // 2 * P:j // 2 * P + P]
                                last = mm(o, v2[:, s, h * DV:(h + 1) * DV], probsT[:, n % 2, j], start=True, stop=True)
                            else:
                                last = mm(a_bank[n % 2][XD * j:XD * (j + 1), 0:P], v[:, s, h * XD:(h + 1) * XD],
                                          probsT[:, n % 2, j], start=True, stop=True)
                        last.then_inc(av_ready[0], 1)

            for k in range(2):
                pe.wait_ge(copied[k][0], at(copied[k], NI, 0))
            pe.wait_ge(loaded["gate"][0], 16)
            for n in range(2):
                for k in range(KD):
                    last = mm(job_bank[n][0:E, :], WgT[:, k], x3nT[:, k, n * 512:(n + 1) * 512], start=k == 0, stop=k == KD - 1)
                last.then_inc(gate_filled[0], 1)
            pe.wait_ge(gate_copied[0], 2)
            pe.wait_ge(av_copied[0], at(av_copied, NI, 0))
            for t in range(NT):
                last = nc.tensor.transpose(a_bank[0][:, t * E:(t + 1) * E], lgT[0:E, t * P:(t + 1) * P], cst[0:E, C_ID:C_ID + E])
            last.then_inc(logits_ready[0], 1)
            pe.wait_ge(loaded["sg"][0], 16)
            pe.wait_ge(loaded["su"][0], 16)
            for n in range(2 * (SI // P)):
                m, half = n % (SI // P), n // (SI // P)
                if n >= 2:
                    pe.wait_ge(up_done[0], n - 1)
                for b, w in enumerate((WsgT, WsuT)):
                    for k in range(KD):
                        last = mm([s_bank, t_bank][n % 2][b][:, :], w[:, k, m * P:(m + 1) * P],
                                  x3nT[:, k, half * 512:(half + 1) * 512], start=k == 0, stop=k == KD - 1)
                last.then_inc(up_filled[0], 1)
            pe.wait_ge(before_ready[0], 1)
            mm(a_bank[0][:, :], cst[:, C_BEFORE:C_BEFORE + P], chosen_by.rearrange("p t e -> p (t e)"), start=True, stop=False)
            mm(a_bank[0][:, :], cst[:, C_ONES:C_ONES + P], before.rearrange("p t e -> p (t e)"), start=False, stop=True).then_inc(pos_filled[0], 1)
            pe.wait_ge(loaded["sd"][0], 16)
            pe.wait_ge(up_done[0], 2 * (SI // P))
            for t in range(NT):
                if t >= 4:
                    pe.wait_ge(down_added[0], t - 3)
                for k in range(SI // P):
                    last = mm([s_bank, t_bank][t % 2][t // 2 % 2][:, :], hidT[:, k, t * P:(t + 1) * P], WsdT[:, k], start=k == 0, stop=k == SI // P - 1)
                last.then_inc(down_filled[0], 1)
            pe.wait_ge(pair_ready[0], 1)
            for n in range(NT * TOPK):
                if n % TOPK == 0:
                    pe.wait_ge(hot_ready[0], n // TOPK + 1)
                last = mm(a_bank[1][:, 0:P], pair[:, n].rearrange("p a e -> p (a e)"), hot[:, n], start=n == 0, stop=n == NT * TOPK - 1)
            last.then_inc(table_filled[0], 1)
            pe.wait_ge(table_copied[0], 1)
            nc.tensor.transpose(a_bank[1][:, P:2 * P], silu_e[:, 0, 0:P], ident).then_inc(table_turned[0], 1)

            def before_down(i, r):
                first = type(i) is int and i == 0
                pe.wait_ge(gx_loaded[r][0], at(gx_loaded[r], i, 16))
                if not first or r >= 2:
                    pe.wait_ge(gxT_copied[0], i * R + (r - 1))
                for k in range(KD):
                    last = nc.tensor.transpose(t_bank[r % 2][:, k * P:(k + 1) * P], gx[:, r, k * P:(k + 1) * P], ident)
                last.then_inc(gx_turned[0], 1)
                pe.wait_ge(w_loaded[r][0], at(w_loaded[r], i, 64))
                pe.wait_ge(gxT_copied[0], at(gxT_copied, i, r + 1))
                if not first or r >= 2:
                    pe.wait_ge(hid_ready[0], i * R + (r - 1))
                w = wgu[:, r].rearrange("p k (f m) -> p k m f", m=3)
                for m in range(3):
                    for k in range(KD):
                        last = mm(s_bank[r % 2][:, m * P:(m + 1) * P], w[:, k, m],
                                  gxT[:, r % 2, k * P:(k + 1) * P], start=k == 0, stop=k == KD - 1)
                last.then_inc(gu_filled[0], 1)

            def down_product(i, r):
                first = type(i) is int and i == 0
                pe.wait_ge(hid_ready[0], at(hid_ready, i, r + 1))
                if not first or r >= 2:
                    pe.wait_ge(eo_ready[0], i * R + (r - 1))
                mm(job_bank[r % 2][:, :], hid_e[:, r % 2, 0:P], wd0[:, r], start=True, stop=False)
                mm(job_bank[r % 2][:, :], hid_e[0:H3, r % 2, P:2 * P], wd1[0:H3, r], start=False, stop=True).then_inc(eo_filled[0], 1)

            pe.wait_ge(rows_known[0], 1)
            for r in range(R):
                before_down(0, r)
                if r:
                    down_product(0, r - 1)
            with pe.Fori(1, E // R) as i:
                for r in range(R):
                    before_down(i, r)
                    down_product(i - 1, R - 1) if r == 0 else down_product(i, r - 1)
            down_product(E // R - 1, R - 1)


def kernel(x, ctx_512, L0_xattn_Wq, L0_xattn_Wkv_expand, L0_xattn_Wout, L0_attn_q_a_w, L0_attn_q_a_ln_w,
           L0_attn_q_b_w, L0_attn_kv_a_w, L0_attn_kv_a_ln_w, L0_attn_kv_b_w, L0_attn_o_w, L0_ffn_gate_w,
           L0_ffn_gate_up_proj, L0_ffn_down_proj, L0_ffn_shared_gate_w, L0_ffn_shared_up_w, L0_ffn_shared_down_w):
    import concourse.bacc as bacc
    from concourse.bass_utils import run_bass_kernel_spmd

    a = np.asarray
    qb = a(L0_attn_q_b_w).reshape(MH, DN + DR, QR)
    kvb = a(L0_attn_kv_b_w).reshape(MH, DN + DV, KL)
    arrays = {
        "x": a(x).reshape(TOK, D),
        "ctxT": a(ctx_512)[:, :SQ].transpose(2, 0, 1).reshape(XL, TOK),
        "consts": constant_table(),
        "wqT": a(L0_xattn_Wq).T, "wkvT": a(L0_xattn_Wkv_expand).T, "woutT": a(L0_xattn_Wout).T,
        "waT": np.concatenate([a(L0_attn_q_a_w), a(L0_attn_kv_a_w)], 0).T,
        "lnq": a(L0_attn_q_a_ln_w).reshape(QR, 1), "lnkv": a(L0_attn_kv_a_ln_w).reshape(KL, 1),
        "wqb": qb[:, :DN].transpose(1, 0, 2), "wqrT": qb[:, DN:].transpose(2, 0, 1).reshape(QR, MH * DR),
        "wkb": kvb[:, :DN].transpose(1, 0, 2), "wvbT": kvb[:, DN:].transpose(2, 0, 1).reshape(KL, MH * DV),
        "woT": a(L0_attn_o_w).T, "gateT": a(L0_ffn_gate_w).T,
        "gate_up": a(L0_ffn_gate_up_proj), "down": a(L0_ffn_down_proj),
        "sgT": a(L0_ffn_shared_gate_w).T, "suT": a(L0_ffn_shared_up_w).T, "sdT": a(L0_ffn_shared_down_w).T,
    }
    arrays = {k: np.ascontiguousarray(v) for k, v in arrays.items()}
    nc = bacc.Bacc("TRN2", target_bir_lowering=False, num_devices=1)
    aps = [nc.dram_tensor(k, v.shape, mybir.dt.from_np(v.dtype), kind="ExternalInput").ap() for k, v in arrays.items()]
    out = nc.dram_tensor("out", (TOK, D), mybir.dt.float32, kind="ExternalOutput").ap()
    build(nc, *aps, out)
    r = run_bass_kernel_spmd(nc, [arrays], core_ids=[0])
    return r.results[0]["out"].reshape(B, SQ, D)
```

```python
from contextlib import ExitStack

import numpy as np
import concourse.bass as bass
from concourse import mybir

B, SQ, D = 16, 64, 512
TOK = B * SQ
P = 128
NT = TOK // P
KD = D // P
XH, XD, XL = 16, 32, 128
MH, DN, DR, DV = 20, 192, 64, 64
QR, KL = 192, 128
E, TOPK, CAP, FI = 64, 6, 128, 192
SI = 2 * FI
H3 = FI // 3
R = 4
ROWS = TOK + CAP
NEG = -1.0e30
FLOOR = -3.0e38

C_ID, C_MASK, C_BEFORE, C_IOTA, C_ONES = 0, 128, 256, 384, 512
C_COS, C_SIN, C_TOK = 640, 704, 768
C_SPARE, C_EPS5, C_EPS6, C_HEAD, C_COLS = 776, 777, 778, 779, 784


def constant_table():
    c = np.zeros((P, C_COLS), np.float32)
    p = np.arange(P)
    c[:, C_ID:C_ID + P] = np.eye(P)
    same = (p[:, None] // SQ) == (p[None, :] // SQ)
    c[:, C_MASK:C_MASK + P] = np.where(same & (p[None, :] <= p[:, None]), 0.0, NEG)
    c[:, C_BEFORE:C_BEFORE + P] = p[:, None] < p[None, :]
    c[:, C_IOTA:C_IOTA + P] = p[None, :]
    c[:, C_ONES:C_ONES + P] = 1.0
    inv_freq = (1.0 / np.float32(1000000.0) ** (np.arange(0, DR, 2, dtype=np.float32) / np.float32(DR))).astype(np.float32)
    freqs = np.arange(SQ, dtype=np.float32)[:, None] * inv_freq[None, :]
    emb = np.concatenate([freqs, freqs], axis=-1)
    sign = np.where(np.arange(DR) < DR // 2, -1.0, 1.0).astype(np.float32)
    cos, sin = np.cos(emb), np.sin(emb) * sign
    c[:, C_COS:C_COS + DR] = np.tile(cos, (2, 1))
    c[:, C_SIN:C_SIN + DR] = np.tile(sin, (2, 1))
    c[:, C_TOK:C_TOK + NT] = P * np.arange(NT)[None, :] + p[:, None] + 1
    c[:, C_SPARE] = TOK + 1 + p
    c[:, C_HEAD:C_HEAD + 4] = p[:, None] // XD == np.arange(4)[None, :]
    c[:, C_EPS5] = 1e-5
    c[:, C_EPS6] = 1e-6
    return c


def attend(units, between):
    o = []
    for u in range(len(units) + 3):
        if u < len(units):
            o.append(("S",) + units[u])
        o.extend(between.get(u, []))
        for lag, kind in ((1, "R"), (2, "T"), (3, "A")):
            if 0 <= u - lag < len(units):
                o.append((kind,) + units[u - lag])
    return o


def job(t, *names):
    return [("job", n, t) for n in names]


def keys(t, *groups):
    return [("K", ("A", g), t) for g in groups]


def second_and_next(t, cross=True, start=True):
    b = [(("B", k), t) for k in range(MH // 4)]
    a = [(("A", k), t + 1) for k in range(XH // 4)]
    if cross:
        units = [a[0], a[1], b[0], b[1], a[2], b[2], a[3], b[3], b[4]]
        between = {1: job(t, "r0", "l0") + keys(t + 1, 2), 2: job(t, "l1"), 3: job(t, "v2_0", "r1") + keys(t + 1, 3),
                   4: job(t, "l2"), 5: job(t, "l3"), 6: job(t, "v2_1"), 7: job(t, "r2", "l4"), 8: job(t, "v2_2")}
        if start:
            between[4] = between[4] + [("stat", "ln1", t + 2)]
            between[5] = [("norm", "ln1", t + 2)] + between[5]
    else:
        units = b
        between = {0: job(t, "l1"), 1: job(t, "v2_0", "r1", "l2"), 2: job(t, "l3", "v2_1"), 3: job(t, "r2", "l4"), 4: job(t, "v2_2")}
    o = job(t, "aT") + (job(t, "r0", "l0") if not cross else [])
    if start:
        o.append(("ctx", "ctx", t + 2))
    o += attend(units, between)
    del o[o.index(("R",) + b[4]) + 1:]
    if start:
        o += job(t + 2, "xT")
    o += [("T",) + b[3], ("A",) + (a[3] if cross else b[2])]
    if start:
        o += job(t + 2, "v")
    o += [("T",) + b[4]]
    if cross:
        o += job(t + 1, "o") + [("stat", "ln2", t + 1)]
    o += [("A",) + b[3], ("A",) + b[4]]
    if cross:
        o.append(("norm", "ln2", t + 1))
    o += job(t, "o2") + [("stat", "ln3", t)]
    if cross:
        o += job(t + 1, "x2T")
    if start:
        o += job(t + 2, "k") + keys(t + 2, 0, 1)
    if cross:
        o += job(t + 1, "a")
    o.append(("norm", "ln3", t))
    if start:
        o += job(t + 2, "q")
    return o + job(t, "x3T")


def first_steps():
    o = [("stat", "ln1", 0), ("norm", "ln1", 0), ("ctx", "ctx", 0)] + job(0, "v", "k") + keys(0, 0, 1) + job(0, "xT", "q")
    o += [("stat", "ln1", 1), ("norm", "ln1", 1)]
    o += attend([(("A", k), 0) for k in range(XH // 4)],
                {1: keys(0, 2), 2: [("ctx", "ctx", 1)] + keys(0, 3) + job(0, "M0"), 3: job(0, "M1"), 4: job(0, "M2"), 5: job(0, "M3")})
    o += job(0, "M4", "M5", "M6", "M7")
    o += job(1, "xT", "v") + job(0, "o") + [("stat", "ln2", 0), ("norm", "ln2", 0)] + job(0, "M8", "x2T")
    return o + job(1, "k") + keys(1, 0, 1) + job(0, "a") + job(1, "q") + job(0, "M9")


REPEATS = 3
FIRST = first_steps()
LOOP = second_and_next(0) + second_and_next(1)
LAST = second_and_next(6, start=False) + second_and_next(7, cross=False, start=False)
ALL = FIRST + [(k, n, t + 2 * i) for i in range(REPEATS) for k, n, t in LOOP] + LAST
NTH = {kind: {(n, t): c for c, (n, t) in enumerate((n, t) for k, n, t in ALL if k == kind)} for kind in ("job", "S")}
PER_LOOP = {kind: sum(k == kind for k, _, _ in LOOP) for kind in ("job", "S")}
NJOBS, NUNITS = len(NTH["job"]), len(NTH["S"])
assert PER_LOOP["job"] % 2 == 0 and PER_LOOP["S"] % 6 == 0


def nth(kind, name, i, t):
    if type(i) is int:
        return NTH[kind][name, t + 2 * i]
    n = [NTH[kind][name, t + 2 * k] - k * PER_LOOP[kind] for k in range(REPEATS)]
    assert min(n) == max(n), (name, t, n)
    return n[0]


def build(nc, x, ctxT, consts, wqT, wkvT, woutT, waT, lnq, lnkv, wqb, wqrT, wkb, wvbT, woT,
          gateT, gate_up, down, sgT, suT, sdT, out):
    fp32, u32 = mybir.dt.float32, mybir.dt.uint32
    ALU, ACT, AX = mybir.AluOpType, mybir.ActivationFunctionType, mybir.AxisListType

    hold = ExitStack()
    with hold:
        x3n_rows = nc.dram_tensor("x3n_rows", [ROWS, D], fp32).ap()
        sums = nc.dram_tensor("sums", [ROWS, D], fp32).ap()

        def sb(name, shape, dt=fp32):
            return hold.enter_context(nc.sbuf_tensor(name, shape, dt))

        cst = sb("cst", [P, C_COLS])
        x_all = sb("x_all", [P, NT, D])
        x3nT = sb("x3nT", [P, KD, TOK])
        small = sb("small", [P, 64])
        ARENA = 43700
        arena = sb("arena", [P, ARENA])
        used = [0]

        def take(*shape):
            n = int(np.prod(shape))
            v = arena[:, used[0]:used[0] + n]
            used[0] += n
            assert used[0] <= ARENA, used
            if len(shape) == 2:
                v = v.rearrange("p (a b) -> p a b", b=shape[1])
            elif len(shape) == 3:
                v = v.rearrange("p (a b c) -> p a b c", b=shape[1], c=shape[2])
            return v

        WqT, WkvT, WoutT, WaT = take(KD, D), take(2 * D), take(KD, D), take(KD, QR + KL + DR)
        ctxT_all, ctx_cur = take(TOK), take(P)
        xn1, xnT, kT, qT, v, cT = take(D), take(KD, P), take(KD, P), take(KD, P), take(D), take(KD, P)
        kz = take(2, 4, P)
        xn2, x2T = take(D), take(KD, P)
        dead_at_last_tile = used[0]
        M0, M1 = take(MH, KL), take(MH, KL)
        WqrT0, WqrT1, WvbT = take(MH * DR), take(MH * DR), take(MH * DV)
        an, xn3 = take(QR + KL + 2 * DR), take(D)
        masked, probs, probsT = take(2, 4, P), take(3, 4, P), take(2, 4, P)
        rot1, rot2, junk = take(DR), take(DR), take(QR + KL)
        krz = take(2, P)
        mark = used[0]
        wqb0, wqb1, wkb0, wkb1 = take(MH, QR), take(MH, QR), take(MH, KL), take(MH, KL)
        end_attention = used[0]
        used[0] = mark
        WoT, v2, qr, c2T, ql = take(MH // 2, D), take(MH * DV), take(MH // 2, P), take(MH // 2, P), take(MH, P)
        qc0, qc1, klT = take(P), take(P), take(P)
        assert used[0] <= end_attention

        used[0] = 0
        WgT, WsgT, WsuT, WsdT = take(KD, E), take(KD, SI), take(KD, SI), take(SI // P, D)
        hidT, silu_s = take(SI // P, TOK), take(2, 512)
        assert used[0] <= dead_at_last_tile
        wgu, wd0, wd1 = take(R, KD, 2 * FI), take(R, D), take(R, D)
        choice_at = used[0]
        gx, gxT, eo = take(R, D), take(2, D), take(R, D)
        choice = arena[:, choice_at:choice_at + NT * TOPK * E].rearrange("p (a b) -> p a b", b=E)
        silu_e, hid_e = take(2, 3 * P), take(2, 2 * P)
        idx_w = take(2, E)
        spare = take(E)
        gather_rows, add_rows = take(R).bitcast(u32), take(R).bitcast(u32)
        row_of = take(E).bitcast(u32)
        lgT, lg, ex = take(TOK), take(NT, E), take(NT, E)
        top_w, top_i, top_f = take(NT, 8), take(NT, 8).bitcast(u32), take(NT, 8)
        chosen_by, before, rank_of = take(NT, E), take(NT, E), take(NT * TOPK)
        mark = used[0]
        hot = take(NT * TOPK, P)
        used[0] = mark
        scratch = take(NT * TOPK, E)
        used[0] = mark + NT * TOPK * P
        pair = take(NT * TOPK, 2, E)

        LN = ("ln1", "ln2", "ln3")
        stat = small[:, 0:6]
        mv = {n: small[:, 6 + 2 * k:8 + 2 * k] for k, n in enumerate(LN)}
        std = {n: small[:, 12 + k:13 + k] for k, n in enumerate(LN)}
        rstd = {n: small[:, 15 + k:16 + k] for k, n in enumerate(LN)}
        ss, rms, rrms = (small[:, 18 + 2 * k:20 + 2 * k] for k in range(3))
        lnq0, lnq1, lnk = small[:, 26:27], small[:, 27:28], small[:, 28:29]
        mx, nmx, den, rden = (sb(n, [P, 3, 4]) for n in ("mx", "nmx", "den", "rden"))
        mx8, sum8, rsum8 = small[:, 32:40], small[:, 40:48], small[:, 48:56]

        ident, mask = cst[:, C_ID:C_ID + P], cst[:, C_MASK:C_MASK + P]
        eps5, eps6 = cst[:, C_EPS5:C_EPS5 + 1], cst[:, C_EPS6:C_EPS6 + 1]

        def bank_pair(name):
            return [hold.enter_context(nc.psum_tensor(f"{name}{k}", [P, 512], fp32)) for k in range(2)]

        job_bank, s_bank, t_bank, a_bank = (bank_pair(n) for n in ("job_bank", "s_bank", "t_bank", "a_bank"))

        PER = {}

        def sem(name, per=0):
            s = hold.enter_context(nc.semaphore(name))
            PER[name] = per
            return s, name

        def at(s, i, k):
            return i * PER[s[1]] + k

        def tiles(i, t):
            return i * 2 + (t + 1)

        def units(name, i, t, behind=0):
            n = nth("S", name, i, t) + 1 - behind
            return n if type(i) is int else i * PER_LOOP["S"] + n

        def wait_unit(eng, s, name, i, t, behind=0):
            if nth("S", name, i, t) + 1 > behind:
                eng.wait_ge(s[0], units(name, i, t, behind))

        loaded = {n: sem(f"loaded_{n}") for n in (
            "consts", "ctx", "x0", "x1", "wkv", "wq", "qkb0", "qkb1", "wout", "wa", "qr0", "qr1",
            "wvb", "wo", "lnq0", "lnq1", "lnkv", "gate", "sg", "su", "sd")}
        filled = [sem(f"filled{k}") for k in range(2)]
        copied = [sem(f"copied{k}") for k in range(2)]
        ctx_ready = sem("ctx_ready")
        ln_var, ln_std, ln_done = ({n: sem(f"{what}_{n}") for n in LN} for what in ("ln_var", "ln_std", "ln_done"))
        rms_sum, rms_std = sem("rms_sum"), sem("rms_std")
        zeros_ready = sem("zeros_ready")
        kz_ready = sem("kz_ready")
        scores_ready, masked_ready = sem("scores_ready"), sem("masked_ready")
        exp_done, rden_ready, norm_done = sem("exp_done"), sem("rden_ready"), sem("norm_done")
        pT_ready, pT_copied = sem("pT_ready"), sem("pT_copied")
        av_ready, av_copied = sem("av_ready"), sem("av_copied")
        dve_chain = sem("dve_chain")
        rows_stored = sem("rows_stored")
        rows_gone = sem("rows_gone")
        zero_ready, spare_stored = sem("zero_ready"), sem("spare_stored")

        def bank_of(i, name, t):
            return job_bank[nth("job", name, i, t) % 2]

        def jobs(i, n):
            return n // 2 + 1 if type(i) is int else i * (PER_LOOP["job"] // 2) + (n // 2 + 1)

        def wait_filled(eng, i, name, t):
            n = nth("job", name, i, t)
            eng.wait_ge(filled[n % 2][0], jobs(i, n))

        def wait_copied(eng, i, *names, free_for=None):
            latest = {}
            if free_for is not None:
                n = nth("job", free_for[0], i, free_for[1]) - 2
                latest[n % 2] = n
            for name, t in names:
                n = nth("job", name, i, t)
                latest[n % 2] = max(n, latest.get(n % 2, n))
            for slot, n in sorted(latest.items()):
                if n >= 0:
                    eng.wait_ge(copied[slot][0], jobs(i, n))

        JOBS_IN = [(NJOBS + 1) // 2, NJOBS // 2]

        def residual(i, t):
            return x_all[:, t] if type(i) is int else x_all[:, bass.ds(i * 2 + t, 1), :].rearrange("p o d -> p (o d)")

        def tokens(i, t):
            return slice(t * P, (t + 1) * P) if type(i) is int else bass.ds(i * (2 * P) + t * P, P)

        def all_steps(eng, do):
            for kind, name, t in FIRST:
                do(0, kind, name, t)
            with eng.Fori(0, REPEATS) as i:
                for kind, name, t in LOOP:
                    do(i, kind, name, t)
            for kind, name, t in LAST:
                do(0, kind, name, t)

        gate_filled, gate_copied = sem("gate_filled"), sem("gate_copied")
        logits_ready = sem("logits_ready")
        lg_shifted, lg_exp = sem("lg_shifted"), sem("lg_exp")
        up_filled, up_silu, up_done = sem("up_filled"), sem("up_silu"), sem("up_done")
        down_filled, down_added = sem("down_filled"), sem("down_added")
        before_ready, pos_filled = sem("before_ready"), sem("pos_filled")
        choice_ready, pair_ready, hot_ready = sem("choice_ready"), sem("pair_ready"), sem("hot_ready")
        table_filled, table_copied, table_turned = sem("table_filled"), sem("table_copied"), sem("table_turned")
        rows_known = sem("rows_known")
        route_chain = sem("route_chain")
        pool_chain = sem("pool_chain")
        sums_stored = sem("sums_stored")
        w_loaded = [sem(f"w_loaded{r}", 64) for r in range(R)]
        gx_loaded = [sem(f"gx_loaded{r}", 16) for r in range(R)]
        gx_turned, gxT_copied = sem("gx_turned", R), sem("gxT_copied", R)
        gu_filled, silu_done, hid_ready = sem("gu_filled", R), sem("silu_done", R), sem("hid_ready", R)
        rows_copied = sem("rows_copied")
        eo_filled, eo_ready = sem("eo_filled", R), sem("eo_ready", R)
        added = sem("added", 16 * R)
        out_stored = sem("out_stored")

        block = hold.enter_context(nc.Block())

        @block.sync
        def _(sp):
            sp.sem_inc(rows_gone[0], 1)
            xt = x.rearrange("(t p) d -> p t d", p=P)
            sp.dma_start(cst[:], consts).then_inc(loaded["consts"][0], 16)
            sp.dma_start(x_all[:, 0:2], xt[:, 0:2]).then_inc(loaded["x0"][0], 16)
            sp.dma_start(ctxT_all, ctxT).then_inc(loaded["ctx"][0], 16)
            sp.dma_start(WkvT, wkvT).then_inc(loaded["wkv"][0], 16)
            sp.dma_start(WqT, wqT.rearrange("(k p) n -> p k n", p=P)).then_inc(loaded["wq"][0], 16)
            for c in range(2):
                h = slice(c * MH // 2, (c + 1) * MH // 2)
                for dst, src in ((wqb0[:, h], wqb[0:P, h]), (wkb0[:, h], wkb[0:P, h]),
                                 (wqb1[0:DN - P, h], wqb[P:DN, h]), (wkb1[0:DN - P, h], wkb[P:DN, h])):
                    sp.dma_start(dst, src).then_inc(loaded[f"qkb{c}"][0], 16)
            for name, dst, src in (
                    ("wout", WoutT, woutT.rearrange("(k p) n -> p k n", p=P)),
                    ("wa", WaT, waT.rearrange("(k p) n -> p k n", p=P)),
                    ("lnq0", lnq0, lnq[0:P]), ("lnq1", lnq1[0:QR - P], lnq[P:QR]), ("lnkv", lnk, lnkv),
                    ("wvb", WvbT, wvbT), ("qr0", WqrT0, wqrT[0:P]), ("qr1", WqrT1[0:QR - P], wqrT[P:QR]),
                    ("x1", x_all[:, 2:NT], xt[:, 2:NT])):
                sp.dma_start(dst, src).then_inc(loaded[name][0], 16)
            wait_filled(sp, 0, "M9", 0)
            sp.dma_start(WoT, woT.rearrange("(k p) n -> p k n", p=P)).then_inc(loaded["wo"][0], 16)

            def step(i, kind, name, t):
                if (kind, name) == ("norm", "ln3"):
                    sp.wait_ge(ln_done["ln3"][0], tiles(i, t))
                    rows = x3n_rows[tokens(i, t), :]
                    sp.dma_start(rows, xn3).then_inc(rows_stored[0], 16)
                    sp.wait_ge(rows_stored[0], 16 * (t + 1) if type(i) is int else i * 32 + 16 * (t + 1))
                    sp.sem_inc(rows_gone[0], 1)
                if (kind, name, t) == ("job", "x3T", NT - 2) and type(i) is int:
                    wait_copied(sp, 0, ("a", NT - 1), ("x3T", NT - 2))
                    sp.dma_start(WgT, gateT.rearrange("(k p) n -> p k n", p=P)).then_inc(loaded["gate"][0], 16)
                    sp.dma_start(WsgT, sgT.rearrange("(k p) n -> p k n", p=P)).then_inc(loaded["sg"][0], 16)
                    sp.dma_start(WsuT, suT.rearrange("(k p) n -> p k n", p=P)).then_inc(loaded["su"][0], 16)
                    sp.dma_start(WsdT, sdT.rearrange("(k p) n -> p k n", p=P)).then_inc(loaded["sd"][0], 16)

            all_steps(sp, step)
            for k in range(2):
                sp.wait_ge(copied[k][0], JOBS_IN[k])

            def load_expert(i, r):
                e = i * R + r
                sp.dma_start(wgu[:, r], gate_up[bass.ds(e, 1)].rearrange("o (k p) n -> p (o k) n", p=P)).then_inc(w_loaded[r][0], 16)
                rows = down[bass.ds(e, 1)].rearrange("o (f m) n -> m (o f) n", m=3)
                for m in range(3):
                    dst = wd1[0:H3, r] if m == 2 else wd0[m * H3:(m + 1) * H3, r]
                    sp.dma_start(dst, rows[m]).then_inc(w_loaded[r][0], 16)

            for r in range(R):
                load_expert(0, r)
            for h in range(2):
                sp.wait_ge(down_added[0], (h + 1) * NT // 2)
                sp.dma_start(sums[h * TOK // 2:(h + 1) * TOK // 2].rearrange("(t p) d -> p t d", p=P),
                             x_all[:, h * NT // 2:(h + 1) * NT // 2]).then_inc(sums_stored[0], 16)
            with sp.Fori(1, E // R) as i:
                for r in range(R):
                    sp.wait_ge(eo_filled[0], i * R + (r + 1 - R))
                    load_expert(i, r)
            sp.wait_ge(added[0], 16 * E)
            sp.dma_start(out, sums[0:TOK]).then_inc(out_stored[0], 16)
            sp.wait_ge(out_stored[0], 16)

        @block.gpsimd
        def _(pool):
            def stand():
                nc.gpsimd.tensor_tensor(small[:, 61:62], eps5, eps5, ALU.add)

            pool.memset(x3nT[:, 0, 0:D], 0.0).then_inc(zero_ready[0], 1)
            nc.gpsimd.memset(krz, 0.0).then_inc(zeros_ready[0], 1)
            pool.wait_ge(zero_ready[0], 1)
            pool.dma_start(x3n_rows[TOK:ROWS], x3nT[:, 0, 0:D]).then_inc(spare_stored[0], 16)
            pool.dma_start(sums[TOK:ROWS], x3nT[:, 0, 0:D]).then_inc(spare_stored[0], 16)
            pool.wait_ge(loaded["consts"][0], 16)
            pool.wait_ge(loaded["ctx"][0], 16)

            def step(i, kind, name, t):
                if kind == "ctx":
                    if t + (type(i) is not int) > 0:
                        wait_filled(pool, i, "k", t - 1)
                        if type(i) is not int:
                            stand()
                    nc.gpsimd.tensor_copy(ctx_cur, ctxT_all[:, tokens(i, t)]).then_inc(ctx_ready[0], 1)
                elif kind == "K":
                    hg = name[1]
                    if hg == 0:
                        wait_copied(pool, i, ("k", t))
                    if hg >= 2:
                        wait_unit(pool, scores_ready, ("A", hg - 2), i, t)
                    elif type(i) is not int or t > 0:
                        wait_unit(pool, scores_ready, ("A", hg + 2), i, t - 1)
                    nc.gpsimd.tensor_tensor(
                        kz[:, hg % 2], kT[:, hg].unsqueeze(1).to_broadcast([P, 4, P]),
                        cst[:, C_HEAD:C_HEAD + 4].unsqueeze(2).to_broadcast([P, 4, P]), ALU.mult).then_inc(kz_ready[0], 1)
                elif kind == "R":
                    n = nth("S", name, i, t)
                    wait_unit(pool, rden_ready, name, i, t)
                    nc.gpsimd.tensor_tensor(
                        probs[:, n % 3], probs[:, n % 3], rden[:, n % 3, :].unsqueeze(2).to_broadcast([P, 4, P]),
                        ALU.mult).then_inc(norm_done[0], 1)

            all_steps(pool, step)
            pool.wait_ge(choice_ready[0], 1)
            for t in range(NT):
                nc.gpsimd.tensor_scalar(
                    pair[:, t * TOPK:(t + 1) * TOPK, 0], choice[:, t * TOPK:(t + 1) * TOPK],
                    cst[:, C_TOK + t:C_TOK + t + 1], None, ALU.mult)
                last = nc.gpsimd.tensor_tensor(
                    pair[:, t * TOPK:(t + 1) * TOPK, 1], choice[:, t * TOPK:(t + 1) * TOPK],
                    top_w[:, t, 0:TOPK].unsqueeze(2).to_broadcast([P, TOPK, E]), ALU.mult)
            last.then_inc(pair_ready[0], 1)

            def rows_in_place(dst, e, n):
                nc.gpsimd.tensor_copy(dst, row_of[:, bass.ds(e, 1)]).then_inc(rows_copied[0], 1)
                pool.wait_ge(rows_copied[0], n + 1)
                stand()

            def gather(i, r, n):
                pool.wait_ge(gx_turned[0], i * R + (r + 1 - R))
                rows_in_place(gather_rows[:, r:r + 1], i * R + r, n)
                nc.gpsimd.indirect_dma_start(
                    gx[:, r], None, x3n_rows, bass.IndirectOffsetOnAxis(gather_rows[:, r:r + 1], 0)
                ).then_inc(gx_loaded[r][0], 16)

            def add(i, r, n):
                pool.wait_ge(eo_ready[0], at(eo_ready, i, r + 1))
                rows_in_place(add_rows[:, r:r + 1], i * R + r, n)
                nc.gpsimd.indirect_dma_start(
                    sums, bass.IndirectOffsetOnAxis(add_rows[:, r:r + 1], 0), eo[:, r], None,
                    compute_op=ALU.add).then_inc(added[0], 16)

            pool.wait_ge(rows_known[0], 1)
            pool.wait_ge(spare_stored[0], 32)
            pool.wait_ge(rows_stored[0], 16 * NT)
            for r in range(R):
                nc.gpsimd.indirect_dma_start(
                    gx[:, r], None, x3n_rows, bass.IndirectOffsetOnAxis(row_of[:, r:r + 1], 0)
                ).then_inc(gx_loaded[r][0], 16)
            pool.wait_ge(sums_stored[0], 32)
            with pool.Fori(0, E // R - 1) as i:
                for r in range(R):
                    add(i, r, i * 2 * R + 2 * r)
                    gather(i + 1, r, i * 2 * R + 2 * r + 1)
                    pool.wait_ge(added[0], at(added, i, 16 * (r + 1)))
            for r in range(R):
                add(E // R - 1, r, (E // R - 1) * 2 * R + r)
                pool.wait_ge(added[0], at(added, E // R - 1, 16 * (r + 1)))

        @block.scalar
        def _(act):
            act.wait_ge(loaded["consts"][0], 16)
            act.wait_ge(spare_stored[0], 32)

            def step(i, kind, name, t):
                def to(dst, src=None):
                    wait_filled(act, i, name, t)
                    n = nth("job", name, i, t)
                    return nc.scalar.copy(dst, job_bank[n % 2][:, :] if src is None else src).then_inc(copied[n % 2][0], 1)

                def flat(v):
                    return v.rearrange("p a b -> p (a b)")

                if kind == "stat":
                    act.wait_ge(ln_var[name][0], tiles(i, t))
                    nc.scalar.activation(std[name], mv[name][:, 1:2], ACT.Sqrt, bias=eps5).then_inc(ln_std[name][0], 1)
                elif kind == "S":
                    n, scale = nth("S", name, i, t), (float(DN + DR) if name[0] == "B" else float(XD)) ** -0.5
                    wait_unit(act, masked_ready, name, i, t)
                    wait_unit(act, pT_ready, name, i, t, behind=3)
                    for j in range(4):
                        last = nc.scalar.activation(
                            probs[:, n % 3, j], masked[:, n % 2, j], ACT.Exp, bias=nmx[:, n % 3, j:j + 1],
                            scale=scale, accum_out=den[:, n % 3, j:j + 1])
                    last.then_inc(exp_done[0], 1)
                elif kind == "A":
                    n, hg = nth("S", name, i, t), name[1]
                    wait_unit(act, av_ready, name, i, t)
                    if name[0] == "B":
                        last = nc.scalar.copy(c2T[:, 2 * hg:2 * hg + 2], a_bank[n % 2][:, 0:2 * P].rearrange("p (a b) -> p a b", b=P))
                    else:
                        last = nc.scalar.copy(cT[:, hg], a_bank[n % 2][:, 0:P])
                    last.then_inc(av_copied[0], 1)
                elif kind == "job":
                    if name[0] == "M":
                        n, m = nth("job", name, i, t), int(name[1])
                        bank = job_bank[n % 2][:, :].rearrange("p (a b c) -> p a b c", a=2, c=P)
                        wait_filled(act, i, name, t)
                        nc.scalar.copy(M0[:, 2 * m:2 * m + 2], bank[:, 0])
                        nc.scalar.copy(M1[0:QR - P, 2 * m:2 * m + 2], bank[0:QR - P, 1]).then_inc(copied[n % 2][0], 1)
                    elif name == "k":
                        to(flat(kT))
                    elif name == "x2T":
                        to(flat(x2T))
                    elif name == "a":
                        bank = bank_of(i, name, t)
                        wait_filled(act, i, name, t)
                        nc.scalar.activation(junk[:, 0:QR], bank[:, 0:QR], ACT.Square, accum_out=ss[:, 0:1])
                        nc.scalar.activation(junk[:, QR:QR + KL], bank[:, QR:QR + KL], ACT.Square, accum_out=ss[:, 1:2]).then_inc(rms_sum[0], 1)
                        act.wait_ge(rms_sum[0], tiles(i, t))
                        nc.scalar.activation(rms[:, 0:1], ss[:, 0:1], ACT.Sqrt, bias=eps6, scale=1.0 / QR)
                        nc.scalar.activation(rms[:, 1:2], ss[:, 1:2], ACT.Sqrt, bias=eps6, scale=1.0 / KL).then_inc(rms_std[0], 1)
                    elif name in ("v2_0", "v2_1"):
                        m = int(name[3])
                        to(v2[:, m * 512:(m + 1) * 512])
                    elif name == "v2_2":
                        to(v2[:, 1024:MH * DV], bank_of(i, name, t)[:, 0:MH * DV - 1024])
                    elif name[0] == "r":
                        m = int(name[1])
                        w = min(4, MH // 2 - 4 * m)
                        to(flat(qr[:, 4 * m:4 * m + w]), bank_of(i, name, t)[:, 0:w * P])
                    elif name[0] == "l" and int(name[1]) % 2 == 0:
                        m = int(name[1])
                        to(flat(ql[:, 4 * m:4 * m + 4]))
                    elif name == "x3T":
                        to(x3nT[:, :, tokens(i, t)], bank_of(i, name, t)[:, :].rearrange("p (k t) -> p k t", t=P))

            all_steps(act, step)
            for n in range(2):
                act.wait_ge(gate_filled[0], n + 1)
                nc.scalar.copy(lgT[0:E, n * 512:(n + 1) * 512], job_bank[n][0:E, :]).then_inc(gate_copied[0], 1)
            for n in range(2 * (SI // P)):
                act.wait_ge(up_filled[0], n + 1)
                if n >= 2:
                    act.wait_ge(up_done[0], n - 1)
                nc.scalar.activation(silu_s[:, n % 2], [s_bank, t_bank][n % 2][0][:, :], ACT.Silu).then_inc(up_silu[0], 1)
                if n == 0:
                    act.wait_ge(lg_shifted[0], 1)
                    nc.scalar.activation(ex, lg, ACT.Exp).then_inc(lg_exp[0], 1)
            act.wait_ge(table_filled[0], 1)
            nc.scalar.copy(silu_e[:, 0, 0:P], a_bank[1][:, 0:P]).then_inc(table_copied[0], 1)

            def expert(i, r):
                act.wait_ge(gx_turned[0], at(gx_turned, i, r + 1))
                act.wait_ge(gu_filled[0], i * R + max(r - 1, 0) if type(i) is int and i == 0 else i * R + (r - 1))
                nc.scalar.copy(gxT[:, r % 2], t_bank[r % 2][:, :]).then_inc(gxT_copied[0], 1)
                act.wait_ge(gu_filled[0], at(gu_filled, i, r + 1))
                act.wait_ge(hid_ready[0], i * R + max(r - 1, 0) if type(i) is int and i == 0 else i * R + (r - 1))
                nc.scalar.activation(silu_e[0:H3, r % 2], s_bank[r % 2][0:H3, 0:3 * P], ACT.Silu).then_inc(silu_done[0], 1)

            act.wait_ge(table_turned[0], 1)
            for r in range(R):
                expert(0, r)
            with act.Fori(1, E // R) as i:
                for r in range(R):
                    expert(i, r)

        @block.vector
        def _(dve):
            for n in ("consts", "x0"):
                dve.wait_ge(loaded[n][0], 16)
            def links_of(kind, name):
                return 2 if (kind, name) == ("job", "a") else int(kind in ("stat", "norm", "S"))

            links = [0]
            LINKS_PER_LOOP = sum(links_of(k, n) for k, n, _ in LOOP)
            FIRST_LINKS = sum(links_of(k, n) for k, n, _ in FIRST)
            scale_of = {"A": float(XD) ** -0.5, "B": float(DN + DR) ** -0.5}

            def step(i, kind, name, t):
                in_loop = type(i) is not int

                def chained(ins):
                    links[0] += 1
                    ins.then_inc(dve_chain[0], 1)
                    dve.wait_ge(dve_chain[0], i * LINKS_PER_LOOP + links[0] if in_loop else links[0])

                def stand():
                    if in_loop:
                        k = 59 if kind == "S" else 60
                        nc.vector.memset(small[:, k:k + 1], 0.0)

                def to(dst, src=None):
                    wait_filled(dve, i, name, t)
                    n = nth("job", name, i, t)
                    nc.vector.tensor_copy(dst, job_bank[n % 2][:, :] if src is None else src).then_inc(copied[n % 2][0], 1)

                def flat(v):
                    return v.rearrange("p a b -> p (a b)")

                if kind == "stat":
                    if name != "ln1":
                        wait_copied(dve, i, ("o" if name == "ln2" else "o2", t))
                    stand()
                    chained(nc.vector.bn_stats(stat, residual(i, t)))
                    stand()
                    nc.vector.bn_aggr(mv[name], stat).then_inc(ln_var[name][0], 1)
                elif kind == "norm":
                    dve.wait_ge(ln_std[name][0], tiles(i, t))
                    chained(nc.vector.reciprocal(rstd[name], std[name]))
                    if name == "ln3":
                        dve.wait_ge(rows_gone[0], tiles(i, t))
                    dst = {"ln1": xn1, "ln2": xn2, "ln3": xn3}[name]
                    nc.vector.tensor_scalar(dst, residual(i, t), mv[name][:, 0:1], rstd[name],
                                            ALU.subtract, ALU.mult).then_inc(ln_done[name][0], 1)
                elif kind == "S":
                    n = nth("S", name, i, t)
                    wait_unit(dve, scores_ready, name, i, t)
                    stand()
                    for j in range(4):
                        last = nc.vector.tensor_tensor_reduce(
                            out=masked[:, n % 2, j], in0=s_bank[n % 2][:, j * P:(j + 1) * P], in1=mask,
                            scale=1.0, scalar=FLOOR, op0=ALU.add, op1=ALU.max, accum_out=mx[:, n % 3, j:j + 1])
                    chained(last)
                    nc.vector.tensor_scalar(nmx[:, n % 3], mx[:, n % 3], -scale_of[name[0]], None, ALU.mult).then_inc(masked_ready[0], 1)
                elif kind == "R":
                    n = nth("S", name, i, t)
                    wait_unit(dve, exp_done, name, i, t)
                    nc.vector.reciprocal(rden[:, n % 3], den[:, n % 3]).then_inc(rden_ready[0], 1)
                elif kind == "T":
                    n = nth("S", name, i, t)
                    wait_unit(dve, pT_ready, name, i, t)
                    wait_unit(dve, av_ready, name, i, t, behind=2)
                    nc.vector.tensor_copy(flat(probsT[:, n % 2]), t_bank[n % 2][:, :]).then_inc(pT_copied[0], 1)
                elif kind == "job":
                    bank, slot = bank_of(i, name, t), nth("job", name, i, t) % 2
                    if name == "v":
                        to(v)
                    elif name == "xT":
                        to(flat(xnT))
                    elif name == "q":
                        to(flat(qT))
                    elif name[0] == "l" and int(name[1]) % 2 == 1:
                        m = int(name[1])
                        to(flat(ql[:, 4 * m:4 * m + 4]))
                    elif name in ("o", "o2"):
                        wait_filled(dve, i, name, t)
                        nc.vector.tensor_tensor(residual(i, t), residual(i, t), bank[:, :], ALU.add).then_inc(copied[slot][0], 1)
                    elif name == "a":
                        kr = bank[:, QR + KL:QR + KL + DR]
                        cos, sin, h = cst[:, C_COS:C_COS + DR], cst[:, C_SIN:C_SIN + DR], DR // 2
                        dve.wait_ge(rms_sum[0], tiles(i, t))
                        nc.vector.tensor_tensor(rot1, kr, cos, ALU.mult)
                        nc.vector.tensor_tensor(rot2[:, 0:h], kr[:, h:DR], sin[:, 0:h], ALU.mult)
                        chained(nc.vector.tensor_tensor(rot2[:, h:DR], kr[:, 0:h], sin[:, h:DR], ALU.mult))
                        for c in range(2):
                            nc.vector.tensor_tensor(an[:, QR + KL + c * DR:QR + KL + (c + 1) * DR], rot1, rot2, ALU.add)
                        dve.wait_ge(rms_std[0], tiles(i, t))
                        chained(nc.vector.reciprocal(rrms, rms))
                        nc.vector.tensor_scalar(an[:, 0:QR], bank[:, 0:QR], rrms[:, 0:1], None, ALU.mult)
                        nc.vector.tensor_scalar(an[:, QR:QR + KL], bank[:, QR:QR + KL], rrms[:, 1:2], None, ALU.mult).then_inc(copied[slot][0], 1)
                    elif name == "aT":
                        wait_filled(dve, i, name, t)
                        nc.vector.tensor_scalar(qc0, bank[:, 0:P], lnq0, None, ALU.mult)
                        nc.vector.tensor_scalar(qc1[0:QR - P], bank[0:QR - P, P:2 * P], lnq1[0:QR - P], None, ALU.mult)
                        nc.vector.tensor_scalar(klT, bank[:, 2 * P:3 * P], lnk, None, ALU.mult)
                        nc.vector.tensor_copy(krz[0:DR, 0], bank[0:DR, 3 * P:4 * P])
                        nc.vector.tensor_copy(krz[DR:2 * DR, 1], bank[DR:2 * DR, 3 * P:4 * P]).then_inc(copied[slot][0], 1)

            for kind, name, t in FIRST:
                step(0, kind, name, t)
            assert links[0] == FIRST_LINKS
            for n in ("lnq0", "lnq1", "lnkv", "x1"):
                dve.wait_ge(loaded[n][0], 16)
            dve.wait_ge(zeros_ready[0], 1)
            with dve.Fori(0, REPEATS) as i:
                for kind, name, t in LOOP:
                    step(i, kind, name, t)
            links[0] = FIRST_LINKS + REPEATS * LINKS_PER_LOOP
            for kind, name, t in LAST:
                step(0, kind, name, t)

            count = [0]

            def link(ins):
                count[0] += 1
                ins.then_inc(route_chain[0], 1)
                dve.wait_ge(route_chain[0], count[0])

            def bc8(v8):
                return v8.unsqueeze(2).to_broadcast([P, NT, E])

            def shared_product(n):
                m, half = n % (SI // P), n // (SI // P)
                dve.wait_ge(up_silu[0], n + 1)
                nc.vector.tensor_tensor(hidT[:, m, half * 512:(half + 1) * 512], silu_s[:, n % 2],
                                        [s_bank, t_bank][n % 2][1][:, :], ALU.mult).then_inc(up_done[0], 1)

            dve.wait_ge(logits_ready[0], 1)
            logits = a_bank[0][:, :].rearrange("p (t e) -> p t e", e=E)
            link(nc.vector.tensor_reduce(mx8, logits, AX.X, ALU.max))
            nc.vector.tensor_tensor(lg, logits, bc8(mx8), ALU.subtract).then_inc(lg_shifted[0], 1)
            shared_product(0)
            dve.wait_ge(lg_exp[0], 1)
            link(nc.vector.tensor_reduce(sum8, ex, AX.X, ALU.add))
            link(nc.vector.reciprocal(rsum8, sum8))
            link(nc.vector.tensor_tensor(lg, ex, bc8(rsum8), ALU.mult))
            for t in range(NT):
                last = nc.vector.max(top_w[:, t], lg[:, t])
            link(last)
            shared_product(1)
            for t in range(NT):
                last = nc.vector.max_index(top_i[:, t], top_w[:, t], lg[:, t])
            link(last)
            link(nc.vector.tensor_copy(top_f, top_i))
            for t in range(NT):
                last = nc.vector.tensor_tensor(
                    choice[:, t * TOPK:(t + 1) * TOPK], cst[:, C_IOTA:C_IOTA + E].unsqueeze(1).to_broadcast([P, TOPK, E]),
                    top_f[:, t, 0:TOPK].unsqueeze(2).to_broadcast([P, TOPK, E]), ALU.is_equal)
                if t == NT // 2:
                    shared_product(2)
            last.then_inc(choice_ready[0], 1)
            dve.wait_ge(choice_ready[0], 1)
            link(nc.vector.tensor_reduce(chosen_by, choice.rearrange("p (t k) e -> p t e k", k=TOPK), AX.X, ALU.add))
            shared_product(3)
            link(nc.vector.memset(before[:, 0], 0.0))
            for t in range(1, NT):
                last = nc.vector.tensor_tensor(before[:, t], before[:, t - 1], chosen_by[:, t - 1], ALU.add)
                if t < NT - 1:
                    link(last)
            last.then_inc(before_ready[0], 1)
            shared_product(4)
            shared_product(5)
            dve.wait_ge(pos_filled[0], 1)
            for t in range(NT):
                last = nc.vector.tensor_tensor(
                    scratch[:, t * TOPK:(t + 1) * TOPK], choice[:, t * TOPK:(t + 1) * TOPK],
                    a_bank[0][:, t * E:(t + 1) * E].unsqueeze(1).to_broadcast([P, TOPK, E]), ALU.mult)
            link(last)
            link(nc.vector.tensor_reduce(rank_of, scratch, AX.X, ALU.add))
            for n in range(NT * TOPK):
                last = nc.vector.tensor_scalar(hot[:, n], cst[:, C_IOTA:C_IOTA + P], rank_of[:, n:n + 1], None, ALU.is_equal)
                if n % TOPK == TOPK - 1:
                    last.then_inc(hot_ready[0], 1)
            for t in range(NT):
                dve.wait_ge(down_filled[0], t + 1)
                nc.vector.tensor_tensor(x_all[:, t], x_all[:, t], [s_bank, t_bank][t % 2][t // 2 % 2][:, :], ALU.add).then_inc(down_added[0], 1)
            dve.wait_ge(table_turned[0], 1)
            link(nc.vector.tensor_copy(idx_w.rearrange("p a b -> p (a b)"), a_bank[1][:, P:2 * P]))
            link(nc.vector.tensor_scalar(spare, idx_w[:, 0], 0.0, cst[:, C_SPARE:C_SPARE + 1], ALU.is_equal, ALU.mult))
            nc.vector.scalar_tensor_tensor(row_of, idx_w[:, 0], -1.0, spare, ALU.add, ALU.add).then_inc(rows_known[0], 1)

            def expert(i, r):
                dve.wait_ge(silu_done[0], at(silu_done, i, r + 1))
                dve.wait_ge(eo_filled[0], i * R + max(r - 1, 0) if type(i) is int and i == 0 else i * R + (r - 1))
                g = silu_e[0:H3, r % 2].rearrange("p (m t) -> p m t", t=P)
                u = s_bank[r % 2][H3:2 * H3, 0:3 * P].rearrange("p (m t) -> p m t", t=P)
                nc.vector.tensor_tensor(hid_e[0:H3, r % 2].rearrange("p (m t) -> p m t", t=P), g[:, 0:3:2], u[:, 0:3:2], ALU.mult)
                nc.vector.tensor_tensor(hid_e[H3:2 * H3, r % 2, 0:P], g[:, 1], u[:, 1], ALU.mult).then_inc(hid_ready[0], 1)

            def output(i, r):
                dve.wait_ge(eo_filled[0], at(eo_filled, i, r + 1))
                if not (type(i) is int and i == 0):
                    dve.wait_ge(added[0], 16 * (i * R + (r + 1 - R)))
                e = i * R + r
                w = idx_w[:, 1, bass.ds(e, 1)] if type(i) is not int else idx_w[:, 1, e:e + 1]
                nc.vector.tensor_scalar(eo[:, r], job_bank[r % 2][:, :], w, None, ALU.mult).then_inc(eo_ready[0], 1)

            for r in range(R):
                expert(0, r)
                if r:
                    output(0, r - 1)
            with dve.Fori(1, E // R) as i:
                for r in range(R):
                    expert(i, r)
                    output(i - 1, R - 1) if r == 0 else output(i, r - 1)
            output(E // R - 1, R - 1)

        @block.tensor
        def _(pe):
            mm = nc.tensor.matmul
            met = set()

            def loads(*names):
                for n in names:
                    if n not in met:
                        met.add(n)
                        pe.wait_ge(loaded[n][0], 16 * (4 if n[:3] == "qkb" else 1))

            def job(i, name, t):
                n = nth("job", name, i, t)
                bank, slot = job_bank[n % 2], n % 2

                def ready(*names):
                    wait_copied(pe, i, *((m, t) for m in names), free_for=(name, t))

                if name[0] == "M":
                    m = int(name[1])
                    loads("qkb0", *(("qkb1",) if 2 * m + 1 >= MH // 2 else ()))
                    ready()
                    for a, (r0, rn) in enumerate(((0, P), (P, QR - P))):
                        for b in range(2):
                            h = 2 * m + b
                            o = bank[0:rn, (2 * a + b) * P:(2 * a + b + 1) * P]
                            mm(o, wqb0[:, h, r0:r0 + rn], wkb0[:, h], start=True, stop=False)
                            last = mm(o, wqb1[0:DN - P, h, r0:r0 + rn], wkb1[0:DN - P, h], start=False, stop=True)
                elif name == "k":
                    ready()
                    for m in range(KD):
                        last = mm(bank[:, m * P:(m + 1) * P], WkvT[:, m * P:(m + 1) * P], ctx_cur, start=True, stop=True)
                elif name == "v":
                    loads("wkv")
                    ready()
                    pe.wait_ge(ctx_ready[0], tiles(i, t))
                    last = mm(bank[:, :], ctx_cur, WkvT[:, D:2 * D], start=True, stop=True)
                elif name in ("xT", "x2T", "x3T"):
                    ln, src = {"xT": ("ln1", xn1), "x2T": ("ln2", xn2), "x3T": ("ln3", xn3)}[name]
                    ready()
                    pe.wait_ge(ln_done[ln][0], tiles(i, t))
                    for k in range(KD):
                        last = nc.tensor.transpose(bank[:, k * P:(k + 1) * P], src[:, k * P:(k + 1) * P], ident)
                elif name == "q":
                    loads("wq")
                    ready("xT")
                    for m in range(KD):
                        for k in range(KD):
                            last = mm(bank[:, m * P:(m + 1) * P], WqT[:, k, m * P:(m + 1) * P], xnT[:, k], start=k == 0, stop=k == KD - 1)
                elif name == "o":
                    loads("wout")
                    ready()
                    wait_unit(pe, av_copied, ("A", XH // 4 - 1), i, t)
                    for k in range(KD):
                        last = mm(bank[:, :], cT[:, k], WoutT[:, k], start=k == 0, stop=k == KD - 1)
                elif name == "a":
                    loads("wa")
                    ready("x2T")
                    for k in range(KD):
                        last = mm(bank[:, 0:QR + KL + DR], x2T[:, k], WaT[:, k], start=k == 0, stop=k == KD - 1)
                elif name == "aT":
                    ready("a")
                    for c, (f, w) in enumerate(((0, P), (P, QR - P), (QR, KL), (QR + KL, 2 * DR))):
                        last = nc.tensor.transpose(bank[0:w, c * P:(c + 1) * P], an[:, f:f + w], ident)
                elif name[0:2] == "v2":
                    f = 512 * int(name[3])
                    w = min(512, MH * DV - f)
                    ready("aT")
                    last = mm(bank[:, 0:w], klT, WvbT[:, f:f + w], start=True, stop=True)
                elif name[0] == "r":
                    ready("aT")
                    for m in range(4 * int(name[1]), min(4 * int(name[1]) + 4, MH // 2)):
                        o = bank[:, m % 4 * P:(m % 4 + 1) * P]
                        mm(o, WqrT0[:, m * P:(m + 1) * P], qc0, start=True, stop=False)
                        last = mm(o, WqrT1[0:QR - P, m * P:(m + 1) * P], qc1[0:QR - P], start=False, stop=True)
                elif name[0] == "l":
                    ready("aT")
                    for j in range(4):
                        h, o = 4 * int(name[1]) + j, bank[:, j * P:(j + 1) * P]
                        mm(o, M0[:, h], qc0, start=True, stop=False)
                        last = mm(o, M1[0:QR - P, h], qc1[0:QR - P], start=False, stop=True)
                elif name == "o2":
                    pe.wait_ge(loaded["wo"][0], 16)
                    ready()
                    wait_unit(pe, av_copied, ("B", MH // 4 - 1), i, t)
                    for k in range(MH // 2):
                        last = mm(bank[:, :], c2T[:, k], WoT[:, k], start=k == 0, stop=k == MH // 2 - 1)
                last.then_inc(filled[slot][0], 1)

            def step(i, kind, name, t):
                if kind == "job":
                    job(i, name, t)
                elif kind == "S":
                    n, (which, hg) = nth("S", name, i, t), name
                    wait_unit(pe, masked_ready, name, i, t, behind=2)
                    if which == "B":
                        wait_copied(pe, i, (f"l{hg}", t), (f"r{hg // 2}", t))
                        for j in range(4):
                            o, h = s_bank[n % 2][:, j * P:(j + 1) * P], 4 * hg + j
                            mm(o, ql[:, h], klT, start=True, stop=False)
                            last = mm(o, qr[:, h // 2], krz[:, h % 2], start=False, stop=True)
                    else:
                        if hg == 0:
                            wait_copied(pe, i, ("q", t))
                        pe.wait_ge(kz_ready[0], t * 4 + hg + 1 if type(i) is int else i * 8 + (t * 4 + hg + 1))
                        last = mm(s_bank[n % 2][:, :], qT[:, hg], kz[:, hg % 2].rearrange("p a b -> p (a b)"), start=True, stop=True)
                    last.then_inc(scores_ready[0], 1)
                elif kind == "T":
                    n = nth("S", name, i, t)
                    wait_unit(pe, norm_done, name, i, t)
                    wait_unit(pe, pT_copied, name, i, t, behind=2)
                    for j in range(4):
                        last = nc.tensor.transpose(t_bank[n % 2][:, j * P:(j + 1) * P], probs[:, n % 3, j], ident)
                    last.then_inc(pT_ready[0], 1)
                elif kind == "A":
                    n, (which, hg) = nth("S", name, i, t), name
                    wait_unit(pe, pT_copied, name, i, t)
                    wait_unit(pe, av_copied, name, i, t, behind=2)
                    if name == ("A", 0):
                        wait_copied(pe, i, ("v", t))
                    elif which == "B" and hg % 2 == 0:
                        wait_copied(pe, i, (f"v2_{hg // 2}", t))
                    for j in range(4):
                        h = 4 * hg + j
                        if which == "B":
                            o = a_bank[n % 2][DV * (j % 2):DV * (j % 2) + DV, j // 2 * P:j // 2 * P + P]
                            last = mm(o, v2[:, h * DV:(h + 1) * DV], probsT[:, n % 2, j], start=True, stop=True)
                        else:
                            last = mm(a_bank[n % 2][XD * j:XD * (j + 1), 0:P], v[:, h * XD:(h + 1) * XD],
                                      probsT[:, n % 2, j], start=True, stop=True)
                    last.then_inc(av_ready[0], 1)

            pe.wait_ge(loaded["consts"][0], 16)
            for kind, name, t in FIRST:
                step(0, kind, name, t)
            for n in ("wvb", "qr0", "qr1"):
                pe.wait_ge(loaded[n][0], 16)
            with pe.Fori(0, REPEATS) as i:
                for kind, name, t in LOOP:
                    step(i, kind, name, t)
            for kind, name, t in LAST:
                step(0, kind, name, t)

            for k in range(2):
                pe.wait_ge(copied[k][0], JOBS_IN[k])
            pe.wait_ge(loaded["gate"][0], 16)
            for n in range(2):
                for k in range(KD):
                    last = mm(job_bank[n][0:E, :], WgT[:, k], x3nT[:, k, n * 512:(n + 1) * 512], start=k == 0, stop=k == KD - 1)
                last.then_inc(gate_filled[0], 1)
            pe.wait_ge(gate_copied[0], 2)
            pe.wait_ge(av_copied[0], NUNITS)
            for t in range(NT):
                last = nc.tensor.transpose(a_bank[0][:, t * E:(t + 1) * E], lgT[0:E, t * P:(t + 1) * P], cst[0:E, C_ID:C_ID + E])
            last.then_inc(logits_ready[0], 1)
            pe.wait_ge(loaded["sg"][0], 16)
            pe.wait_ge(loaded["su"][0], 16)
            for n in range(2 * (SI // P)):
                m, half = n % (SI // P), n // (SI // P)
                if n >= 2:
                    pe.wait_ge(up_done[0], n - 1)
                for b, w in enumerate((WsgT, WsuT)):
                    for k in range(KD):
                        last = mm([s_bank, t_bank][n % 2][b][:, :], w[:, k, m * P:(m + 1) * P],
                                  x3nT[:, k, half * 512:(half + 1) * 512], start=k == 0, stop=k == KD - 1)
                last.then_inc(up_filled[0], 1)
            pe.wait_ge(before_ready[0], 1)
            mm(a_bank[0][:, :], cst[:, C_BEFORE:C_BEFORE + P], chosen_by.rearrange("p t e -> p (t e)"), start=True, stop=False)
            mm(a_bank[0][:, :], cst[:, C_ONES:C_ONES + P], before.rearrange("p t e -> p (t e)"), start=False, stop=True).then_inc(pos_filled[0], 1)
            pe.wait_ge(loaded["sd"][0], 16)
            pe.wait_ge(up_done[0], 2 * (SI // P))
            for t in range(NT):
                if t >= 4:
                    pe.wait_ge(down_added[0], t - 3)
                for k in range(SI // P):
                    last = mm([s_bank, t_bank][t % 2][t // 2 % 2][:, :], hidT[:, k, t * P:(t + 1) * P], WsdT[:, k], start=k == 0, stop=k == SI // P - 1)
                last.then_inc(down_filled[0], 1)
            pe.wait_ge(pair_ready[0], 1)
            for n in range(NT * TOPK):
                if n % TOPK == 0:
                    pe.wait_ge(hot_ready[0], n // TOPK + 1)
                last = mm(a_bank[1][:, 0:P], pair[:, n].rearrange("p a e -> p (a e)"), hot[:, n], start=n == 0, stop=n == NT * TOPK - 1)
            last.then_inc(table_filled[0], 1)
            pe.wait_ge(table_copied[0], 1)
            nc.tensor.transpose(a_bank[1][:, P:2 * P], silu_e[:, 0, 0:P], ident).then_inc(table_turned[0], 1)

            def before_down(i, r):
                first = type(i) is int and i == 0
                pe.wait_ge(gx_loaded[r][0], at(gx_loaded[r], i, 16))
                if not first or r >= 2:
                    pe.wait_ge(gxT_copied[0], i * R + (r - 1))
                for k in range(KD):
                    last = nc.tensor.transpose(t_bank[r % 2][:, k * P:(k + 1) * P], gx[:, r, k * P:(k + 1) * P], ident)
                last.then_inc(gx_turned[0], 1)
                pe.wait_ge(w_loaded[r][0], at(w_loaded[r], i, 64))
                pe.wait_ge(gxT_copied[0], at(gxT_copied, i, r + 1))
                if not first or r >= 2:
                    pe.wait_ge(hid_ready[0], i * R + (r - 1))
                w = wgu[:, r].rearrange("p k (f m) -> p k m f", m=3)
                for m in range(3):
                    for k in range(KD):
                        last = mm(s_bank[r % 2][:, m * P:(m + 1) * P], w[:, k, m],
                                  gxT[:, r % 2, k * P:(k + 1) * P], start=k == 0, stop=k == KD - 1)
                last.then_inc(gu_filled[0], 1)

            def down_product(i, r):
                first = type(i) is int and i == 0
                pe.wait_ge(hid_ready[0], at(hid_ready, i, r + 1))
                if not first or r >= 2:
                    pe.wait_ge(eo_ready[0], i * R + (r - 1))
                mm(job_bank[r % 2][:, :], hid_e[:, r % 2, 0:P], wd0[:, r], start=True, stop=False)
                mm(job_bank[r % 2][:, :], hid_e[0:H3, r % 2, P:2 * P], wd1[0:H3, r], start=False, stop=True).then_inc(eo_filled[0], 1)

            pe.wait_ge(rows_known[0], 1)
            for r in range(R):
                before_down(0, r)
                if r:
                    down_product(0, r - 1)
            with pe.Fori(1, E // R) as i:
                for r in range(R):
                    before_down(i, r)
                    down_product(i - 1, R - 1) if r == 0 else down_product(i, r - 1)
            down_product(E // R - 1, R - 1)


def kernel(x, ctx_512, L0_xattn_Wq, L0_xattn_Wkv_expand, L0_xattn_Wout, L0_attn_q_a_w, L0_attn_q_a_ln_w,
           L0_attn_q_b_w, L0_attn_kv_a_w, L0_attn_kv_a_ln_w, L0_attn_kv_b_w, L0_attn_o_w, L0_ffn_gate_w,
           L0_ffn_gate_up_proj, L0_ffn_down_proj, L0_ffn_shared_gate_w, L0_ffn_shared_up_w, L0_ffn_shared_down_w):
    import concourse.bacc as bacc
    from concourse.bass_utils import run_bass_kernel_spmd

    a = np.asarray
    qb = a(L0_attn_q_b_w).reshape(MH, DN + DR, QR)
    kvb = a(L0_attn_kv_b_w).reshape(MH, DN + DV, KL)
    arrays = {
        "x": a(x).reshape(TOK, D),
        "ctxT": a(ctx_512)[:, :SQ].transpose(2, 0, 1).reshape(XL, TOK),
        "consts": constant_table(),
        "wqT": a(L0_xattn_Wq).T, "wkvT": a(L0_xattn_Wkv_expand).T, "woutT": a(L0_xattn_Wout).T,
        "waT": np.concatenate([a(L0_attn_q_a_w), a(L0_attn_kv_a_w)], 0).T,
        "lnq": a(L0_attn_q_a_ln_w).reshape(QR, 1), "lnkv": a(L0_attn_kv_a_ln_w).reshape(KL, 1),
        "wqb": qb[:, :DN].transpose(1, 0, 2), "wqrT": qb[:, DN:].transpose(2, 0, 1).reshape(QR, MH * DR),
        "wkb": kvb[:, :DN].transpose(1, 0, 2), "wvbT": kvb[:, DN:].transpose(2, 0, 1).reshape(KL, MH * DV),
        "woT": a(L0_attn_o_w).T, "gateT": a(L0_ffn_gate_w).T,
        "gate_up": a(L0_ffn_gate_up_proj), "down": a(L0_ffn_down_proj),
        "sgT": a(L0_ffn_shared_gate_w).T, "suT": a(L0_ffn_shared_up_w).T, "sdT": a(L0_ffn_shared_down_w).T,
    }
    arrays = {k: np.ascontiguousarray(v) for k, v in arrays.items()}
    nc = bacc.Bacc("TRN2", target_bir_lowering=False, num_devices=1)
    aps = [nc.dram_tensor(k, v.shape, mybir.dt.from_np(v.dtype), kind="ExternalInput").ap() for k, v in arrays.items()]
    out = nc.dram_tensor("out", (TOK, D), mybir.dt.float32, kind="ExternalOutput").ap()
    build(nc, *aps, out)
    r = run_bass_kernel_spmd(nc, [arrays], core_ids=[0])
    return r.results[0]["out"].reshape(B, SQ, D)
```

```python
from contextlib import ExitStack

import numpy as np
import concourse.bass as bass
from concourse import mybir

B, SQ, D = 16, 64, 512
TOK = B * SQ
P = 128
NT = TOK // P
KD = D // P
XH, XD, XL = 16, 32, 128
MH, DN, DR, DV = 20, 192, 64, 64
QR, KL = 192, 128
E, TOPK, CAP, FI = 64, 6, 128, 192
SI = 2 * FI
H3 = FI // 3
R = 4
ROWS = TOK + CAP
NEG = -1.0e30
FLOOR = -3.0e38

C_ID, C_MASK, C_BEFORE, C_IOTA, C_ONES = 0, 128, 256, 384, 512
C_COS, C_SIN, C_TOK = 640, 704, 768
C_SPARE, C_EPS5, C_EPS6, C_HEAD, C_COLS = 776, 777, 778, 779, 784


def constant_table():
    c = np.zeros((P, C_COLS), np.float32)
    p = np.arange(P)
    c[:, C_ID:C_ID + P] = np.eye(P)
    same = (p[:, None] // SQ) == (p[None, :] // SQ)
    c[:, C_MASK:C_MASK + P] = np.where(same & (p[None, :] <= p[:, None]), 0.0, NEG)
    c[:, C_BEFORE:C_BEFORE + P] = p[:, None] < p[None, :]
    c[:, C_IOTA:C_IOTA + P] = p[None, :]
    c[:, C_ONES:C_ONES + P] = 1.0
    inv_freq = (1.0 / np.float32(1000000.0) ** (np.arange(0, DR, 2, dtype=np.float32) / np.float32(DR))).astype(np.float32)
    freqs = np.arange(SQ, dtype=np.float32)[:, None] * inv_freq[None, :]
    emb = np.concatenate([freqs, freqs], axis=-1)
    sign = np.where(np.arange(DR) < DR // 2, -1.0, 1.0).astype(np.float32)
    cos, sin = np.cos(emb), np.sin(emb) * sign
    c[:, C_COS:C_COS + DR] = np.tile(cos, (2, 1))
    c[:, C_SIN:C_SIN + DR] = np.tile(sin, (2, 1))
    c[:, C_TOK:C_TOK + NT] = P * np.arange(NT)[None, :] + p[:, None] + 1
    c[:, C_SPARE] = TOK + 1 + p
    c[:, C_HEAD:C_HEAD + 4] = p[:, None] // XD == np.arange(4)[None, :]
    c[:, C_EPS5] = 1e-5
    c[:, C_EPS6] = 1e-6
    return c


def attend(units, between):
    o = []
    for u in range(len(units) + 3):
        if u < len(units):
            o.append(("S",) + units[u])
        o.extend(between.get(u, []))
        for lag, kind in ((1, "R"), (2, "T"), (3, "A")):
            if 0 <= u - lag < len(units):
                o.append((kind,) + units[u - lag])
    return o


def job(t, *names):
    return [("job", n, t) for n in names]


def keys(t, *groups):
    return [("K", ("A", g), t) for g in groups]


def second_and_next(t, cross=True, start=True):
    b = [(("B", k), t) for k in range(MH // 4)]
    a = [(("A", k), t + 1) for k in range(XH // 4)]
    if cross:
        units = [a[0], a[1], b[0], b[1], a[2], b[2], a[3], b[3], b[4]]
        between = {0: job(t, "r0", "l0"), 1: job(t, "l1", "v2_0") + keys(t + 1, 2), 2: job(t, "r1"),
                   3: job(t, "l2") + keys(t + 1, 3), 4: job(t, "r2"), 5: job(t, "l3"), 6: job(t, "l4"), 7: job(t, "v2_1"), 8: job(t, "v2_2")}
        if start:
            between[4] = between[4] + [("stat", "ln1", t + 2)]
            between[5] = [("norm", "ln1", t + 2)] + between[5]
        else:
            between[5] = between[5] + job(t, "g00", "g01", "g02")
            between[8] = between[8] + job(t, "u00")
    else:
        units = b
        between = {0: job(t, "l1", "v2_0", "gt0"), 1: job(t, "r1", "l2") + [("exps", 0, t)],
                   2: job(t, "r2", "l3", "v2_1"), 3: job(t, "l4"), 4: job(t, "v2_2", "d1")}
    o = job(t, "d0", "r0", "l0") if not cross else []
    if start:
        o.append(("ctx", "ctx", t + 2))
    o += attend(units, between)
    del o[o.index(("R",) + b[4]) + 1:]
    if start:
        o += job(t + 2, "xT", "v")
    o += [("T",) + b[3], ("A",) + (a[3] if cross else b[2])]
    o += [("T",) + b[4]] if cross else job(t, "d2") + [("T",) + b[4]]
    if cross:
        o += job(t + 1, "o")
    o += [("A",) + b[3], ("A",) + b[4]]
    if cross:
        o += [("stat", "ln2", t + 1), ("norm", "ln2", t + 1)]
        if not start:
            o += job(t, "u01")
    else:
        o.append(("top", 0, t))
    o.append(("begin", "o2", t))
    if cross:
        o += job(t + 1, "x2T")
    o += job(t, "o2") + [("stat", "ln3", t)]
    o += job(t + 2, "k") + keys(t + 2, 0, 1) if start else job(t, "u02" if cross else "d3")
    if cross:
        o += job(t + 1, "a")
    o.append(("norm", "ln3", t))
    if start:
        o += job(t + 2, "q")
    elif cross:
        o += job(t, "gl0")
    if cross:
        o += job(t + 1, "aT")
    return o + job(t, "x3T")


def last_steps(t):
    def slots(*of):
        return [("slots", k, t) for k in of]

    def hot(*of):
        return [("hot", k, t) for k in of]

    o = job(t, "rk0", "gl1") + hot(0, 1, 2, 3) + job(t, "g10", "gt1") + [("exps", 1, t)] + job(t, "g11", "g12") + slots(0, 1)
    o += [("top", 1, t)] + job(t, "u10") + slots(2, 3) + job(t, "rk1", "u11") + hot(4, 5) + job(t, "u12", "d4")
    o += slots(4) + hot(6) + slots(5) + hot(7) + slots(6, 7) + [("rows", None, t)]
    return o + job(t, "d5", "d6", "d7")


def first_steps():
    o = [("stat", "ln1", 0), ("norm", "ln1", 0), ("ctx", "ctx", 0)] + job(0, "v", "k") + keys(0, 0, 1) + job(0, "xT", "q")
    o += [("stat", "ln1", 1), ("norm", "ln1", 1)]
    o += attend([(("A", k), 0) for k in range(XH // 4)],
                {1: keys(0, 2) + job(0, "M0"), 2: [("ctx", "ctx", 1)] + keys(0, 3) + job(0, "M1"),
                 3: job(0, "M2"), 4: job(0, "M3"), 5: job(0, "M4")})
    o += job(0, "M5", "M6", "M7")
    o += job(1, "xT", "v") + job(0, "o") + [("stat", "ln2", 0), ("norm", "ln2", 0)] + [("begin", "M8", 0)] + job(0, "x2T", "M8")
    return o + job(1, "k") + keys(1, 0, 1) + job(0, "a") + job(1, "q") + job(0, "aT", "M9")


O2_BEGIN = 6
REPEATS = 3
FIRST = first_steps()
LOOP = second_and_next(0) + second_and_next(1)
LAST = second_and_next(6, start=False) + second_and_next(7, cross=False, start=False) + last_steps(7)
ALL = FIRST + [(k, n, t + 2 * i) for i in range(REPEATS) for k, n, t in LOOP] + LAST
NTH = {kind: {(n, t): c for c, (n, t) in enumerate((n, t) for k, n, t in ALL if k == kind)} for kind in ("job", "S")}
PER_LOOP = {kind: sum(k == kind for k, _, _ in LOOP) for kind in ("job", "S")}
NJOBS, NUNITS = len(NTH["job"]), len(NTH["S"])
assert PER_LOOP["job"] % 2 == 0 and PER_LOOP["S"] % 6 == 0


def nth(kind, name, i, t):
    if type(i) is int:
        return NTH[kind][name, t + 2 * i]
    n = [NTH[kind][name, t + 2 * k] - k * PER_LOOP[kind] for k in range(REPEATS)]
    assert min(n) == max(n), (name, t, n)
    return n[0]


def build(nc, x, ctxT, consts, wqT, wkvT, woutT, waT, lnq, lnkv, wqb, wqrT, wkb, wvbT, woT,
          gateT, gate_up, down, sgT, suT, sdT, out):
    fp32, u32 = mybir.dt.float32, mybir.dt.uint32
    ALU, ACT, AX = mybir.AluOpType, mybir.ActivationFunctionType, mybir.AxisListType

    hold = ExitStack()
    with hold:
        x3n_rows = nc.dram_tensor("x3n_rows", [ROWS, D], fp32).ap()
        sums = [nc.dram_tensor(f"sums{k}", [ROWS, D], fp32).ap() for k in range(2)]

        def sb(name, shape, dt=fp32):
            return hold.enter_context(nc.sbuf_tensor(name, shape, dt))

        cst = sb("cst", [P, C_COLS])
        x_all = sb("x_all", [P, NT, D])
        x3nT = sb("x3nT", [P, KD, TOK])
        small = sb("small", [P, 64])
        ARENA = 43700
        arena = sb("arena", [P, ARENA])
        used = [0]

        def take(*shape):
            n = int(np.prod(shape))
            v = arena[:, used[0]:used[0] + n]
            used[0] += n
            assert used[0] <= ARENA, used
            if len(shape) == 2:
                v = v.rearrange("p (a b) -> p a b", b=shape[1])
            elif len(shape) == 3:
                v = v.rearrange("p (a b c) -> p a b c", b=shape[1], c=shape[2])
            return v

        WqT, WkvT, ctxT_all, ctx_cur = take(KD, D), take(2 * D), take(TOK), take(P)
        dead_at_last_two = used[0]
        WoutT, WaT = take(KD, D), take(KD, QR + KL + DR)
        xn1, xnT, kT, qT, v, cT = take(D), take(KD, P), take(KD, P), take(KD, P), take(2, D), take(KD, P)
        kz = take(2, 4, P)
        xn2, x2T = take(D), take(KD, P)
        dead_at_last_tile = used[0]
        M0, M1 = take(MH, KL), take(MH, KL)
        WqrT0, WqrT1, WvbT = take(MH * DR), take(MH * DR), take(MH * DV)
        an, xn3 = take(QR + KL + 2 * DR), take(D)
        masked, probs, probsT = take(2, 4, P), take(3, 4, P), take(2, 4, P)
        rot1, rot2, junk = take(DR), take(DR), take(QR + KL)
        zeros = take(D)
        hid_first = take(SI // P, 512)
        qc0, qc1, klT = take(P), take(P), take(P)
        krz = take(2, P)
        mark = used[0]
        wqb0, wqb1, wkb0, wkb1 = take(MH, QR), take(MH, QR), take(MH, KL), take(MH, KL)
        end_attention = used[0]
        used[0] = mark
        WoT, v2, qr, c2T, ql = take(MH // 2, D), take(MH * DV), take(MH // 2, P), take(MH // 2, P), take(MH, P)
        assert used[0] <= end_attention

        used[0] = 0
        WgT, WsgT, WsuT = take(KD, E), take(KD, SI), take(KD, SI)
        assert used[0] <= dead_at_last_two
        used[0] = dead_at_last_two
        WsdT = take(SI // P, D)
        assert used[0] <= dead_at_last_two + KD * D
        lgT, lg, ex = take(TOK // 2), take(NT, E), take(NT, E)
        top_w, top_i, top_f = take(NT, 8), take(NT, 8).bitcast(u32), take(NT, 8)
        choice, chosen_by = take(NT * TOPK, E), take(NT, E)
        before, rank_of = take(NT, E), take(NT * TOPK)
        mark = used[0]
        hid_second = take(SI // P, 512)
        assert used[0] <= dead_at_last_tile
        used[0] = mark
        picked_first = take(NT // 2 * TOPK, E)
        used[0] = dead_at_last_tile
        wgu, wd0, wd1 = take(R, KD, 2 * FI), take(R, D), take(R, D)
        gx, gxT, eo = take(R, D), take(2, D), take(R, D)
        silu_e, hid_e = take(2, 3 * P), take(2, 2 * P)
        idx_w = take(2, E)
        spare = take(E)
        gather_rows, add_rows = take(R).bitcast(u32), take(R).bitcast(u32)
        row_of = take(E).bitcast(u32)
        mark = used[0]
        hot = take(NT * TOPK, P)
        used[0] = mark + NT // 2 * TOPK * P
        picked_second = take(NT // 2 * TOPK, E)
        used[0] = mark + NT * TOPK * P
        last_tokens = arena[:, mark:mark + NT * P].rearrange("p (a b) -> p a b", b=P)
        odd_sums = arena[:, used[0]:used[0] + NT * D].rearrange("p (a b) -> p a b", b=D)
        pair = take(NT * TOPK, 2, E)

        LN = ("ln1", "ln2", "ln3")
        stat = small[:, 0:6]
        mv = {n: small[:, 6 + 2 * k:8 + 2 * k] for k, n in enumerate(LN)}
        std = {n: small[:, 12 + k:13 + k] for k, n in enumerate(LN)}
        rstd = {n: small[:, 15 + k:16 + k] for k, n in enumerate(LN)}
        ss, rms, rrms = (small[:, 18 + 2 * k:20 + 2 * k] for k in range(3))
        lnq0, lnq1, lnk = small[:, 26:27], small[:, 27:28], small[:, 28:29]
        mx, nmx, den, rden = (sb(n, [P, 3, 4]) for n in ("mx", "nmx", "den", "rden"))
        mx8, sum8, rsum8 = small[:, 32:40], small[:, 40:48], small[:, 48:56]

        ident, mask = cst[:, C_ID:C_ID + P], cst[:, C_MASK:C_MASK + P]
        eps5, eps6 = cst[:, C_EPS5:C_EPS5 + 1], cst[:, C_EPS6:C_EPS6 + 1]

        def bank_pair(name):
            return [hold.enter_context(nc.psum_tensor(f"{name}{k}", [P, 512], fp32)) for k in range(2)]

        job_bank, s_bank, t_bank, a_bank = (bank_pair(n) for n in ("job_bank", "s_bank", "t_bank", "a_bank"))
        last_bank = [*a_bank, *t_bank, *s_bank, *job_bank]

        PER = {}

        def sem(name, per=0):
            s = hold.enter_context(nc.semaphore(name))
            PER[name] = per
            return s, name

        def at(s, i, k):
            return i * PER[s[1]] + k

        def tiles(i, t):
            return i * 2 + (t + 1)

        def units(name, i, t, behind=0):
            n = nth("S", name, i, t) + 1 - behind
            return n if type(i) is int else i * PER_LOOP["S"] + n

        def wait_unit(eng, s, name, i, t, behind=0):
            if nth("S", name, i, t) + 1 > behind:
                eng.wait_ge(s[0], units(name, i, t, behind))

        loaded = {n: sem(f"loaded_{n}") for n in (
            "consts", "ctx0", "ctx2", "x0", "x1", "x2", "wkv", "wq", "qkb0", "qkb1", "wout", "wa", "qr0", "qr1",
            "wvb", "wo", "lnq0", "lnq1", "lnkv", "gate", "sg", "su", "sd")}
        filled = [sem(f"filled{k}") for k in range(2)]
        copied = [sem(f"copied{k}") for k in range(2)]
        ctx_ready = sem("ctx_ready")
        ln_var, ln_std, ln_done = ({n: sem(f"{what}_{n}") for n in LN} for what in ("ln_var", "ln_std", "ln_done"))
        rms_sum, rms_std = sem("rms_sum"), sem("rms_std")
        zeros_ready = sem("zeros_ready")
        kz_ready = sem("kz_ready")
        scores_ready, masked_ready = sem("scores_ready"), sem("masked_ready")
        exp_done, rden_ready, norm_done = sem("exp_done"), sem("rden_ready"), sem("norm_done")
        pT_ready, pT_copied = sem("pT_ready"), sem("pT_copied")
        av_ready, av_copied = sem("av_ready"), sem("av_copied")
        dve_chain = sem("dve_chain")
        rows_stored = sem("rows_stored")
        rows_gone = sem("rows_gone")
        zeros_stored = sem("zeros_stored")

        def bank_of(i, name, t):
            return job_bank[nth("job", name, i, t) % 2]

        def jobs(i, n):
            return n // 2 + 1 if type(i) is int else i * (PER_LOOP["job"] // 2) + (n // 2 + 1)

        def wait_filled(eng, i, name, t):
            n = nth("job", name, i, t)
            eng.wait_ge(filled[n % 2][0], jobs(i, n))

        def wait_copied(eng, i, *names, free_for=None):
            latest = {}
            if free_for is not None:
                n = nth("job", free_for[0], i, free_for[1]) - 2
                latest[n % 2] = n
            for name, t in names:
                n = nth("job", name, i, t)
                latest[n % 2] = max(n, latest.get(n % 2, n))
            for slot, n in sorted(latest.items()):
                if n >= 0:
                    eng.wait_ge(copied[slot][0], jobs(i, n))

        JOBS_IN = [(NJOBS + 1) // 2, NJOBS // 2]

        def residual(i, t):
            return x_all[:, t] if type(i) is int else x_all[:, bass.ds(i * 2 + t, 1), :].rearrange("p o d -> p (o d)")

        def tokens(i, t):
            return slice(t * P, (t + 1) * P) if type(i) is int else bass.ds(i * (2 * P) + t * P, P)

        def all_steps(eng, do):
            for kind, name, t in FIRST:
                do(0, kind, name, t)
            with eng.Fori(0, REPEATS) as i:
                for kind, name, t in LOOP:
                    do(i, kind, name, t)
            for kind, name, t in LAST:
                do(0, kind, name, t)

        lg_exp, choice_ready = sem("lg_exp"), sem("choice_ready")
        before_ready = sem("before_ready")
        pair_ready, hot_ready = sem("pair_ready"), sem("hot_ready")
        table_filled = sem("table_filled")
        rows_known = sem("rows_known")
        sums_stored = sem("sums_stored")
        w_loaded = [sem(f"w_loaded{r}", 64) for r in range(R)]
        gx_loaded = [sem(f"gx_loaded{r}", 16) for r in range(R)]
        gx_turned, gxT_copied = sem("gx_turned", R), sem("gxT_copied", R)
        gu_filled = sem("gu_filled", R)
        silu_done, hid_ready = sem("silu_done", R), sem("hid_ready", R)
        rows_copied = sem("rows_copied")
        eo_filled, eo_ready = sem("eo_filled", R), sem("eo_ready", R)
        added = [sem(f"added{k}", 8 * R) for k in range(2)]
        odd_loaded = [sem(f"odd_loaded{h}") for h in range(2)]
        even_loaded = [sem(f"even_loaded{t}") for t in range(NT)]
        last_known, last_filled = sem("last_known"), sem("last_filled")
        both_added, out_ready = sem("both_added"), sem("out_ready")
        out_stored = sem("out_stored")

        block = hold.enter_context(nc.Block())

        @block.sync
        def _(sp):
            sp.sem_inc(rows_gone[0], 1)
            xt = x.rearrange("(t p) d -> p t d", p=P)
            sp.dma_start(cst[:], consts).then_inc(loaded["consts"][0], 16)
            sp.dma_start(x_all[:, 0], xt[:, 0]).then_inc(loaded["x0"][0], 16)
            sp.dma_start(ctxT_all[:, 0:2 * P], ctxT[:, 0:2 * P]).then_inc(loaded["ctx0"][0], 16)
            sp.dma_start(WkvT, wkvT).then_inc(loaded["wkv"][0], 16)
            sp.dma_start(WqT, wqT.rearrange("(k p) n -> p k n", p=P)).then_inc(loaded["wq"][0], 16)
            sp.dma_start(x_all[:, 1], xt[:, 1]).then_inc(loaded["x1"][0], 16)
            for c in range(2):
                h = slice(c * MH // 2, (c + 1) * MH // 2)
                for dst, src in ((wqb0[:, h], wqb[0:P, h]), (wkb0[:, h], wkb[0:P, h]),
                                 (wqb1[0:DN - P, h], wqb[P:DN, h]), (wkb1[0:DN - P, h], wkb[P:DN, h])):
                    sp.dma_start(dst, src).then_inc(loaded[f"qkb{c}"][0], 16)
            for name, dst, src in (
                    ("wout", WoutT, woutT.rearrange("(k p) n -> p k n", p=P)),
                    ("wa", WaT, waT.rearrange("(k p) n -> p k n", p=P)),
                    ("lnq0", lnq0, lnq[0:P]), ("lnq1", lnq1[0:QR - P], lnq[P:QR]), ("lnkv", lnk, lnkv),
                    ("wvb", WvbT, wvbT), ("qr0", WqrT0, wqrT[0:P]), ("qr1", WqrT1[0:QR - P], wqrT[P:QR]),
                    ("x2", x_all[:, 2:NT], xt[:, 2:NT]), ("ctx2", ctxT_all[:, 2 * P:], ctxT[:, 2 * P:])):
                sp.dma_start(dst, src).then_inc(loaded[name][0], 16)
            wait_filled(sp, 0, "M9", 0)
            sp.dma_start(WoT, woT.rearrange("(k p) n -> p k n", p=P)).then_inc(loaded["wo"][0], 16)
            sp.wait_ge(zeros_ready[0], 2)
            for rows in (x3n_rows[TOK:ROWS], sums[0][TOK:ROWS], *(sums[1][k * P:(k + 1) * P] for k in range(ROWS // P))):
                sp.dma_start(rows, zeros).then_inc(zeros_stored[0], 16)

            def load_expert(i, r):
                e = i * R + r
                sp.dma_start(wgu[:, r], gate_up[bass.ds(e, 1)].rearrange("o (k p) n -> p (o k) n", p=P)).then_inc(w_loaded[r][0], 16)
                rows = down[bass.ds(e, 1)].rearrange("o (f m) n -> m (o f) n", m=3)
                for m in range(3):
                    dst = wd1[0:H3, r] if m == 2 else wd0[m * H3:(m + 1) * H3, r]
                    sp.dma_start(dst, rows[m]).then_inc(w_loaded[r][0], 16)

            def step(i, kind, name, t):
                if (kind, name) == ("norm", "ln3"):
                    sp.wait_ge(ln_done["ln3"][0], tiles(i, t))
                    rows = x3n_rows[tokens(i, t), :]
                    sp.dma_start(rows, xn3).then_inc(rows_stored[0], 16)
                    sp.wait_ge(rows_stored[0], 16 * (t + 1) if type(i) is int else i * 32 + 16 * (t + 1))
                    sp.sem_inc(rows_gone[0], 1)
                if type(i) is int and (kind, t) == ("job", NT - 2):
                    if name == "v2_0":
                        wait_filled(sp, 0, "q", NT - 1)
                        wait_filled(sp, 0, "k", NT - 1)
                        sp.dma_start(WsgT, sgT.rearrange("(k p) n -> p k n", p=P)).then_inc(loaded["sg"][0], 16)
                        sp.dma_start(WsuT, suT.rearrange("(k p) n -> p k n", p=P)).then_inc(loaded["su"][0], 16)
                        sp.dma_start(WgT, gateT.rearrange("(k p) n -> p k n", p=P)).then_inc(loaded["gate"][0], 16)
                    elif name == "o2":
                        wait_filled(sp, 0, "o", NT - 1)
                        sp.dma_start(WsdT, sdT.rearrange("(k p) n -> p k n", p=P)).then_inc(loaded["sd"][0], 16)

                if (kind, name) == ("job", "x3T") and type(i) is int and t == NT - 1:
                    wait_copied(sp, 0, ("o2", t), ("x3T", t))
                    for r in range(R):
                        load_expert(0, r)

            all_steps(sp, step)
            for h in range(2):
                wait_copied(sp, 0, *((f"d{m}", NT - 1) for m in range(h * NT // 2, (h + 1) * NT // 2)))
                sp.dma_start(sums[0][h * TOK // 2:(h + 1) * TOK // 2].rearrange("(t p) d -> p t d", p=P),
                             x_all[:, h * NT // 2:(h + 1) * NT // 2]).then_inc(sums_stored[0], 16)
            with sp.Fori(1, E // R) as i:
                for r in range(R):
                    sp.wait_ge(eo_filled[0], i * R + (r + 1 - R))
                    load_expert(i, r)
            sp.wait_ge(added[1][0], 16 * (E // 2 - 1))
            for h in range(2):
                half = slice(h * NT // 2, (h + 1) * NT // 2)
                sp.dma_start(odd_sums[:, half], sums[1][h * TOK // 2:(h + 1) * TOK // 2].rearrange("(t p) d -> p t d", p=P)
                             ).then_inc(odd_loaded[h][0], 16)
                sp.wait_ge(added[0][0], 16 * E // 2)
                for t in range(h * NT // 2, (h + 1) * NT // 2):
                    sp.dma_start(x_all[:, t], sums[0][t * P:(t + 1) * P]).then_inc(even_loaded[t][0], 16)
            for t in range(NT):
                sp.wait_ge(out_ready[0], t + 1)
                sp.dma_start(out[t * P:(t + 1) * P], x_all[:, t]).then_inc(out_stored[0], 16)
            sp.wait_ge(out_stored[0], 16 * NT)

        @block.gpsimd
        def _(pool):
            def stand():
                nc.gpsimd.tensor_tensor(small[:, 61:62], eps5, eps5, ALU.add)

            nc.gpsimd.memset(zeros, 0.0).then_inc(zeros_ready[0], 1)
            nc.gpsimd.memset(krz, 0.0).then_inc(zeros_ready[0], 1)
            pool.wait_ge(loaded["consts"][0], 16)
            pool.wait_ge(loaded["ctx0"][0], 16)

            def step(i, kind, name, t):
                if kind == "ctx":
                    if t + (type(i) is not int) > 0:
                        wait_filled(pool, i, "k", t - 1)
                        if type(i) is not int:
                            pool.wait_ge(loaded["ctx2"][0], 16)
                            stand()
                    nc.gpsimd.tensor_copy(ctx_cur, ctxT_all[:, tokens(i, t)]).then_inc(ctx_ready[0], 1)
                elif kind == "K":
                    hg = name[1]
                    if hg == 0:
                        wait_copied(pool, i, ("k", t))
                    if hg >= 2:
                        wait_unit(pool, scores_ready, ("A", hg - 2), i, t)
                    elif type(i) is not int or t > 0:
                        wait_unit(pool, scores_ready, ("A", hg + 2), i, t - 1)
                    nc.gpsimd.tensor_tensor(
                        kz[:, hg % 2], kT[:, hg].unsqueeze(1).to_broadcast([P, 4, P]),
                        cst[:, C_HEAD:C_HEAD + 4].unsqueeze(2).to_broadcast([P, 4, P]), ALU.mult).then_inc(kz_ready[0], 1)
                elif kind == "R":
                    n = nth("S", name, i, t)
                    wait_unit(pool, rden_ready, name, i, t)
                    nc.gpsimd.tensor_tensor(
                        probs[:, n % 3], probs[:, n % 3], rden[:, n % 3, :].unsqueeze(2).to_broadcast([P, 4, P]),
                        ALU.mult).then_inc(norm_done[0], 1)

                elif type(i) is int and (kind, name, t) in (("job", "x3T", NT - 1), ("top", 1, NT - 1)):
                    half = int(kind == "top")
                    if half == 0:
                        wait_copied(pool, 0, ("o2", t), ("x3T", t))
                    pool.wait_ge(choice_ready[0], half + 1)
                    for k in range(half * NT // 2, (half + 1) * NT // 2):
                        of = slice(k * TOPK, (k + 1) * TOPK)
                        nc.gpsimd.tensor_scalar(pair[:, of, 0], choice[:, of], cst[:, C_TOK + k:C_TOK + k + 1], None, ALU.mult)
                        nc.gpsimd.tensor_tensor(pair[:, of, 1], choice[:, of], top_w[:, k, 0:TOPK].unsqueeze(2).to_broadcast([P, TOPK, E]),
                                                ALU.mult).then_inc(pair_ready[0], 1)

            all_steps(pool, step)

            def rows_in_place(dst, e, n):
                nc.gpsimd.tensor_copy(dst, row_of[:, bass.ds(e, 1)]).then_inc(rows_copied[0], 1)
                pool.wait_ge(rows_copied[0], n + 1)
                stand()

            def gather(i, r, n):
                pool.wait_ge(gx_turned[0], i * R + (r + 1 - R))
                rows_in_place(gather_rows[:, r:r + 1], i * R + r, n)
                nc.gpsimd.indirect_dma_start(
                    gx[:, r], None, x3n_rows, bass.IndirectOffsetOnAxis(gather_rows[:, r:r + 1], 0)
                ).then_inc(gx_loaded[r][0], 16)

            def add(i, r, n):
                pool.wait_ge(eo_ready[0], at(eo_ready, i, r + 1))
                rows_in_place(add_rows[:, r:r + 1], i * R + r, n)
                nc.gpsimd.indirect_dma_start(
                    sums[r % 2], bass.IndirectOffsetOnAxis(add_rows[:, r:r + 1], 0), eo[:, r], None,
                    compute_op=ALU.add).then_inc(added[r % 2][0], 16)

            pool.wait_ge(rows_known[0], 1)
            pool.wait_ge(zeros_stored[0], 16 * (2 + ROWS // P))
            pool.wait_ge(rows_stored[0], 16 * NT)
            for r in range(R):
                nc.gpsimd.indirect_dma_start(
                    gx[:, r], None, x3n_rows, bass.IndirectOffsetOnAxis(row_of[:, r:r + 1], 0)
                ).then_inc(gx_loaded[r][0], 16)
            pool.wait_ge(sums_stored[0], 32)

            def adds(i, last=False):
                for r in range(R - last):
                    if not last:
                        gather(i + 1, r, i * 2 * R + 2 * r)
                    if type(i) is not int or i * R + r >= 2:
                        pool.wait_ge(added[r % 2][0], at(added[r % 2], i, 16 * (r // 2)))
                    add(i, r, i * 2 * R + (r if last else 2 * r + 1))

            adds(0)
            with pool.Fori(1, E // R - 1) as i:
                adds(i)
            adds(E // R - 1, last=True)

        @block.scalar
        def _(act):
            act.wait_ge(loaded["consts"][0], 16)

            def step(i, kind, name, t):
                def to(dst, src=None):
                    wait_filled(act, i, name, t)
                    n = nth("job", name, i, t)
                    return nc.scalar.copy(dst, job_bank[n % 2][:, :] if src is None else src).then_inc(copied[n % 2][0], 1)

                def flat(v):
                    return v.rearrange("p a b -> p (a b)")

                if kind == "stat":
                    act.wait_ge(ln_var[name][0], tiles(i, t))
                    nc.scalar.activation(std[name], mv[name][:, 1:2], ACT.Sqrt, bias=eps5).then_inc(ln_std[name][0], 1)
                elif kind == "S":
                    n, scale = nth("S", name, i, t), (float(DN + DR) if name[0] == "B" else float(XD)) ** -0.5
                    wait_unit(act, masked_ready, name, i, t)
                    wait_unit(act, pT_ready, name, i, t, behind=3)
                    for j in range(4):
                        last = nc.scalar.activation(
                            probs[:, n % 3, j], masked[:, n % 2, j], ACT.Exp, bias=nmx[:, n % 3, j:j + 1],
                            scale=scale, accum_out=den[:, n % 3, j:j + 1])
                    last.then_inc(exp_done[0], 1)
                elif kind == "A":
                    n, hg = nth("S", name, i, t), name[1]
                    wait_unit(act, av_ready, name, i, t)
                    if name[0] == "B":
                        last = nc.scalar.copy(c2T[:, 2 * hg:2 * hg + 2], a_bank[n % 2][:, 0:2 * P].rearrange("p (a b) -> p a b", b=P))
                    else:
                        last = nc.scalar.copy(cT[:, hg], a_bank[n % 2][:, 0:P])
                    last.then_inc(av_copied[0], 1)
                elif kind == "job":
                    if name[0] == "M":
                        n, m = nth("job", name, i, t), int(name[1])
                        bank = job_bank[n % 2][:, :].rearrange("p (a b c) -> p a b c", a=2, c=P)
                        wait_filled(act, i, name, t)
                        nc.scalar.copy(M0[:, 2 * m:2 * m + 2], bank[:, 0])
                        nc.scalar.copy(M1[0:QR - P, 2 * m:2 * m + 2], bank[0:QR - P, 1]).then_inc(copied[n % 2][0], 1)
                    elif name == "k":
                        to(flat(kT))
                    elif name == "x2T":
                        to(flat(x2T))
                    elif name == "a":
                        bank = bank_of(i, name, t)
                        wait_filled(act, i, name, t)
                        nc.scalar.activation(junk[:, 0:QR], bank[:, 0:QR], ACT.Square, accum_out=ss[:, 0:1])
                        nc.scalar.activation(junk[:, QR:QR + KL], bank[:, QR:QR + KL], ACT.Square, accum_out=ss[:, 1:2]).then_inc(rms_sum[0], 1)
                        act.wait_ge(rms_sum[0], tiles(i, t))
                        nc.scalar.activation(rms[:, 0:1], ss[:, 0:1], ACT.Sqrt, bias=eps6, scale=1.0 / QR)
                        nc.scalar.activation(rms[:, 1:2], ss[:, 1:2], ACT.Sqrt, bias=eps6, scale=1.0 / KL).then_inc(rms_std[0], 1)
                    elif name[0:2] == "gl":
                        h = int(name[2])
                        to(lgT[0:E], bank_of(i, name, t)[0:E, :])
                    elif name[0] == "g" and name[1] != "t":
                        wait_filled(act, i, name, t)
                        n = nth("job", name, i, t)
                        hid = (hid_first, hid_second)[int(name[1])]
                        if name == "g10":
                            act.wait_ge(hot_ready[0], 1)
                        nc.scalar.activation(hid[:, int(name[2])], job_bank[n % 2][:, :], ACT.Silu).then_inc(copied[n % 2][0], 1)
                    elif name in ("v2_0", "v2_1"):
                        m = int(name[3])
                        to(v2[:, m * 512:(m + 1) * 512])
                    elif name[0] == "r" and name[1] != "k":
                        m = int(name[1])
                        w = min(4, MH // 2 - 4 * m)
                        to(flat(qr[:, 4 * m:4 * m + w]), bank_of(i, name, t)[:, 0:w * P])
                    elif name[0] == "l" and int(name[1]) % 2 == 0:
                        m = int(name[1])
                        to(flat(ql[:, 4 * m:4 * m + 4]))
                    elif name == "x3T":
                        to(x3nT[:, :, tokens(i, t)], bank_of(i, name, t)[:, :].rearrange("p (k t) -> p k t", t=P))

                elif kind == "exps":
                    of = slice(name * NT // 2, (name + 1) * NT // 2)
                    wait_copied(act, i, (f"gt{name}", t))
                    nc.scalar.activation(ex[:, of], lg[:, of], ACT.Exp).then_inc(lg_exp[0], 1)

            all_steps(act, step)
            def turned(i, r):
                i, r = i + r // R, r % R
                act.wait_ge(gx_turned[0], at(gx_turned, i, r + 1))
                if type(i) is not int or i * R + r >= 2:
                    act.wait_ge(gu_filled[0], i * R + (r - 1))
                nc.scalar.copy(gxT[:, r % 2], t_bank[r % 2][:, :]).then_inc(gxT_copied[0], 1)

            def experts(i):
                for r in range(R):
                    if type(i) is not int or i * R + r + 1 < E:
                        turned(i, r + 1)
                    act.wait_ge(gu_filled[0], at(gu_filled, i, r + 1))
                    if type(i) is not int or i * R + r >= 2:
                        act.wait_ge(hid_ready[0], i * R + (r - 1))
                    nc.scalar.activation(silu_e[0:H3, r % 2], s_bank[r % 2][0:H3, 0:3 * P], ACT.Silu).then_inc(silu_done[0], 1)

            act.wait_ge(table_filled[0], 1)
            turned(0, 0)
            experts(0)
            with act.Fori(1, E // R - 1) as i:
                experts(i)
            experts(E // R - 1)

        @block.vector
        def _(dve):
            for n in ("consts", "x0"):
                dve.wait_ge(loaded[n][0], 16)
            def links_of(kind, name):
                return 2 if (kind, name) == ("job", "a") else int(kind in ("stat", "norm", "S"))

            links = [0]
            LINKS_PER_LOOP = sum(links_of(k, n) for k, n, _ in LOOP)
            FIRST_LINKS = sum(links_of(k, n) for k, n, _ in FIRST)
            scale_of = {"A": float(XD) ** -0.5, "B": float(DN + DR) ** -0.5}

            def step(i, kind, name, t):
                in_loop = type(i) is not int

                def chained(ins):
                    links[0] += 1
                    ins.then_inc(dve_chain[0], 1)
                    dve.wait_ge(dve_chain[0], i * LINKS_PER_LOOP + links[0] if in_loop else links[0])

                def stand():
                    if in_loop:
                        k = 59 if kind == "S" else 60
                        nc.vector.memset(small[:, k:k + 1], 0.0)

                def to(dst, src=None):
                    wait_filled(dve, i, name, t)
                    n = nth("job", name, i, t)
                    nc.vector.tensor_copy(dst, job_bank[n % 2][:, :] if src is None else src).then_inc(copied[n % 2][0], 1)

                def flat(v):
                    return v.rearrange("p a b -> p (a b)")

                if kind == "stat":
                    if name != "ln1":
                        wait_copied(dve, i, ("o" if name == "ln2" else "o2", t))
                    stand()
                    chained(nc.vector.bn_stats(stat, residual(i, t)))
                    stand()
                    nc.vector.bn_aggr(mv[name], stat).then_inc(ln_var[name][0], 1)
                elif kind == "norm":
                    dve.wait_ge(ln_std[name][0], tiles(i, t))
                    chained(nc.vector.reciprocal(rstd[name], std[name]))
                    if name == "ln3":
                        dve.wait_ge(rows_gone[0], tiles(i, t))
                    dst = {"ln1": xn1, "ln2": xn2, "ln3": xn3}[name]
                    nc.vector.tensor_scalar(dst, residual(i, t), mv[name][:, 0:1], rstd[name],
                                            ALU.subtract, ALU.mult).then_inc(ln_done[name][0], 1)
                elif kind == "S":
                    n = nth("S", name, i, t)
                    wait_unit(dve, scores_ready, name, i, t)
                    stand()
                    for j in range(4):
                        last = nc.vector.tensor_tensor_reduce(
                            out=masked[:, n % 2, j], in0=s_bank[n % 2][:, j * P:(j + 1) * P], in1=mask,
                            scale=1.0, scalar=FLOOR, op0=ALU.add, op1=ALU.max, accum_out=mx[:, n % 3, j:j + 1])
                    chained(last)
                    nc.vector.tensor_scalar(nmx[:, n % 3], mx[:, n % 3], -scale_of[name[0]], None, ALU.mult).then_inc(masked_ready[0], 1)
                elif kind == "R":
                    n = nth("S", name, i, t)
                    wait_unit(dve, exp_done, name, i, t)
                    nc.vector.reciprocal(rden[:, n % 3], den[:, n % 3]).then_inc(rden_ready[0], 1)
                elif kind == "T":
                    n = nth("S", name, i, t)
                    wait_unit(dve, pT_ready, name, i, t)
                    wait_unit(dve, av_ready, name, i, t, behind=2)
                    nc.vector.tensor_copy(flat(probsT[:, n % 2]), t_bank[n % 2][:, :]).then_inc(pT_copied[0], 1)
                elif kind == "job":
                    bank, slot = bank_of(i, name, t), nth("job", name, i, t) % 2
                    if name == "v":
                        to(v[:, t % 2])
                    elif name == "v2_2":
                        to(v2[:, 1024:MH * DV], bank[:, 0:MH * DV - 1024])
                    elif name == "xT":
                        to(flat(xnT))
                    elif name == "q":
                        to(flat(qT))
                    elif name[0] == "l" and int(name[1]) % 2 == 1:
                        m = int(name[1])
                        to(flat(ql[:, 4 * m:4 * m + 4]))
                    elif name[0] == "u":
                        hid, m = (hid_first, hid_second)[int(name[1])], int(name[2])
                        wait_copied(dve, i, (f"g{name[1:]}", t))
                        wait_filled(dve, i, name, t)
                        nc.vector.tensor_tensor(hid[:, m], hid[:, m], bank[:, :], ALU.mult).then_inc(copied[slot][0], 1)
                    elif name[0:2] == "rk":
                        h = int(name[2])
                        picked = (picked_first, picked_second)[h]
                        wait_filled(dve, i, name, t)
                        for k in range(NT // 2):
                            n = h * NT // 2 + k
                            last = nc.vector.tensor_tensor(
                                picked[:, k * TOPK:(k + 1) * TOPK], choice[:, n * TOPK:(n + 1) * TOPK],
                                bank[:, k * E:(k + 1) * E].unsqueeze(1).to_broadcast([P, TOPK, E]), ALU.mult)
                        last.then_inc(copied[slot][0], 1)
                        wait_copied(dve, i, (name, t))
                        n = NT // 2 * TOPK
                        chained(nc.vector.tensor_reduce(rank_of[:, h * n:(h + 1) * n], picked, AX.X, ALU.add))
                    elif name[0:2] == "gt":
                        h = int(name[2])
                        of = slice(h * NT // 2, (h + 1) * NT // 2)
                        logits = bank[:, 0:NT // 2 * E].rearrange("p (t e) -> p t e", e=E)
                        wait_filled(dve, i, name, t)
                        chained(nc.vector.tensor_reduce(mx8[:, of], logits, AX.X, ALU.max))
                        nc.vector.tensor_tensor(lg[:, of], logits, mx8[:, of].unsqueeze(2).to_broadcast([P, NT // 2, E]),
                                                ALU.subtract).then_inc(copied[slot][0], 1)
                    elif name[0] == "d":
                        m = int(name[1])
                        wait_filled(dve, i, name, t)
                        nc.vector.tensor_tensor(x_all[:, m], x_all[:, m], bank[:, :], ALU.add).then_inc(copied[slot][0], 1)
                    elif name in ("o", "o2"):
                        wait_filled(dve, i, name, t)
                        nc.vector.tensor_tensor(residual(i, t), residual(i, t), bank[:, :], ALU.add).then_inc(copied[slot][0], 1)
                    elif name == "a":
                        kr = bank[:, QR + KL:QR + KL + DR]
                        cos, sin, h = cst[:, C_COS:C_COS + DR], cst[:, C_SIN:C_SIN + DR], DR // 2
                        dve.wait_ge(rms_sum[0], tiles(i, t))
                        nc.vector.tensor_tensor(rot1, kr, cos, ALU.mult)
                        nc.vector.tensor_tensor(rot2[:, 0:h], kr[:, h:DR], sin[:, 0:h], ALU.mult)
                        chained(nc.vector.tensor_tensor(rot2[:, h:DR], kr[:, 0:h], sin[:, h:DR], ALU.mult))
                        for c in range(2):
                            nc.vector.tensor_tensor(an[:, QR + KL + c * DR:QR + KL + (c + 1) * DR], rot1, rot2, ALU.add)
                        dve.wait_ge(rms_std[0], tiles(i, t))
                        chained(nc.vector.reciprocal(rrms, rms))
                        nc.vector.tensor_scalar(an[:, 0:QR], bank[:, 0:QR], rrms[:, 0:1], None, ALU.mult)
                        nc.vector.tensor_scalar(an[:, QR:QR + KL], bank[:, QR:QR + KL], rrms[:, 1:2], None, ALU.mult).then_inc(copied[slot][0], 1)
                    elif name == "aT":
                        wait_filled(dve, i, name, t)
                        nc.vector.tensor_scalar(qc0, bank[:, 0:P], lnq0, None, ALU.mult)
                        nc.vector.tensor_scalar(qc1[0:QR - P], bank[0:QR - P, P:2 * P], lnq1[0:QR - P], None, ALU.mult)
                        nc.vector.tensor_scalar(klT, bank[:, 2 * P:3 * P], lnk, None, ALU.mult)
                        nc.vector.tensor_copy(krz[0:DR, 0], bank[0:DR, 3 * P:4 * P])
                        nc.vector.tensor_copy(krz[DR:2 * DR, 1], bank[DR:2 * DR, 3 * P:4 * P]).then_inc(copied[slot][0], 1)

                elif kind == "top":
                    half = range(name * NT // 2, (name + 1) * NT // 2)
                    of = slice(half.start, half.stop)
                    dve.wait_ge(lg_exp[0], name + 1)
                    chained(nc.vector.tensor_reduce(sum8[:, of], ex[:, of], AX.X, ALU.add))
                    chained(nc.vector.reciprocal(rsum8[:, of], sum8[:, of]))
                    chained(nc.vector.tensor_tensor(lg[:, of], ex[:, of], rsum8[:, of].unsqueeze(2).to_broadcast([P, NT // 2, E]), ALU.mult))
                    for k in half:
                        last = nc.vector.max(top_w[:, k], lg[:, k])
                    chained(last)
                    for k in half:
                        last = nc.vector.max_index(top_i[:, k], top_w[:, k], lg[:, k])
                    chained(last)
                    chained(nc.vector.tensor_copy(top_f[:, of], top_i[:, of]))
                    for k in half:
                        last = nc.vector.tensor_tensor(
                            choice[:, k * TOPK:(k + 1) * TOPK], cst[:, C_IOTA:C_IOTA + E].unsqueeze(1).to_broadcast([P, TOPK, E]),
                            top_f[:, k, 0:TOPK].unsqueeze(2).to_broadcast([P, TOPK, E]), ALU.is_equal)
                    last.then_inc(choice_ready[0], 1)
                    dve.wait_ge(choice_ready[0], name + 1)
                    chained(nc.vector.tensor_reduce(chosen_by[:, of], choice[:, half.start * TOPK:half.stop * TOPK].rearrange(
                        "p (t k) e -> p t e k", k=TOPK), AX.X, ALU.add))
                    for k in half:
                        last = nc.vector.memset(before[:, 0], 0.0) if k == 0 else nc.vector.tensor_tensor(
                            before[:, k], before[:, k - 1], chosen_by[:, k - 1], ALU.add)
                        if k < half.stop - 1:
                            chained(last)
                    last.then_inc(before_ready[0], 1)
                elif kind == "hot":
                    for n in range(name * TOPK, (name + 1) * TOPK):
                        last = nc.vector.tensor_scalar(hot[:, n], cst[:, C_IOTA:C_IOTA + P], rank_of[:, n:n + 1], None, ALU.is_equal)
                    last.then_inc(hot_ready[0], 1)
                elif kind == "rows":
                    dve.wait_ge(table_filled[0], 1)
                    chained(nc.vector.tensor_copy(idx_w.rearrange("p a b -> p (a b)"), a_bank[1][:, 0:P]))
                    chained(nc.vector.tensor_scalar(spare, idx_w[:, 0], 0.0, cst[:, C_SPARE:C_SPARE + 1], ALU.is_equal, ALU.mult))
                    nc.vector.scalar_tensor_tensor(row_of, idx_w[:, 0], -1.0, spare, ALU.add, ALU.add).then_inc(rows_known[0], 1)

            for kind, name, t in FIRST:
                if (kind, name, t) == ("stat", "ln1", 1):
                    dve.wait_ge(loaded["x1"][0], 16)
                if name == "aT":
                    for n in ("lnq0", "lnq1", "lnkv"):
                        dve.wait_ge(loaded[n][0], 16)
                    dve.wait_ge(zeros_ready[0], 2)
                step(0, kind, name, t)
            assert links[0] == FIRST_LINKS
            dve.wait_ge(loaded["x2"][0], 16)
            with dve.Fori(0, REPEATS) as i:
                for kind, name, t in LOOP:
                    step(i, kind, name, t)
            links[0] = FIRST_LINKS + REPEATS * LINKS_PER_LOOP
            for kind, name, t in LAST:
                step(0, kind, name, t)

            def expert(i, r):
                dve.wait_ge(silu_done[0], at(silu_done, i, r + 1))
                dve.wait_ge(eo_filled[0], i * R + max(r - 1, 0) if type(i) is int and i == 0 else i * R + (r - 1))
                g = silu_e[0:H3, r % 2].rearrange("p (m t) -> p m t", t=P)
                u = s_bank[r % 2][H3:2 * H3, 0:3 * P].rearrange("p (m t) -> p m t", t=P)
                nc.vector.tensor_tensor(hid_e[0:H3, r % 2].rearrange("p (m t) -> p m t", t=P), g[:, 0:3:2], u[:, 0:3:2], ALU.mult)
                nc.vector.tensor_tensor(hid_e[H3:2 * H3, r % 2, 0:P], g[:, 1], u[:, 1], ALU.mult).then_inc(hid_ready[0], 1)

            def output(i, r):
                dve.wait_ge(eo_filled[0], at(eo_filled, i, r + 1))
                if not (type(i) is int and i == 0):
                    dve.wait_ge(added[r % 2][0], at(added[r % 2], i, 16 * (r // 2 + 1 - R // 2)))
                e = i * R + r
                w = idx_w[:, 1, bass.ds(e, 1)] if type(i) is not int else idx_w[:, 1, e:e + 1]
                nc.vector.tensor_scalar(eo[:, r], job_bank[r % 2][:, :], w, None, ALU.mult).then_inc(eo_ready[0], 1)

            for r in range(R):
                expert(0, r)
                if r:
                    output(0, r - 1)
            first, token = small[:, 32:40], idx_w[:, 0, E - 1:E]
            for t in range(NT):
                last = nc.vector.tensor_scalar(first[:, t:t + 1], token, float(-1 - t * P), None, ALU.add)
            last.then_inc(last_known[0], 1)
            dve.wait_ge(last_known[0], 1)
            for t in range(NT):
                last = nc.vector.tensor_scalar(last_tokens[:, t], cst[:, C_IOTA:C_IOTA + P], first[:, t:t + 1], None, ALU.is_equal)
            last.then_inc(last_known[0], 1)
            with dve.Fori(1, E // R) as i:
                for r in range(R):
                    expert(i, r)
                    output(i - 1, R - 1) if r == 0 else output(i, r - 1)
            output(E // R - 1, R - 1)
            for h in range(2):
                dve.wait_ge(odd_loaded[h][0], 16)
                for t in range(h * NT // 2, (h + 1) * NT // 2):
                    dve.wait_ge(last_filled[0], t + 1)
                    nc.vector.tensor_tensor(odd_sums[:, t], odd_sums[:, t], last_bank[t][:, :], ALU.add).then_inc(both_added[0], 1)
                for t in range(h * NT // 2, (h + 1) * NT // 2):
                    dve.wait_ge(even_loaded[t][0], 16)
                    dve.wait_ge(both_added[0], t + 1)
                    nc.vector.tensor_tensor(x_all[:, t], x_all[:, t], odd_sums[:, t], ALU.add).then_inc(out_ready[0], 1)

        @block.tensor
        def _(pe):
            mm = nc.tensor.matmul
            met = set()

            def loads(*names):
                for n in names:
                    if n not in met:
                        met.add(n)
                        pe.wait_ge(loaded[n][0], 16 * (4 if n[:3] == "qkb" else 1))

            def m_products(name, bank, parts, ready):
                m = int(name[1])
                loads("qkb0", *(("qkb1",) if 2 * m + 1 >= MH // 2 else ()))
                ready()
                for part in parts:
                    (r0, rn), h = ((0, P), (P, QR - P))[part // 2], 2 * m + part % 2
                    o = bank[0:rn, part * P:(part + 1) * P]
                    mm(o, wqb0[:, h, r0:r0 + rn], wkb0[:, h], start=True, stop=False)
                    last = mm(o, wqb1[0:DN - P, h, r0:r0 + rn], wkb1[0:DN - P, h], start=False, stop=True)
                return last

            def job(i, name, t):
                n = nth("job", name, i, t)
                bank, slot = job_bank[n % 2], n % 2

                def ready(*names):
                    wait_copied(pe, i, *((m, t) for m in names), free_for=(name, t))

                if name[0] == "M":
                    last = m_products(name, bank, (3,) if name == "M8" else range(4), lambda: name == "M8" or ready())
                elif name == "k":
                    ready()
                    for m in range(KD):
                        last = mm(bank[:, m * P:(m + 1) * P], WkvT[:, m * P:(m + 1) * P], ctx_cur, start=True, stop=True)
                elif name == "v":
                    loads("wkv")
                    ready()
                    pe.wait_ge(ctx_ready[0], tiles(i, t))
                    last = mm(bank[:, :], ctx_cur, WkvT[:, D:2 * D], start=True, stop=True)
                elif name in ("xT", "x2T", "x3T"):
                    ln, src = {"xT": ("ln1", xn1), "x2T": ("ln2", xn2), "x3T": ("ln3", xn3)}[name]
                    ready()
                    pe.wait_ge(ln_done[ln][0], tiles(i, t))
                    for k in range(KD):
                        last = nc.tensor.transpose(bank[:, k * P:(k + 1) * P], src[:, k * P:(k + 1) * P], ident)
                elif name == "q":
                    loads("wq")
                    ready("xT")
                    for m in range(KD):
                        for k in range(KD):
                            last = mm(bank[:, m * P:(m + 1) * P], WqT[:, k, m * P:(m + 1) * P], xnT[:, k], start=k == 0, stop=k == KD - 1)
                elif name == "o":
                    loads("wout")
                    ready()
                    wait_unit(pe, av_copied, ("A", XH // 4 - 1), i, t)
                    for k in range(KD):
                        last = mm(bank[:, :], cT[:, k], WoutT[:, k], start=k == 0, stop=k == KD - 1)
                elif name == "a":
                    loads("wa")
                    ready("x2T")
                    for k in range(KD):
                        last = mm(bank[:, 0:QR + KL + DR], x2T[:, k], WaT[:, k], start=k == 0, stop=k == KD - 1)
                elif name == "aT":
                    ready("a")
                    for c, (f, w) in enumerate(((0, P), (P, QR - P), (QR, KL), (QR + KL, 2 * DR))):
                        last = nc.tensor.transpose(bank[0:w, c * P:(c + 1) * P], an[:, f:f + w], ident)
                elif name[0:2] == "v2":
                    f = 512 * int(name[3])
                    w = min(512, MH * DV - f)
                    ready("aT")
                    last = mm(bank[:, 0:w], klT, WvbT[:, f:f + w], start=True, stop=True)
                elif name[0] == "r" and name[1] != "k":
                    ready("aT")
                    for m in range(4 * int(name[1]), min(4 * int(name[1]) + 4, MH // 2)):
                        o = bank[:, m % 4 * P:(m % 4 + 1) * P]
                        mm(o, WqrT0[:, m * P:(m + 1) * P], qc0, start=True, stop=False)
                        last = mm(o, WqrT1[0:QR - P, m * P:(m + 1) * P], qc1[0:QR - P], start=False, stop=True)
                elif name[0] == "l":
                    ready("aT")
                    for j in range(4):
                        h, o = 4 * int(name[1]) + j, bank[:, j * P:(j + 1) * P]
                        mm(o, M0[:, h], qc0, start=True, stop=False)
                        last = mm(o, M1[0:QR - P, h], qc1[0:QR - P], start=False, stop=True)
                elif name == "o2":
                    wait_unit(pe, av_copied, ("B", MH // 4 - 1), i, t)
                    for k in range(O2_BEGIN, MH // 2):
                        last = mm(bank[:, :], c2T[:, k], WoT[:, k], start=False, stop=k == MH // 2 - 1)
                elif name[0:2] == "gl":
                    loads("gate")
                    h = int(name[2])
                    ready(*(("x3T",) if h == 1 else ()))
                    for k in range(KD):
                        last = mm(bank[0:E, :], WgT[:, k], x3nT[:, k, h * 512:(h + 1) * 512], start=k == 0, stop=k == KD - 1)
                elif name[0:2] == "gt":
                    h = int(name[2])
                    ready()
                    wait_copied(pe, i, (f"gl{h}", NT - 2 + h))
                    for k in range(NT // 2):
                        last = nc.tensor.transpose(bank[:, k * E:(k + 1) * E], lgT[0:E, k * P:(k + 1) * P], cst[0:E, C_ID:C_ID + E])
                elif name[0:2] == "rk":
                    ready()
                    h = int(name[2])
                    pe.wait_ge(before_ready[0], h + 1)
                    of = slice(h * NT // 2, (h + 1) * NT // 2)
                    o = bank[:, 0:NT // 2 * E]
                    mm(o, cst[:, C_BEFORE:C_BEFORE + P], chosen_by[:, of].rearrange("p t e -> p (t e)"), start=True, stop=False)
                    last = mm(o, cst[:, C_ONES:C_ONES + P], before[:, of].rearrange("p t e -> p (t e)"), start=False, stop=True)
                elif name[0] in "gu":
                    loads("sg", "su")
                    ready()
                    h, m, w = int(name[1]), int(name[2]), WsgT if name[0] == "g" else WsuT
                    for k in range(KD):
                        last = mm(bank[:, :], w[:, k, m * P:(m + 1) * P], x3nT[:, k, h * 512:(h + 1) * 512], start=k == 0, stop=k == KD - 1)
                elif name[0] == "d":
                    loads("sd")
                    h, m = divmod(int(name[1]), NT // 2)
                    if m == 0:
                        wait_copied(pe, i, *((f"u{h}{k}", NT - 2 + h) for k in range(SI // P)))
                    ready()
                    for k in range(SI // P):
                        last = mm(bank[:, :], (hid_first, hid_second)[h][:, k, m * P:(m + 1) * P], WsdT[:, k], start=k == 0, stop=k == SI // P - 1)
                last.then_inc(filled[slot][0], 1)

            def step(i, kind, name, t):
                if kind == "job":
                    job(i, name, t)
                elif (kind, name) == ("begin", "M8"):
                    m_products(name, bank_of(i, name, t), range(3), lambda: wait_copied(pe, i, free_for=(name, t)))
                elif kind == "begin":
                    pe.wait_ge(loaded["wo"][0], 16)
                    wait_copied(pe, i, free_for=("o2", t))
                    wait_unit(pe, av_copied, ("B", MH // 4 - 2), i, t)
                    for k in range(O2_BEGIN):
                        mm(bank_of(i, "o2", t)[:, :], c2T[:, k], WoT[:, k], start=k == 0, stop=False)
                elif kind == "S":
                    n, (which, hg) = nth("S", name, i, t), name
                    wait_unit(pe, masked_ready, name, i, t, behind=2)
                    if which == "B":
                        wait_copied(pe, i, (f"l{hg}", t), (f"r{hg // 2}", t))
                        for j in range(4):
                            o, h = s_bank[n % 2][:, j * P:(j + 1) * P], 4 * hg + j
                            mm(o, ql[:, h], klT, start=True, stop=False)
                            last = mm(o, qr[:, h // 2], krz[:, h % 2], start=False, stop=True)
                    else:
                        if hg == 0:
                            wait_copied(pe, i, ("q", t))
                        pe.wait_ge(kz_ready[0], t * 4 + hg + 1 if type(i) is int else i * 8 + (t * 4 + hg + 1))
                        last = mm(s_bank[n % 2][:, :], qT[:, hg], kz[:, hg % 2].rearrange("p a b -> p (a b)"), start=True, stop=True)
                    last.then_inc(scores_ready[0], 1)
                elif kind == "T":
                    n = nth("S", name, i, t)
                    wait_unit(pe, norm_done, name, i, t)
                    wait_unit(pe, pT_copied, name, i, t, behind=2)
                    for j in range(4):
                        last = nc.tensor.transpose(t_bank[n % 2][:, j * P:(j + 1) * P], probs[:, n % 3, j], ident)
                    last.then_inc(pT_ready[0], 1)
                elif kind == "A":
                    n, (which, hg) = nth("S", name, i, t), name
                    wait_unit(pe, pT_copied, name, i, t)
                    wait_unit(pe, av_copied, name, i, t, behind=2)
                    if name == ("A", 0):
                        wait_copied(pe, i, ("v", t))
                    elif which == "B" and hg % 2 == 0:
                        wait_copied(pe, i, (f"v2_{hg // 2}", t))
                    for j in range(4):
                        h = 4 * hg + j
                        if which == "B":
                            o = a_bank[n % 2][DV * (j % 2):DV * (j % 2) + DV, j // 2 * P:j // 2 * P + P]
                            last = mm(o, v2[:, h * DV:(h + 1) * DV], probsT[:, n % 2, j], start=True, stop=True)
                        else:
                            last = mm(a_bank[n % 2][XD * j:XD * (j + 1), 0:P], v[:, t % 2, h * XD:(h + 1) * XD],
                                      probsT[:, n % 2, j], start=True, stop=True)
                    last.then_inc(av_ready[0], 1)

                elif kind == "slots":
                    pe.wait_ge(av_copied[0], NUNITS)
                    pe.wait_ge(pair_ready[0], name + 1)
                    pe.wait_ge(hot_ready[0], name + 1)
                    for n in range(name * TOPK, (name + 1) * TOPK):
                        last = mm(a_bank[1][:, 0:P], hot[:, n], pair[:, n].rearrange("p a e -> p (a e)"), start=n == 0, stop=n == NT * TOPK - 1)
                    if name == NT - 1:
                        last.then_inc(table_filled[0], 1)

            pe.wait_ge(loaded["consts"][0], 16)
            for kind, name, t in FIRST:
                step(0, kind, name, t)
            for n in ("wvb", "qr0", "qr1"):
                pe.wait_ge(loaded[n][0], 16)
            with pe.Fori(0, REPEATS) as i:
                for kind, name, t in LOOP:
                    step(i, kind, name, t)
            for kind, name, t in LAST:
                step(0, kind, name, t)

            def turn(i, r):
                i, r = i + r // R, r % R
                pe.wait_ge(gx_loaded[r][0], at(gx_loaded[r], i, 16))
                if type(i) is not int or i * R + r >= 2:
                    pe.wait_ge(gxT_copied[0], i * R + (r - 1))
                for k in range(KD):
                    last = nc.tensor.transpose(t_bank[r % 2][:, k * P:(k + 1) * P], gx[:, r, k * P:(k + 1) * P], ident)
                last.then_inc(gx_turned[0], 1)

            def gate_and_up(i, r):
                pe.wait_ge(w_loaded[r][0], at(w_loaded[r], i, 64))
                pe.wait_ge(gxT_copied[0], at(gxT_copied, i, r + 1))
                if type(i) is not int or i * R + r >= 2:
                    pe.wait_ge(hid_ready[0], i * R + (r - 1))
                w = wgu[:, r].rearrange("p k (f m) -> p k m f", m=3)
                for m in range(3):
                    for k in range(KD):
                        last = mm(s_bank[r % 2][:, m * P:(m + 1) * P], w[:, k, m],
                                  gxT[:, r % 2, k * P:(k + 1) * P], start=k == 0, stop=k == KD - 1)
                last.then_inc(gu_filled[0], 1)

            def down_product(i, r):
                if r < 0:
                    i, r = i - 1, r + R
                pe.wait_ge(hid_ready[0], at(hid_ready, i, r + 1))
                if type(i) is not int or i * R + r >= 2:
                    pe.wait_ge(eo_ready[0], i * R + (r - 1))
                mm(job_bank[r % 2][:, :], hid_e[:, r % 2, 0:P], wd0[:, r], start=True, stop=False)
                mm(job_bank[r % 2][:, :], hid_e[0:H3, r % 2, P:2 * P], wd1[0:H3, r], start=False, stop=True).then_inc(eo_filled[0], 1)

            def experts(i):
                for r in range(R):
                    if type(i) is not int or i * R + r + 1 < E:
                        turn(i, r + 1)
                    gate_and_up(i, r)
                    if type(i) is not int or i * R + r > 0:
                        down_product(i, r - 1)

            for k in range(2):
                pe.wait_ge(copied[k][0], JOBS_IN[k])
            pe.wait_ge(rows_known[0], 1)
            turn(0, 0)
            experts(0)
            with pe.Fori(1, E // R - 1) as i:
                experts(i)
            experts(E // R - 1)
            down_product(E // R - 1, R - 1)
            pe.wait_ge(last_known[0], 2)
            pe.wait_ge(eo_ready[0], E)
            for t in range(NT):
                mm(last_bank[t][:, :], last_tokens[:, t], eo[:, R - 1], start=True, stop=True).then_inc(last_filled[0], 1)


def kernel(x, ctx_512, L0_xattn_Wq, L0_xattn_Wkv_expand, L0_xattn_Wout, L0_attn_q_a_w, L0_attn_q_a_ln_w,
           L0_attn_q_b_w, L0_attn_kv_a_w, L0_attn_kv_a_ln_w, L0_attn_kv_b_w, L0_attn_o_w, L0_ffn_gate_w,
           L0_ffn_gate_up_proj, L0_ffn_down_proj, L0_ffn_shared_gate_w, L0_ffn_shared_up_w, L0_ffn_shared_down_w):
    import concourse.bacc as bacc
    from concourse.bass_utils import run_bass_kernel_spmd

    a = np.asarray
    qb = a(L0_attn_q_b_w).reshape(MH, DN + DR, QR)
    kvb = a(L0_attn_kv_b_w).reshape(MH, DN + DV, KL)
    arrays = {
        "x": a(x).reshape(TOK, D),
        "ctxT": a(ctx_512)[:, :SQ].transpose(2, 0, 1).reshape(XL, TOK),
        "consts": constant_table(),
        "wqT": a(L0_xattn_Wq).T, "wkvT": a(L0_xattn_Wkv_expand).T, "woutT": a(L0_xattn_Wout).T,
        "waT": np.concatenate([a(L0_attn_q_a_w), a(L0_attn_kv_a_w)], 0).T,
        "lnq": a(L0_attn_q_a_ln_w).reshape(QR, 1), "lnkv": a(L0_attn_kv_a_ln_w).reshape(KL, 1),
        "wqb": qb[:, :DN].transpose(1, 0, 2), "wqrT": qb[:, DN:].transpose(2, 0, 1).reshape(QR, MH * DR),
        "wkb": kvb[:, :DN].transpose(1, 0, 2), "wvbT": kvb[:, DN:].transpose(2, 0, 1).reshape(KL, MH * DV),
        "woT": a(L0_attn_o_w).T, "gateT": a(L0_ffn_gate_w).T,
        "gate_up": a(L0_ffn_gate_up_proj), "down": a(L0_ffn_down_proj),
        "sgT": a(L0_ffn_shared_gate_w).T, "suT": a(L0_ffn_shared_up_w).T, "sdT": a(L0_ffn_shared_down_w).T,
    }
    arrays = {k: np.ascontiguousarray(v) for k, v in arrays.items()}
    nc = bacc.Bacc("TRN2", target_bir_lowering=False, num_devices=1)
    aps = [nc.dram_tensor(k, v.shape, mybir.dt.from_np(v.dtype), kind="ExternalInput").ap() for k, v in arrays.items()]
    out = nc.dram_tensor("out", (TOK, D), mybir.dt.float32, kind="ExternalOutput").ap()
    build(nc, *aps, out)
    r = run_bass_kernel_spmd(nc, [arrays], core_ids=[0])
    return r.results[0]["out"].reshape(B, SQ, D)
```
